# Optimizing a Trainium2 kernel written in Bass

```python
import numpy as np
import jax
import jax.numpy as jnp

def _softmax(x, axis=-1):
    return jax.nn.softmax(x, axis=axis)

def _gelu(x):
    return jax.nn.gelu(x, approximate=True)

def _silu(x):
    return jax.nn.silu(x)

def _sigmoid(x):
    return jax.nn.sigmoid(x)

def _layernorm(x, axis=-1, eps=1e-05):
    m = jnp.mean(x, axis=axis, keepdims=True)
    v = jnp.var(x, axis=axis, keepdims=True)
    return (x - m) / jnp.sqrt(v + eps)

def _scatter_add(tgt, idx, src, axis=0):
    return tgt.at[idx].add(src)

def _segment_sum(src, seg, n):
    return jax.ops.segment_sum(src, seg, n)
kernel_name = 'mk_adaln_d1_jaxref_r8_40eb1a'

def setup_inputs(seed: int=0):
    np.random.seed(seed)
    _w = jnp.asarray

    def _L0_attn_setup():
        import jax, jax.numpy as jnp
        import numpy as np
        import math
        NUM_HEADS = 8
        EMB = 128
        HEAD_DIM = 128
        B, T = (1, 512)

        def sinusoidal_pe(T, d, dtype=jnp.float32):
            pos = jnp.arange(T, dtype=dtype)[:, None]
            inv_freq = jnp.exp(-math.log(10000.0) * jnp.arange(0, d, 2, dtype=dtype) / d)
            ang = pos * inv_freq[None, :]
            pe = jnp.zeros((T, d), dtype=dtype)
            pe = pe.at[:, 0::2].set(jnp.sin(ang))
            pe = pe.at[:, 1::2].set(jnp.cos(ang))
            return pe
        key = jax.random.key(seed)
        ks = jax.random.split(key, 6)
        s = lambda fan_in: 1.0 / math.sqrt(fan_in)
        x = jax.random.normal(ks[0], (B, T, EMB), dtype=jnp.float32)
        Wq = jax.random.normal(ks[1], (EMB, NUM_HEADS * HEAD_DIM), dtype=jnp.float32) * s(EMB)
        bq = jax.random.normal(ks[2], (NUM_HEADS * HEAD_DIM,), dtype=jnp.float32) * s(EMB)
        Wkv = jax.random.normal(ks[3], (EMB, 2 * HEAD_DIM), dtype=jnp.float32) * s(EMB)
        bkv = jax.random.normal(ks[4], (2 * HEAD_DIM,), dtype=jnp.float32) * s(EMB)
        Wo = jax.random.normal(ks[5], (NUM_HEADS * HEAD_DIM, EMB), dtype=jnp.float32) * s(NUM_HEADS * HEAD_DIM)
        return {'x': x, 'Wq': Wq, 'bq': bq, 'Wkv': Wkv, 'bkv': bkv, 'Wo': Wo}
    _L0_attn_in = _L0_attn_setup()

    def _L0_ffn_setup():
        import jax, jax.numpy as jnp
        import numpy as np
        H, I, E, K = (128, 64, 32, 8)
        B, S = (4, 128)

        def silu(x):
            return x * jax.nn.sigmoid(x)
        key = jax.random.key(seed)
        ks = jax.random.split(key, 14)

        def w(k, shape, fan_in):
            return jax.random.normal(k, shape, jnp.float32) / np.float32(np.sqrt(fan_in))
        return {'hidden_states': jax.random.normal(ks[0], (B, S, H), jnp.float32), 'Wr': w(ks[1], (H, E), H), 'br': jnp.zeros((E,), jnp.float32), 'Wg_s': w(ks[2], (H, I), H), 'bg_s': jnp.zeros((I,), jnp.float32), 'Wu_s': w(ks[3], (H, I), H), 'bu_s': jnp.zeros((I,), jnp.float32), 'Wd_s': w(ks[4], (I, H), I), 'bd_s': jnp.zeros((H,), jnp.float32), 'Wg': w(ks[5], (E, H, I), H), 'bg': jnp.zeros((E, I), jnp.float32), 'Wu': w(ks[6], (E, H, I), H), 'bu': jnp.zeros((E, I), jnp.float32), 'Wd': w(ks[7], (E, I, H), I), 'bd': jnp.zeros((E, H), jnp.float32)}
    _L0_ffn_in = _L0_ffn_setup()
    _L0_c = _w((lambda *s: np.random.randn(*s).astype(np.float32) * 0.05)(4, 128))
    _L0_wmod = _w((lambda *s: np.random.randn(*s).astype(np.float32) * 0.05)(128, 6 * 128) * 128 ** (-0.5))
    _d = {'L0_attn_x': _L0_attn_in['x'], 'L0_attn_Wq': _L0_attn_in['Wq'], 'L0_attn_bq': _L0_attn_in['bq'], 'L0_attn_Wkv': _L0_attn_in['Wkv'], 'L0_attn_bkv': _L0_attn_in['bkv'], 'L0_attn_Wo': _L0_attn_in['Wo'], 'L0_ffn_Wr': _L0_ffn_in['Wr'], 'L0_ffn_br': _L0_ffn_in['br'], 'L0_ffn_Wg_s': _L0_ffn_in['Wg_s'], 'L0_ffn_bg_s': _L0_ffn_in['bg_s'], 'L0_ffn_Wu_s': _L0_ffn_in['Wu_s'], 'L0_ffn_bu_s': _L0_ffn_in['bu_s'], 'L0_ffn_Wd_s': _L0_ffn_in['Wd_s'], 'L0_ffn_bd_s': _L0_ffn_in['bd_s'], 'L0_ffn_Wg': _L0_ffn_in['Wg'], 'L0_ffn_bg': _L0_ffn_in['bg'], 'L0_ffn_Wu': _L0_ffn_in['Wu'], 'L0_ffn_bu': _L0_ffn_in['bu'], 'L0_ffn_Wd': _L0_ffn_in['Wd'], 'L0_ffn_bd': _L0_ffn_in['bd'], 'L0_c': _L0_c, 'L0_wmod': _L0_wmod}
    _x0 = _d['L0_attn_x']
    _d['L0_attn_x'] = jax.random.normal(jax.random.fold_in(jax.random.key(seed), 1), (4, 1024, 128), dtype=_x0.dtype)
    del _x0
    return _d

def reference(L0_attn_x, L0_attn_Wq, L0_attn_bq, L0_attn_Wkv, L0_attn_bkv, L0_attn_Wo, L0_ffn_Wr, L0_ffn_br, L0_ffn_Wg_s, L0_ffn_bg_s, L0_ffn_Wu_s, L0_ffn_bu_s, L0_ffn_Wd_s, L0_ffn_bd_s, L0_ffn_Wg, L0_ffn_bg, L0_ffn_Wu, L0_ffn_bu, L0_ffn_Wd, L0_ffn_bd, L0_c, L0_wmod):

    def _L0_attn_ref(x, Wq, bq, Wkv, bkv, Wo):
        import jax, jax.numpy as jnp
        import numpy as np
        import math
        NUM_HEADS = 8
        EMB = 128
        HEAD_DIM = 128
        B, T = (1, 512)

        def sinusoidal_pe(T, d, dtype=jnp.float32):
            pos = jnp.arange(T, dtype=dtype)[:, None]
            inv_freq = jnp.exp(-math.log(10000.0) * jnp.arange(0, d, 2, dtype=dtype) / d)
            ang = pos * inv_freq[None, :]
            pe = jnp.zeros((T, d), dtype=dtype)
            pe = pe.at[:, 0::2].set(jnp.sin(ang))
            pe = pe.at[:, 1::2].set(jnp.cos(ang))
            return pe
        Bsz, Tlen, E = x.shape
        q = (x @ Wq + bq).reshape(Bsz, Tlen, NUM_HEADS, HEAD_DIM)
        kv = x @ Wkv + bkv
        k, v = (kv[..., :HEAD_DIM], kv[..., HEAD_DIM:])
        q = jnp.transpose(q, (0, 2, 1, 3))
        pe = sinusoidal_pe(Tlen, HEAD_DIM, x.dtype)
        q = q + pe[None, None, :, :]
        k = k + pe[None, :, :]
        scale = 1.0 / math.sqrt(HEAD_DIM)
        scores = jnp.einsum('bhqd,bkd->bhqk', q, k) * scale
        causal = jnp.tril(jnp.ones((Tlen, Tlen), dtype=bool))
        scores = jnp.where(causal[None, None, :, :], scores, jnp.finfo(scores.dtype).min)
        probs = jax.nn.softmax(scores, axis=-1)
        attn = jnp.einsum('bhqk,bkd->bhqd', probs, v)
        out = jnp.transpose(attn, (0, 2, 1, 3)).reshape(Bsz, Tlen, NUM_HEADS * HEAD_DIM)
        return out @ Wo

    def _L0_ffn_ref(hidden_states, Wr, br, Wg_s, bg_s, Wu_s, bu_s, Wd_s, bd_s, Wg, bg, Wu, bu, Wd, bd):
        import jax, jax.numpy as jnp
        import numpy as np
        H, I, E, K = (128, 64, 32, 8)
        B, S = (4, 128)

        def silu(x):
            return x * jax.nn.sigmoid(x)
        b, s, h = hidden_states.shape
        T = b * s
        x = hidden_states.reshape(T, h)
        logits = jnp.dot(x.astype(jnp.float32), Wr) + br
        aff = jax.nn.sigmoid(logits)
        top_v, top_i = jax.lax.top_k(aff, K)
        top_w = top_v / (jnp.sum(top_v, axis=-1, keepdims=True) + 1e-09)
        top_w = top_w.astype(hidden_states.dtype)
        e_total = Wr.shape[1]
        w_full = jnp.zeros((T, e_total), hidden_states.dtype)
        w_full = w_full.at[jnp.arange(T)[:, None], top_i].set(top_w)
        shared = jnp.dot(silu(jnp.dot(x, Wg_s) + bg_s) * (jnp.dot(x, Wu_s) + bu_s), Wd_s) + bd_s
        gate = silu(jnp.einsum('th,ehi->eti', x, Wg) + bg[:, None, :])
        up = jnp.einsum('th,ehi->eti', x, Wu) + bu[:, None, :]
        down = jnp.einsum('eti,eih->eth', gate * up, Wd) + bd[:, None, :]
        routed = jnp.einsum('te,eth->th', w_full, down)
        return (shared + routed).reshape(b, s, h)
    x = L0_attn_x
    mod = (_silu(L0_c) @ L0_wmod).reshape(L0_c.shape[0], 6, 1, -1)
    sa, ca, ga, sb, cb, gb = (mod[:, 0], mod[:, 1], mod[:, 2], mod[:, 3], mod[:, 4], mod[:, 5])
    ga = (2 * (ga >= 0) - 1) * jnp.maximum(jnp.abs(ga), 0.25)
    gb = (2 * (gb >= 0) - 1) * jnp.maximum(jnp.abs(gb), 0.25)
    h = _layernorm(x, axis=-1) * (1 + ca) + sa
    x = x + ga * _L0_attn_ref(h, L0_attn_Wq, L0_attn_bq, L0_attn_Wkv, L0_attn_bkv, L0_attn_Wo)
    h = _layernorm(x, axis=-1) * (1 + cb) + sb
    x = x + gb * _L0_ffn_ref(h, L0_ffn_Wr, L0_ffn_br, L0_ffn_Wg_s, L0_ffn_bg_s, L0_ffn_Wu_s, L0_ffn_bu_s, L0_ffn_Wd_s, L0_ffn_bd_s, L0_ffn_Wg, L0_ffn_bg, L0_ffn_Wu, L0_ffn_bu, L0_ffn_Wd, L0_ffn_bd)
    return x

_drawn_inputs = setup_inputs


def setup_inputs(seed=0):
    import zlib

    import numpy as np

    out = dict(_drawn_inputs(seed))
    spreads = {'L0_ffn_br': (0.0, 0.468),
     'L0_ffn_bg_s': (0.0, 0.547),
     'L0_ffn_bu_s': (0.0, 0.59),
     'L0_ffn_bd_s': (0.0, 0.337),
     'L0_ffn_bg': (0.0, 0.8),
     'L0_ffn_bu': (0.0, 0.8),
     'L0_ffn_bd': (0.0, 0.8)}
    factors = {'L0_attn_bq': 8.0}
    for name, (base, spread) in spreads.items():
        noise = np.random.default_rng([zlib.crc32(name.encode()), seed]).standard_normal(out[name].shape)
        drawn = base * np.exp(spread * noise) if base else spread * noise
        out[name] = jnp.asarray(drawn.astype(out[name].dtype))
    for name, factor in factors.items():
        out[name] = (out[name] * factor).astype(out[name].dtype)
    return out
```

```python
import math
from contextlib import ExitStack

import numpy as np

import concourse.bass as bass
from concourse import mybir

F32 = mybir.dt.float32
F32R = mybir.dt.float32r
BF16 = mybir.dt.bfloat16
ALU = mybir.AluOpType
ACT = mybir.ActivationFunctionType
AX_X = mybir.AxisListType.X

P = 128
BATCH, TOKENS = 4, 1024
BLOCKS = TOKENS // P
HEADS = 8
HALF = 512
TILES = TOKENS // HALF
EXPERTS, INNER, TOP = 32, 64, 8
PAIRS = EXPERTS // 2
UNITS = PAIRS + 1
LN_EPS = 1e-5
MASKED = -1e30
SCALE = 1.0 / math.sqrt(P)
HI, LO = 0, 1

SHIFT_A, SCALE_A, GATE_A, SHIFT_F, SCALE_F, GATE_F = range(6)

PASSES = ((HI, HI), (LO, HI), (HI, LO))

ORDER = [3, 2, 1, 0, 7, 6, 5, 4]
PLACE = [ORDER.index(i) for i in range(BLOCKS)]
STEPS = [(0, j) for j in range(4)] + [(1, j) for j in range(8)]
NSTEP = len(STEPS)
PROB_AT = [P * i * (i + 1) // 2 for i in range(BLOCKS + 1)]

PE_A = [("score", 7), ("turn", 0), ("score", 6), ("turn", 1), ("apply", 0), ("project", 0), ("score", 5),
        ("turn", 2), ("apply", 1), ("score", 4), ("turn", 3), ("apply", 2), ("apply", 3)]
PE_B = [("project", 1), ("score", 3), ("score", 2), ("turn", 4), ("turn", 5), ("score", 1), ("turn", 6),
        ("apply", 4), ("score", 0), ("turn", 7), ("apply", 5), ("turn", 8), ("apply", 6), ("turn", 9),
        ("apply", 7), ("turn", 10), ("apply", 8), ("turn", 11), ("apply", 9), ("apply", 10), ("apply", 11)]
DVE_A = [("max", 7), ("out_prev", 1), ("low", 0), ("max", 6), ("low", 1), ("query", 0), ("max", 5), ("inverse", 6),
         ("low", 2), ("max", 4), ("low", 3), ("inverse", 4)]
DVE_B = [("query", 1), ("out", 0), ("max", 3), ("max", 2), ("low", 4), ("inverse", 2), ("max", 1), ("low", 5),
         ("max", 0), ("low", 6), ("inverse", 0)] + [("low", s) for s in range(7, NSTEP)]
ACT_A = [("out_prev", 1), ("high", 0), ("exp", 7), ("high", 1), ("exp", 6), ("high", 2), ("exp", 5), ("high", 3),
         ("exp", 4)]
ACT_B = [("out", 0), ("exp", 3), ("exp", 2), ("high", 4), ("high", 5), ("exp", 1), ("high", 6), ("exp", 0)] + [
    ("high", s) for s in range(7, NSTEP)]
POOL_A = [("weights", 0), ("norm", 7), ("norm", 6), ("query", 0), ("norm", 5), ("norm", 4)]
POOL_B = [("query", 1), ("norm", 3), ("norm", 2), ("norm", 1), ("norm", 0)]
NEXT_HEAD = {("project", 0), ("project", 1), ("query", 0), ("query", 1), ("weights", 0), ("inverse", 2),
             ("inverse", 0)} | {(w, i) for w in ("score", "max", "exp", "norm") for i in range(4)}
RING = 3

CHUNKS = [(0, 1), (1, 3), (3, 9), (9, UNITS)]
LAG = 2


def bass_adaln_attention_moe(nc, x_in, Wq, bq, Wkv, bkv, Wo, Wr, br, Wg_s, bg_s, Wu_s, bu_s, Wd_s, bd_s,
                             Wg, bg, Wu, bu, Wd, bd, c_in, wmod_in, eye_in, pe_in, mask_in, pick_in, out):
    with ExitStack() as ctx:
        def sb(name, shape, dt=F32):
            return ctx.enter_context(nc.sbuf_tensor(name, shape, dt))

        def psum(name, shape):
            return ctx.enter_context(nc.psum_tensor(name, shape, F32))

        def sem(name):
            return ctx.enter_context(nc.semaphore(name))

        x = sb("x", [P, BATCH * BLOCKS, P])
        eye = sb("eye", [P, P])
        eye_b = sb("eye_b", [P, P], BF16)
        mask = sb("mask", [P, P])
        mask_b = sb("mask_b", [P, P], BF16)
        mod = sb("mod", [P, BATCH, 6])
        cur = sb("cur", [P, 6])
        wq = sb("wq", [P, HEADS, P])
        wq_hl = sb("wq_hl", [P, 2, P], F32R)
        wkv = sb("wkv", [P, 2 * P])
        wkv_hl = sb("wkv_hl", [P, 2, 2 * P], F32R)
        wo_hl = sb("wo_hl", [P, 2, HEADS, P], F32R)
        bqT = sb("bqT", [P, HEADS])
        bkvT = sb("bkvT", [P, 2])
        peT = sb("peT", [P, TOKENS])
        stats = sb("stats", [P, BLOCKS, 6])
        mv = sb("mv", [P, BLOCKS, 2])
        var_eps = sb("var_eps", [P, BLOCKS])
        rstd = sb("rstd", [P, BLOCKS])
        minus_half = sb("minus_half", [P, BLOCKS])
        hT = sb("hT", [P, TOKENS])
        hT_hl = sb("hT_hl", [P, 2, TOKENS], F32R)
        kT_hl = sb("kT_hl", [P, 2, TOKENS], F32R)
        v_hl = sb("v_hl", [P, 2, TOKENS], F32R)
        qT = sb("qT", [P, TOKENS])
        qT_hl = sb("qT_hl", [P, 2, TOKENS], F32R)
        nmax = sb("nmax", [P, BLOCKS])
        total = sb("total", [P, BLOCKS])
        rtotal = sb("rtotal", [P, BLOCKS])
        probs = sb("probs", [P, PROB_AT[BLOCKS]])
        pT_hl = sb("pT_hl", [P, 2, RING, HALF], F32R)
        yT = sb("yT", [P, 2, HALF])
        arena = sb("arena", [P, 2 * HEADS * TOKENS], F32R)
        w3 = sb("w3", [P, 3, UNITS, P])
        b2 = sb("b2", [P, 2, UNITS])
        wr = sb("wr", [P, EXPERTS])
        br_rows = sb("br_rows", [P, EXPERTS])
        bd2 = sb("bd2", [2 * EXPERTS, P])
        bd_h = sb("bd_h", [2 * EXPERTS, P], F32R)
        bd_l = sb("bd_l", [2 * EXPERTS, P], F32R)
        bds = sb("bds", [P, 1])
        gate_bds = sb("gate_bds", [P, 1])
        cT = sb("cT", [P, 4, BATCH])
        c_inv = sb("c_inv", [P, BATCH])
        sign = sb("sign", [P, 2, BATCH])
        floor = sb("floor", [P, 2, BATCH])
        lg = sb("lg", [P, 4, EXPERTS])
        aff = sb("aff", [P, 4, EXPERTS])
        top = sb("top", [P, 4, TOP])
        rest = sb("rest", [P, 4, EXPERTS])
        chosen = sb("chosen", [P, 4, EXPERTS])
        top_sum = sb("top_sum", [P, 4])
        top_eps = sb("top_eps", [P, 4])
        top_inv = sb("top_inv", [P, 4])
        weight2 = sb("weight2", [P, 4, 2 * EXPERTS])
        ln_mod = sb("ln_mod", [P, 2])
        oT_hl = arena[:, :].rearrange("p (a h t) -> p a h t", a=2, h=HEADS)
        w3_hl = arena[:, 0:6 * UNITS * P].rearrange("p (a m u n) -> p a m u n", a=2, m=3, u=UNITS)
        xn = yT[:, :, :].rearrange("p u (k e) -> p (u k) e", e=P)
        wo = qT[:, :].rearrange("p (h e) -> p h e", h=HEADS)
        kT = hT
        wmod = probs[:, 0:6 * P]
        gs = probs[:, 0:2 * HALF].rearrange("p (r t) -> p r t", r=2)
        prod = probs[:, 2 * HALF:4 * HALF].rearrange("p (r t) -> p r t", r=2)
        hf = probs[:, 4 * HALF:6 * HALF].rearrange("p (r t) -> p r t", r=2)
        act_hl = kT_hl[:, :, :].rearrange("p a (r t) -> p a r t", r=2)
        x2T = hT[:, :].rearrange("p (r t) -> p r t", r=2)
        x2T_hl = hT_hl[:, :, :].rearrange("p a (r t) -> p a r t", r=2)
        weightT = v_hl[0:2 * EXPERTS, 0, :].rearrange("p (r t) -> p r t", r=2)
        pick_raw = [wq[0:2 * EXPERTS, :, :], wo[0:2 * EXPERTS, :, :]]
        pick = qT_hl[0:2 * EXPERTS, :, :].rearrange("p a (u n) -> p (a u) n", n=P)

        turned = [psum("turned0", [P, HALF]), psum("turned1", [P, HALF])]
        mixed = psum("mixed", [P, HALF])
        project = psum("project", [P, HALF])
        scores = [psum("scores0", [P, 2 * HALF]), psum("scores1", [P, 2 * HALF])]
        gate_ps = turned
        acc_ps = mixed
        misc_ps = project
        up_ps = [scores[0][:, 0:HALF], scores[0][:, HALF:]]
        weight_ps = [scores[1][:, 0:HALF], scores[1][:, HALF:]]

        mod_in = sem("mod_in")
        attn_in = sem("attn_in")
        x_first = sem("x_first")
        x_rest = sem("x_rest")
        ffn_in = sem("ffn_in")
        pick_loaded = sem("pick_loaded")
        stored = sem("stored")
        padded = sem("padded")
        c_exp = sem("c_exp")
        dve_setup = sem("dve_setup")
        mod_mm = sem("mod_mm")
        pool_setup = sem("pool_setup")
        ln_step = sem("ln_step")
        rstd_done = sem("rstd_done")
        xn_done = sem("xn_done")
        x_turned = sem("x_turned")
        hT_done = sem("hT_done")
        hT_high = sem("hT_high")
        hT_split = sem("hT_split")
        k_mm = sem("k_mm")
        k_sum = sem("k_sum")
        k_high = sem("k_high")
        k_split = sem("k_split")
        v_mm = sem("v_mm")
        v_high = sem("v_high")
        v_split = sem("v_split")
        wq_high = sem("wq_high")
        wq_split = sem("wq_split")
        q_mm = sem("q_mm")
        q_sum = sem("q_sum")
        q_high = sem("q_high")
        q_split = sem("q_split")
        score_mm = sem("score_mm")
        max_done = sem("max_done")
        exp_done = sem("exp_done")
        inverted = sem("inverted")
        normed = sem("normed")
        p_turned = sem("p_turned")
        p_high = sem("p_high")
        p_split = sem("p_split")
        applied = sem("applied")
        o_high = sem("o_high")
        o_split = sem("o_split")
        y_mm = sem("y_mm")
        y_done = sem("y_done")
        y_turned = sem("y_turned")
        x1_done = sem("x1_done")
        w_high = sem("w_high")
        w_split = sem("w_split")
        bd_high = sem("bd_high")
        bd_split = sem("bd_split")
        pick_done = sem("pick_done")
        ln2_step = sem("ln2_step")
        rstd2_done = sem("rstd2_done")
        xn2_done = sem("xn2_done")
        x2_turned = sem("x2_turned")
        x2_done = sem("x2_done")
        x2_high = sem("x2_high")
        x2_split = sem("x2_split")
        logit_mm = sem("logit_mm")
        logit_done = sem("logit_done")
        aff_done = sem("aff_done")
        route_step = sem("route_step")
        weight_done = sem("weight_done")
        weight_turned = sem("weight_turned")
        weight_high = sem("weight_high")
        weight_split = sem("weight_split")
        gate_mm = sem("gate_mm")
        up_mm = sem("up_mm")
        silu_done = sem("silu_done")
        prod_done = sem("prod_done")
        hidden = sem("hidden")
        act_high = sem("act_high")
        act_split = sem("act_split")
        down_mm = sem("down_mm")
        gate_cur = sem("gate_cur")
        y2_done = sem("y2_done")
        y2_turned = sem("y2_turned")
        out_done = sem("out_done")

        CREDIT = 2


        def f32(ap):
            return ap.bitcast(F32)

        def row(b):
            return bass.ds(b, 1)

        def wait_apart(engine, loaded, count, *waits):
            known = [(signal, value if isinstance(value, int) else engine.to_reg(value)) for signal, value in waits]
            engine.wait_ge(loaded, count)
            for signal, value in known:
                engine.wait_ge(signal, value)

        def split3(pe, to, left, right, first=True, last=True):
            for n, (a, c) in enumerate(PASSES):
                mm = pe.matmul(to, left[a], right[c], start=first and n == 0, stop=last and n == 2)
            return mm

        def hl(ap, *at):
            return [ap[(slice(None), part) + at] for part in (HI, LO)]

        def is_first(t):
            return isinstance(t, int) and t == 0

        block = ctx.enter_context(nc.Block())

        @block.sync
        def _(sp):
            sp.dma_start(cT[:, 0, :], c_in).then_inc(mod_in, 16)
            sp.dma_start(wmod, wmod_in).then_inc(mod_in, 16)
            xd = x_in.rearrange("b (n p) e -> b p n e", p=P)
            sp.dma_start(x[:, 0:BLOCKS, :], xd[0]).then_inc(x_first, 16)
            sp.dma_start(eye[:], eye_in).then_inc(attn_in, 16)
            sp.dma_start(wkv[:], Wkv).then_inc(attn_in, 16)
            sp.dma_start(wq[:], Wq.rearrange("e (h d) -> e h d", h=HEADS)).then_inc(attn_in, 16)
            sp.dma_start(peT[:], pe_in).then_inc(attn_in, 16)
            sp.dma_start(mask[:], mask_in).then_inc(attn_in, 16)
            sp.dma_start(bqT[:], bq).then_inc(attn_in, 16)
            sp.dma_start(bkvT[:], bkv).then_inc(attn_in, 16)
            sp.dma_start(wo[:], Wo.rearrange("(h d) e -> d h e", h=HEADS)).then_inc(attn_in, 16)
            for b in range(1, BATCH):
                sp.dma_start(x[:, b * BLOCKS:(b + 1) * BLOCKS, :], xd[b]).then_inc(x_rest, 16)
            sp.wait_ge(padded, 1)
            for m, (many, one) in enumerate(((Wg, Wg_s), (Wu, Wu_s))):
                sp.dma_start(w3[:, m, 0:PAIRS, :], many).then_inc(ffn_in, 16)
                sp.dma_start(w3[:, m, PAIRS, 0:INNER], one).then_inc(ffn_in, 16)
            sp.dma_start(w3[:, 2, 0:PAIRS, :], Wd).then_inc(ffn_in, 16)
            sp.dma_start(w3[0:INNER, 2, PAIRS, :], Wd_s).then_inc(ffn_in, 16)
            for m, (many, one) in enumerate(((bg, bg_s), (bu, bu_s))):
                sp.dma_start(b2[:, m, 0:PAIRS], many).then_inc(ffn_in, 16)
                sp.dma_start(b2[0:INNER, m, PAIRS:UNITS], one).then_inc(ffn_in, 16)
            sp.dma_start(bds[:], bd_s).then_inc(ffn_in, 16)
            sp.dma_start(wr[:], Wr).then_inc(ffn_in, 16)
            sp.dma_start(br_rows[:], br.rearrange("(a e) -> a e", a=1).broadcast_to([P, EXPERTS])).then_inc(ffn_in, 16)
            sp.dma_start(bd2[0:EXPERTS, :], bd).then_inc(ffn_in, 16)
            sp.dma_start(bd2[EXPERTS:, :], bd).then_inc(ffn_in, 16)
            sp.wait_ge(y_mm, 2 * BATCH)
            sp.wait_ge(wq_split, BATCH * HEADS)
            for k in range(2):
                sp.dma_start(pick_raw[k], pick_in[:, k * HEADS:(k + 1) * HEADS, :]).then_inc(pick_loaded, 16)
            od = out.rearrange("b (n p) e -> p (b n) e", p=P)
            with sp.Fori(0, BATCH * TILES) as t:
                sp.wait_ge(out_done, t + 1)
                sp.dma_start(od[:, bass.ds(t * 4, 4), :], x[:, bass.ds(t * 4, 4), :]).then_inc(stored, 16)
            sp.wait_ge(stored, 16 * BATCH * TILES)

        ATTN_IN = 16 * 8
        FFN_IN = 16 * 15

        @block.gpsimd
        def _(pool):
            pool.memset(minus_half[:], -0.5).then_inc(pool_setup, 1)
            pool.sem_inc(q_split, CREDIT)
            pool.sem_inc(act_split, CREDIT)
            pool.wait_ge(attn_in, ATTN_IN)
            pool.tensor_scalar(wkv_hl[:, HI, :], wkv[:], 1.0, 1.0, ALU.mult, ALU.mult).then_inc(pool_setup, 1)
            pool.wait_ge(pool_setup, 2)
            pool.tensor_tensor(wkv_hl[:, LO, :], wkv[:], f32(wkv_hl[:, HI, :]), ALU.subtract).then_inc(pool_setup, 1)
            pool.tensor_scalar(eye_b[:], eye[:], 1.0, 1.0, ALU.mult, ALU.mult)
            pool.tensor_scalar(mask_b[:], mask[:], 1.0, 1.0, ALU.mult, ALU.mult)
            pool.tensor_scalar(wo_hl[:, HI, :, :], wo[:], 1.0, 1.0, ALU.mult, ALU.mult).then_inc(pool_setup, 1)
            pool.wait_ge(pool_setup, 4)
            pool.tensor_tensor(wo_hl[:, LO, :, :], wo[:], f32(wo_hl[:, HI, :, :]), ALU.subtract).then_inc(pool_setup, 1)

            def weights(n, h):
                pool.tensor_copy(wq_hl[:, HI, :], wq[:, row(h), :].rearrange("p a d -> p (a d)")).then_inc(wq_high, 1)
                wait_apart(pool, attn_in, ATTN_IN, (wq_high, n + 1))
                pool.tensor_tensor(wq_hl[:, LO, :], wq[:, row(h), :].rearrange("p a d -> p (a d)"),
                                   f32(wq_hl[:, HI, :]), ALU.subtract).then_inc(wq_split, 1)

            def query(n, u):
                at = slice(u * HALF, (u + 1) * HALF)
                wait_apart(pool, attn_in, ATTN_IN, (q_sum, CREDIT + 2 * n + u + 1))
                pool.tensor_scalar(qT_hl[:, HI, at], qT[:, at], 1.0, 1.0, ALU.mult, ALU.mult).then_inc(q_high, 1)
                pool.wait_ge(q_high, 2 * n + u + 1)
                pool.tensor_tensor(qT_hl[:, LO, at], qT[:, at], f32(qT_hl[:, HI, at]), ALU.subtract).then_inc(q_split, 1)

            def norm(n, i):
                wait_apart(pool, attn_in, ATTN_IN, (inverted, 4 * n + PLACE[i] // 2 + 1))
                at = slice(PROB_AT[i], PROB_AT[i + 1])
                pool.tensor_scalar(probs[:, at], probs[:, at], rtotal[:, i:i + 1], 1.0, ALU.mult, ALU.mult)\
                    .then_inc(normed, 1)

            def segment(todo, n, h, more):
                for what, i in todo:
                    if (what, i) in NEXT_HEAD:
                        if more:
                            {"weights": lambda n, i: weights(n, h + 1), "norm": norm, "query": query}[what](n + 1, i)
                    else:
                        norm(n, i)

            with pool.Fori(0, BATCH) as b:
                wait_apart(pool, attn_in, ATTN_IN, (ln_step, b * 3 + 3))
                pool.tensor_tensor(rstd[:], var_eps[:], minus_half[:], ALU.pow).then_inc(rstd_done, 1)
                for u in range(2):
                    at = slice(u * HALF, (u + 1) * HALF)
                    wait_apart(pool, attn_in, ATTN_IN, (hT_done, b * 2 + u + 1))
                    pool.tensor_scalar(hT_hl[:, HI, at], hT[:, at], 1.0, 1.0, ALU.mult, ALU.mult).then_inc(hT_high, 1)
                    pool.wait_ge(hT_high, b * 2 + u + 1)
                    pool.tensor_tensor(hT_hl[:, LO, at], hT[:, at], f32(hT_hl[:, HI, at]), ALU.subtract)\
                        .then_inc(hT_split, 1)
                first = b * HEADS
                weights(first, 0)
                for u in range(2):
                    query(first, u)
                for i in ORDER[0:4]:
                    norm(first, i)
                segment(POOL_A, first, 0, True)
                with pool.Fori(0, HEADS - 2) as h:
                    segment(POOL_B, first + h, h, True)
                    segment(POOL_A, first + (h + 1), h + 1, True)
                segment(POOL_B, first + (HEADS - 2), HEADS - 2, True)
                segment(POOL_A, first + (HEADS - 1), HEADS - 1, False)
                segment(POOL_B, first + (HEADS - 1), HEADS - 1, False)

            pool.wait_ge(ffn_in, FFN_IN)
            pool.wait_ge(pick_loaded, 32)
            for k in range(2):
                pool.tensor_scalar(pick[:, k * HEADS:(k + 1) * HEADS, :], pick_raw[k], 1.0, 1.0, ALU.mult, ALU.mult).then_inc(pick_done, 1)

            def rstd2(t):
                wait_apart(pool, ffn_in, FFN_IN, (ln2_step, t * 3 + 3))
                pool.tensor_tensor(rstd[:, 0:4], var_eps[:, 0:4], minus_half[:, 0:4], ALU.pow).then_inc(rstd2_done, 1)

            def split_x2(t, r):
                wait_apart(pool, ffn_in, FFN_IN, (x2_done, t + 1))
                pool.tensor_scalar(x2T_hl[:, HI, r, :], x2T[:, r, :], 1.0, 1.0, ALU.mult, ALU.mult).then_inc(x2_high, 1)
                pool.wait_ge(x2_high, t + 1)
                pool.tensor_tensor(x2T_hl[:, LO, r, :], x2T[:, r, :], f32(x2T_hl[:, HI, r, :]), ALU.subtract)\
                    .then_inc(x2_split, 1)

            def split_hidden(g, r):
                wait_apart(pool, ffn_in, FFN_IN, (down_mm, CREDIT + g - 1), (hidden, g + 1))
                pool.tensor_scalar(act_hl[:, HI, r, :], hf[:, r, :], 1.0, 1.0, ALU.mult, ALU.mult).then_inc(act_high, 1)
                pool.wait_ge(act_high, g + 1)
                pool.tensor_tensor(act_hl[:, LO, r, :], hf[:, r, :], f32(act_hl[:, HI, r, :]), ALU.subtract)\
                    .then_inc(act_split, 1)

            def tile_body(b, u, more):
                t = b * TILES + u
                for p in range(UNITS):
                    split_hidden(t * UNITS + p, (u + p) % 2)
                    if more and p == 4:
                        rstd2(t + 1)
                    if more and p == 7:
                        split_x2(t + 1, (u + 1) % 2)

            rstd2(0)
            split_x2(0, 0)
            with pool.Fori(0, BATCH - 1) as b:
                tile_body(b, 0, True)
                tile_body(b, 1, True)
            tile_body(BATCH - 1, 0, True)
            tile_body(BATCH - 1, 1, False)

        @block.vector
        def _(dve):
            dve.sem_inc(q_sum, CREDIT)
            dve.sem_inc(p_split, CREDIT)
            dve.sem_inc(o_split, CREDIT)
            dve.memset(w3[:, 0:2, PAIRS, INNER:], 0.0)
            dve.memset(w3[INNER:, 2, PAIRS, :], 0.0)
            dve.memset(b2[INNER:, :, PAIRS:UNITS], 0.0).then_inc(padded, 1)
            dve.wait_ge(c_exp, 1)
            dve.tensor_scalar(cT[:, 2, :], cT[:, 1, :], 1.0, None, ALU.add).then_inc(dve_setup, 1)
            dve.wait_ge(dve_setup, 1)
            dve.reciprocal(c_inv[:], cT[:, 2, :]).then_inc(dve_setup, 1)
            dve.wait_ge(dve_setup, 2)
            dve.tensor_tensor(cT[:, 3, :], cT[:, 0, :], c_inv[:], ALU.mult).then_inc(dve_setup, 1)
            dve.wait_ge(mod_mm, 1)
            dve.tensor_copy(mod[:].rearrange("p b j -> p j b"),
                            project[:, 0:6 * BATCH].rearrange("p (j b) -> p j b", j=6)).then_inc(dve_setup, 1)
            dve.wait_ge(dve_setup, 4)
            gates = list(enumerate((GATE_A, GATE_F)))
            for k, j in gates:
                last = dve.tensor_scalar(sign[:, k, :], mod[:, :, j], 0.0, 2.0, ALU.is_ge, ALU.mult)
            last.then_inc(dve_setup, 1)
            dve.wait_ge(dve_setup, 5)
            for k, j in gates:
                last = dve.scalar_tensor_tensor(floor[:, k, :], sign[:, k, :], -1.0, mod[:, :, j], ALU.add, ALU.mult)
            last.then_inc(dve_setup, 1)
            dve.wait_ge(dve_setup, 6)
            dve.tensor_scalar(floor[:], floor[:], 0.25, None, ALU.max).then_inc(dve_setup, 1)
            dve.wait_ge(dve_setup, 7)
            for k, j in gates:
                dve.scalar_tensor_tensor(mod[:, :, j], sign[:, k, :], -1.0, floor[:, k, :], ALU.add, ALU.mult)
            for j in (SCALE_A, SCALE_F):
                last = dve.tensor_scalar(mod[:, :, j], mod[:, :, j], 1.0, None, ALU.add)
            last.then_inc(dve_setup, 1)
            dve.wait_ge(dve_setup, 8)

            def query(n, u):
                at = slice(u * HALF, (u + 1) * HALF)
                dve.wait_ge(q_split, CREDIT + 2 * n + u - 1)
                dve.wait_ge(q_mm, 2 * n + u + 1)
                return at

            def query_of(n, h, u):
                at = query(n, u)
                dve.scalar_tensor_tensor(qT[:, at], project[:], bqT[:, row(h)], peT[:, at], ALU.add, ALU.add)\
                    .then_inc(q_sum, 1)

            def maximum(n, i):
                k = PLACE[i]
                dve.wait_ge(score_mm, BLOCKS * n + k + 1)
                dve.tensor_reduce(nmax[:, i:i + 1], scores[k % 2][:, 0:P * (i + 1)], AX_X, ALU.max, negate=True)\
                    .then_inc(max_done, 1)

            def inverse(n, i):
                dve.wait_ge(exp_done, BLOCKS * n + PLACE[i] + 1)
                dve.reciprocal(rtotal[:, i:i + 2], total[:, i:i + 2]).then_inc(inverted, 1)

            def low(n, s):
                u, j = STEPS[s]
                at = slice(P * max(j - 4 * u, 0), HALF)
                dve.wait_ge(p_high, NSTEP * n + s + 1)
                dve.tensor_tensor(pT_hl[:, LO, s % RING, at], turned[s % 2][:, at], f32(pT_hl[:, HI, s % RING, at]),
                                  ALU.subtract).then_inc(p_split, 1)

            def out_low(n, h, u):
                at = slice(u * HALF, (u + 1) * HALF)
                dve.wait_ge(o_high, 2 * n + u + 1)
                dve.scalar_tensor_tensor(oT_hl[:, LO, row(h), at].rearrange("p a t -> p (a t)"), mixed[:], bkvT[:, 1:2],
                                         f32(oT_hl[:, HI, row(h), at].rearrange("p a t -> p (a t)")),
                                         ALU.add, ALU.subtract).then_inc(o_split, 1)

            def segment(todo, n, h, more, prev):
                for what, i in todo:
                    m, k = (n + 1, h + 1) if (what, i) in NEXT_HEAD else (n, h)
                    if (what, i) in NEXT_HEAD and not more:
                        continue
                    if what == "max":
                        maximum(m, i)
                    elif what == "inverse":
                        inverse(m, i)
                    elif what == "query":
                        query_of(m, k, i)
                    elif what == "low":
                        low(m, i)
                    elif what == "out":
                        out_low(n, h, i)
                    elif prev:
                        out_low(n - 1, h - 1, i)

            dve.wait_ge(x_first, 16)
            with dve.Fori(0, BATCH) as b:
                dve.tensor_copy(cur[:], mod[:, row(b), :].rearrange("p a j -> p (a j)"))
                for k in range(BLOCKS):
                    last = dve.bn_stats(stats[:, k, :], x[:, row(b * BLOCKS + k), :].rearrange("p a e -> p (a e)"))
                last.then_inc(ln_step, 1)
                wait_apart(dve, x_first, 16, (ln_step, b * 3 + 1))
                for k in range(BLOCKS):
                    last = dve.bn_aggr(mv[:, k, :], stats[:, k, :])
                last.then_inc(ln_step, 1)
                dve.wait_ge(ln_step, b * 3 + 2)
                dve.tensor_scalar(var_eps[:], mv[:, :, 1], LN_EPS, None, ALU.add).then_inc(ln_step, 1)
                dve.wait_ge(rstd_done, b + 1)
                for k in range(BLOCKS):
                    last = dve.tensor_scalar(xn[:, k, :], x[:, row(b * BLOCKS + k), :].rearrange("p a e -> p (a e)"),
                                             mv[:, k, 0:1], rstd[:, k:k + 1], ALU.subtract, ALU.mult)
                last.then_inc(xn_done, 1)
                for u in range(2):
                    at = slice(u * HALF, (u + 1) * HALF)
                    dve.wait_ge(k_mm, b * 2 + u + 1)
                    dve.scalar_tensor_tensor(kT[:, at], scores[1][:, at], bkvT[:, 0:1], peT[:, at], ALU.add, ALU.add)\
                        .then_inc(k_sum, 1)
                first = b * HEADS
                query_of(first, 0, 0)
                for u in range(2):
                    at = slice(u * HALF, (u + 1) * HALF)
                    dve.wait_ge(k_high, b * 2 + u + 1)
                    dve.scalar_tensor_tensor(kT_hl[:, LO, at], kT[:, at], SCALE, f32(kT_hl[:, HI, at]),
                                             ALU.mult, ALU.subtract).then_inc(k_split, 1)
                query_of(first, 0, 1)
                for u in range(2):
                    at = slice(u * HALF, (u + 1) * HALF)
                    dve.wait_ge(v_high, b * 2 + u + 1)
                    dve.tensor_tensor(v_hl[:, LO, at], turned[u][:], f32(v_hl[:, HI, at]), ALU.subtract)\
                        .then_inc(v_split, 1)
                for i in ORDER[0:4]:
                    maximum(first, i)
                    if i % 2 == 0:
                        inverse(first, i)
                dve.wait_ge(x_rest, 16 * (BATCH - 1))
                segment(DVE_A, first, 0, True, False)
                with dve.Fori(0, HEADS - 2) as h:
                    segment(DVE_B, first + h, h, True, True)
                    segment(DVE_A, first + (h + 1), h + 1, True, True)
                segment(DVE_B, first + (HEADS - 2), HEADS - 2, True, True)
                segment(DVE_A, first + (HEADS - 1), HEADS - 1, False, True)
                segment(DVE_B, first + (HEADS - 1), HEADS - 1, False, True)
                out_low(first + (HEADS - 1), HEADS - 1, 1)
                for u in range(2):
                    dve.wait_ge(y_turned, b * 2 + u + 1)
                    rows = x[:, bass.ds(b * BLOCKS + 4 * u, 4), :]
                    dve.tensor_tensor(rows, scores[1][:, u * HALF:(u + 1) * HALF].rearrange("p (k e) -> p k e", k=4),
                                      rows, ALU.add).then_inc(x1_done, 1)

            def stats2(t, b):
                dve.wait_ge(x1_done, 2 * BATCH)
                dve.tensor_copy(ln_mod[:], mod[:, row(b), SHIFT_F:SCALE_F + 1].rearrange("p a j -> p (a j)"))
                for k in range(4):
                    last = dve.bn_stats(stats[:, k, :], x[:, row(t * 4 + k), :].rearrange("p a e -> p (a e)"))
                last.then_inc(ln2_step, 1)
                wait_apart(dve, ffn_in, FFN_IN, (ln2_step, t * 3 + 1))
                for k in range(4):
                    last = dve.bn_aggr(mv[:, k, :], stats[:, k, :])
                last.then_inc(ln2_step, 1)
                dve.wait_ge(ln2_step, t * 3 + 2)
                dve.tensor_scalar(var_eps[:, 0:4], mv[:, 0:4, 1], LN_EPS, None, ALU.add).then_inc(ln2_step, 1)

            def normalise2(t):
                dve.wait_ge(rstd2_done, t + 1)
                for k in range(4):
                    last = dve.tensor_scalar(xn[:, k, :], x[:, row(t * 4 + k), :].rearrange("p a e -> p (a e)"),
                                             mv[:, k, 0:1], rstd[:, k:k + 1], ALU.subtract, ALU.mult)
                last.then_inc(xn2_done, 1)

            def add_br(t):
                dve.wait_ge(logit_mm, t + 1)
                for k in range(4):
                    last = dve.tensor_tensor(lg[:, k, :], misc_ps[:, k * EXPERTS:(k + 1) * EXPERTS], br_rows[:], ALU.add)
                last.then_inc(logit_done, 1)

            def route(t):
                wait_apart(dve, ffn_in, FFN_IN, (aff_done, t + 1))
                for k in range(4):
                    last = dve.max(top[:, k, :], aff[:, k, :])
                last.then_inc(route_step, 1)
                wait_apart(dve, ffn_in, FFN_IN, (route_step, t * 4 + 1))
                for k in range(4):
                    dve.match_replace(rest[:, k, :], top[:, k, :], aff[:, k, :], 0.0)
                dve.tensor_reduce(top_sum[:], top[:], AX_X, ALU.add).then_inc(route_step, 1)
                dve.wait_ge(route_step, t * 4 + 2)
                dve.tensor_tensor(chosen[:], aff[:], rest[:], ALU.subtract)
                dve.tensor_scalar(top_eps[:], top_sum[:], 1e-9, None, ALU.add).then_inc(route_step, 1)
                dve.wait_ge(route_step, t * 4 + 3)
                dve.reciprocal(top_inv[:], top_eps[:]).then_inc(route_step, 1)
                dve.wait_ge(route_step, t * 4 + 4)
                for k in range(4):
                    for c in range(2):
                        last = dve.tensor_scalar(weight2[:, k, c * EXPERTS:(c + 1) * EXPERTS], chosen[:, k, :],
                                                 top_inv[:, k:k + 1], None, ALU.mult)
                last.then_inc(weight_done, 1)

            def split_weight(t, r):
                dve.wait_ge(weight_turned, t + 1)
                dve.tensor_copy(weightT[:, r, :], misc_ps[0:2 * EXPERTS, :]).then_inc(weight_high, 1)
                dve.wait_ge(weight_high, t + 1)
                dve.tensor_tensor(weightT[EXPERTS:, r, :], misc_ps[EXPERTS:2 * EXPERTS, :],
                                  f32(weightT[EXPERTS:, r, :]), ALU.subtract).then_inc(weight_split, 1)

            def hidden_of(t, p, r):
                g = t * UNITS + p
                dve.wait_ge(silu_done, g + 1)
                dve.wait_ge(up_mm, g + 1)
                if p == PAIRS:
                    dve.wait_ge(act_split, CREDIT + g - 1)
                    dve.scalar_tensor_tensor(hf[:, r, :], up_ps[r], b2[:, 1, p:p + 1], gs[:, r, :], ALU.add, ALU.mult)\
                        .then_inc(hidden, 1)
                    return
                dve.scalar_tensor_tensor(prod[:, r, :], up_ps[r], b2[:, 1, p:p + 1], gs[:, r, :], ALU.add, ALU.mult)\
                    .then_inc(prod_done, 1)
                dve.wait_ge(act_split, CREDIT + g - 1)
                dve.wait_ge(prod_done, t * PAIRS + p + 1)
                dve.tensor_tensor(hf[:, r, :], prod[:, r, :], weight_ps[r], ALU.mult).then_inc(hidden, 1)

            def gate_of(b):
                dve.wait_ge(y2_done, b * TILES + 1)
                dve.tensor_copy(cur[:, GATE_F:], mod[:, row(b), GATE_F:].rearrange("p a j -> p (a j)"))
                dve.tensor_tensor(gate_bds[:], mod[:, row(b), GATE_F:].rearrange("p a j -> p (a j)"), bds[:], ALU.mult)\
                    .then_inc(gate_cur, 1)

            def add_out(t):
                dve.wait_ge(y2_turned, t + 1)
                rows = x[:, bass.ds(t * 4, 4), :]
                dve.tensor_tensor(rows, misc_ps[:].rearrange("p (k e) -> p k e", k=4), rows, ALU.add)\
                    .then_inc(out_done, 1)

            def tile_body(b, u, more):
                t = b * TILES + u
                r1 = (u + 1) % 2
                for p in range(LAG + 1, UNITS):
                    hidden_of(t, p, (u + p) % 2)
                    if p == 3 and u == 0:
                        gate_of(b)
                    if more:
                        if p == 3:
                            stats2(t + 1, b + u)
                        if p == 5:
                            normalise2(t + 1)
                        if p == 9:
                            add_br(t + 1)
                        if p == 11:
                            route(t + 1)
                        if p == 13:
                            split_weight(t + 1, r1)
                if more:
                    for p in range(LAG + 1):
                        hidden_of(t + 1, p, (r1 + p) % 2)
                add_out(t)

            dve.wait_ge(ffn_in, FFN_IN)
            dve.memset(f32(bd_l[:]), 0.0)
            dve.tensor_copy(bd_h[:], bd2[:]).then_inc(bd_high, 1)
            dve.wait_ge(bd_high, 1)
            dve.tensor_tensor(bd_l[0:EXPERTS, :], bd2[0:EXPERTS, :], f32(bd_h[0:EXPERTS, :]), ALU.subtract)\
                .then_inc(bd_split, 1)
            stats2(0, 0)
            normalise2(0)
            n = 0
            for a, c in CHUNKS:
                for m in range(3):
                    n += 1
                    dve.wait_ge(w_high, n)
                    dve.tensor_tensor(w3_hl[:, LO, m, a:c, :], w3[:, m, a:c, :], f32(w3_hl[:, HI, m, a:c, :]),
                                      ALU.subtract).then_inc(w_split, 1)
                if a == 0:
                    add_br(0)
                    route(0)
                    split_weight(0, 0)
            for p in range(LAG + 1):
                hidden_of(0, p, p % 2)
            with dve.Fori(0, BATCH - 1) as b:
                tile_body(b, 0, True)
                tile_body(b, 1, True)
            tile_body(BATCH - 1, 0, True)
            tile_body(BATCH - 1, 1, False)

        @block.scalar
        def _(act):
            act.sem_inc(y2_done, 1)
            act.wait_ge(mod_in, 32)
            act.activation(cT[:, 1, :], cT[:, 0, :], ACT.Exp, scale=-1.0).then_inc(c_exp, 1)

            def exponent(n, i):
                k = PLACE[i]
                act.wait_ge(max_done, BLOCKS * n + k + 1)
                act.activation(probs[:, PROB_AT[i]:PROB_AT[i + 1]], scores[k % 2][:, 0:P * (i + 1)], ACT.Exp,
                               bias=nmax[:, i:i + 1], accum_out=total[:, i:i + 1]).then_inc(exp_done, 1)

            def high(n, s):
                u, j = STEPS[s]
                at = slice(P * max(j - 4 * u, 0), HALF)
                act.wait_ge(applied, NSTEP * n + s + 1)
                act.wait_ge(p_turned, NSTEP * n + s + 1)
                act.activation(pT_hl[:, HI, s % RING, at], turned[s % 2][:, at], ACT.Copy).then_inc(p_high, 1)

            def out_high(n, h, u):
                at = slice(u * HALF, (u + 1) * HALF)
                wait_apart(act, attn_in, ATTN_IN, (applied, RING + NSTEP * n + (4, 12)[u]))
                act.activation(oT_hl[:, HI, row(h), at].rearrange("p a t -> p (a t)"), mixed[:], ACT.Identity,
                               bias=bkvT[:, 1:2]).then_inc(o_high, 1)

            def segment(todo, n, h, more, prev):
                for what, i in todo:
                    if what == "exp":
                        if (what, i) not in NEXT_HEAD:
                            exponent(n, i)
                        elif more:
                            exponent(n + 1, i)
                    elif what == "high":
                        high(n, i)
                    elif what == "out":
                        out_high(n, h, i)
                    elif prev:
                        out_high(n - 1, h - 1, i)

            with act.Fori(0, BATCH) as b:
                for u in range(2):
                    at = slice(u * HALF, (u + 1) * HALF)
                    act.wait_ge(x_turned, b * 2 + u + 1)
                    act.activation(hT[:, at], scores[0][:, at], ACT.Identity, bias=cur[:, SHIFT_A:SHIFT_A + 1],
                                   scale=cur[:, SCALE_A:SCALE_A + 1]).then_inc(hT_done, 1)
                for u in range(2):
                    at = slice(u * HALF, (u + 1) * HALF)
                    act.wait_ge(k_sum, b * 2 + u + 1)
                    act.activation(kT_hl[:, HI, at], kT[:, at], ACT.Copy, scale=SCALE).then_inc(k_high, 1)
                for u in range(2):
                    at = slice(u * HALF, (u + 1) * HALF)
                    act.wait_ge(v_mm, b * 2 + u + 1)
                    act.activation(v_hl[:, HI, at], turned[u][:], ACT.Copy).then_inc(v_high, 1)
                first = b * HEADS
                for i in ORDER[0:4]:
                    exponent(first, i)
                segment(ACT_A, first, 0, True, False)
                with act.Fori(0, HEADS - 2) as h:
                    segment(ACT_B, first + h, h, True, True)
                    segment(ACT_A, first + (h + 1), h + 1, True, True)
                segment(ACT_B, first + (HEADS - 2), HEADS - 2, True, True)
                segment(ACT_A, first + (HEADS - 1), HEADS - 1, False, True)
                segment(ACT_B, first + (HEADS - 1), HEADS - 1, False, True)
                out_high(first + (HEADS - 1), HEADS - 1, 1)
                for u in range(2):
                    act.wait_ge(y_mm, b * 2 + u + 1)
                    act.activation(yT[:, u, :], scores[0][:, u * HALF:(u + 1) * HALF], ACT.Identity,
                                   scale=cur[:, GATE_A:GATE_A + 1]).then_inc(y_done, 1)

            act.wait_ge(ffn_in, FFN_IN)
            act.wait_ge(y_mm, 2 * BATCH)

            def modulate2(t, r):
                act.wait_ge(x2_turned, t + 1)
                act.activation(x2T[:, r, :], misc_ps[:], ACT.Identity, bias=ln_mod[:, 0:1], scale=ln_mod[:, 1:2])\
                    .then_inc(x2_done, 1)

            def affinity(t):
                act.wait_ge(logit_done, t + 1)
                act.activation(aff[:], lg[:], ACT.Sigmoid).then_inc(aff_done, 1)

            def silu(t, p, r):
                g = t * UNITS + p
                if p >= 2 or not is_first(t):
                    act.wait_ge(hidden, g - 1)
                act.wait_ge(gate_mm, g + 1)
                act.activation(gs[:, r, :], gate_ps[r][:], ACT.Silu, bias=b2[:, 0, p:p + 1]).then_inc(silu_done, 1)

            def gated_out(t, b):
                act.wait_ge(gate_cur, b + 1)
                act.wait_ge(down_mm, CREDIT + (t + 1) * UNITS)
                act.activation(yT[:, 1, :], acc_ps[:], ACT.Identity, bias=gate_bds[:], scale=cur[:, GATE_F:])\
                    .then_inc(y2_done, 1)

            def tile_body(b, u, more):
                t = b * TILES + u
                r1 = (u + 1) % 2
                for p in range(LAG + 1, UNITS):
                    silu(t, p, (u + p) % 2)
                    if more and p == 6:
                        modulate2(t + 1, r1)
                    if more and p == 10:
                        affinity(t + 1)
                if more:
                    for p in range(2):
                        silu(t + 1, p, (r1 + p) % 2)
                gated_out(t, b)
                if more:
                    silu(t + 1, 2, r1)

            modulate2(0, 0)
            for a, c in CHUNKS:
                for m in range(3):
                    act.activation(w3_hl[:, HI, m, a:c, :], w3[:, m, a:c, :], ACT.Copy).then_inc(w_high, 1)
                if a == 0:
                    affinity(0)
            for p in range(LAG + 1):
                silu(0, p, p % 2)
            with act.Fori(0, BATCH - 1) as b:
                tile_body(b, 0, True)
                tile_body(b, 1, True)
            tile_body(BATCH - 1, 0, True)
            tile_body(BATCH - 1, 1, False)

        @block.tensor
        def _(pe):
            pe.sem_inc(applied, RING)
            pe.sem_inc(down_mm, CREDIT)
            pe.wait_ge(mod_in, 32)
            pe.wait_ge(dve_setup, 3)
            for j in range(6):
                mm = pe.matmul(project[:, j * BATCH:(j + 1) * BATCH], wmod[:, j * P:(j + 1) * P], cT[:, 3, :],
                               start=True, stop=True)
            mm.then_inc(mod_mm, 1)
            pe.wait_ge(attn_in, ATTN_IN)
            pe.wait_ge(pool_setup, 5)

            def project_q(n, u):
                at = slice(u * HALF, (u + 1) * HALF)
                pe.wait_ge(wq_split, n + 1)
                pe.wait_ge(q_sum, CREDIT + 2 * n + u)
                split3(pe, project[:], hl(wq_hl), hl(hT_hl, at)).then_inc(q_mm, 1)

            def score(n, i, wait=True):
                k, u = PLACE[i], i // 4
                pe.wait_ge(q_split, CREDIT + 2 * n + u + 1)
                if wait:
                    pe.wait_ge(exp_done, BLOCKS * n + k - 1)
                width = P * (i + 1)
                diagonal = slice(P * i, width)
                for c in range(0, width, HALF):
                    at = slice(c, min(c + HALF, width))
                    q, kk = hl(qT_hl, slice(P * i, P * (i + 1))), hl(kT_hl, at)
                    pe.matmul(scores[k % 2][:, at], q[HI], kk[HI], start=True, stop=False)
                    if at.stop == width:
                        pe.matmul(scores[k % 2][:, diagonal], eye_b[:], mask_b[:], start=False, stop=False)
                    pe.matmul(scores[k % 2][:, at], q[HI], kk[LO], start=False, stop=False)
                    mm = pe.matmul(scores[k % 2][:, at], q[LO], kk[HI], start=False, stop=True)
                mm.then_inc(score_mm, 1)

            def turn(n, s):
                u, j = STEPS[s]
                pe.wait_ge(normed, BLOCKS * n + 4 * (u + 1))
                pe.wait_ge(p_split, CREDIT + NSTEP * n + s - 1)
                for i in range(max(j, 4 * u), 4 * (u + 1)):
                    mm = pe.transpose(turned[s % 2][:, P * (i - 4 * u):P * (i - 4 * u + 1)],
                                      probs[:, PROB_AT[i] + P * j:PROB_AT[i] + P * (j + 1)], eye[:])
                mm.then_inc(p_turned, 1)

            def apply(n, s):
                u, j = STEPS[s]
                at = slice(P * max(j - 4 * u, 0), HALF)
                pe.wait_ge(p_split, CREDIT + NSTEP * n + s + 1)
                if j == 0:
                    pe.wait_ge(o_split, CREDIT + 2 * n + u)
                values = hl(v_hl, slice(P * j, P * (j + 1)))
                split3(pe, mixed[:, at], values, [pT_hl[:, a, s % RING, at] for a in (HI, LO)],
                       first=(j == 0), last=(j == 4 * u + 3)).then_inc(applied, 1)

            def segment(todo, n, more):
                for what, i in todo:
                    m = n + 1 if (what, i) in NEXT_HEAD else n
                    if (what, i) in NEXT_HEAD and not more:
                        continue
                    {"score": score, "turn": turn, "apply": apply, "project": project_q}[what](m, i)

            with pe.Fori(0, BATCH) as b:
                pe.wait_ge(xn_done, b + 1)
                for u in range(2):
                    for k in range(4 * u, 4 * u + 4):
                        mm = pe.transpose(scores[0][:, P * k:P * (k + 1)], xn[:, k, :], eye[:])
                    mm.then_inc(x_turned, 1)
                for u in range(2):
                    at = slice(u * HALF, (u + 1) * HALF)
                    pe.wait_ge(hT_split, b * 2 + u + 1)
                    split3(pe, scores[1][:, at], hl(wkv_hl, slice(0, P)), hl(hT_hl, at)).then_inc(k_mm, 1)
                first = b * HEADS
                project_q(first, 0)
                for u in range(2):
                    for k in range(4 * u, 4 * u + 4):
                        mm = split3(pe, turned[u][:, P * (k - 4 * u):P * (k - 4 * u + 1)],
                                    hl(hT_hl, slice(P * k, P * (k + 1))), hl(wkv_hl, slice(P, 2 * P)))
                    mm.then_inc(v_mm, 1)
                project_q(first, 1)
                pe.wait_ge(k_split, b * 2 + 2)
                pe.wait_ge(v_split, b * 2 + 2)
                for i in ORDER[0:4]:
                    score(first, i, wait=PLACE[i] >= 2)
                segment(PE_A, first, True)
                with pe.Fori(0, HEADS - 2) as h:
                    segment(PE_B, first + h, True)
                    segment(PE_A, first + (h + 1), True)
                segment(PE_B, first + (HEADS - 2), True)
                segment(PE_A, first + (HEADS - 1), False)
                segment(PE_B, first + (HEADS - 1), False)
                pe.wait_ge(o_split, CREDIT + b * 2 * HEADS + 2 * HEADS)
                for u in range(2):
                    at = slice(u * HALF, (u + 1) * HALF)
                    for h in range(HEADS):
                        mm = split3(pe, scores[0][:, at], hl(wo_hl, h), hl(oT_hl, h, at),
                                    first=(h == 0), last=(h == HEADS - 1))
                    mm.then_inc(y_mm, 1)
                for u in range(2):
                    pe.wait_ge(y_done, b * 2 + u + 1)
                    for k in range(4):
                        mm = pe.transpose(scores[1][:, u * HALF + P * k:u * HALF + P * (k + 1)],
                                          yT[:, u, P * k:P * (k + 1)], eye[:])
                    mm.then_inc(y_turned, 1)

            def turn_x2(t):
                pe.wait_ge(xn2_done, t + 1)
                for k in range(4):
                    mm = pe.transpose(misc_ps[:, P * k:P * (k + 1)], xn[:, k, :], eye[:])
                mm.then_inc(x2_turned, 1)

            def logits(t, r):
                pe.wait_ge(x2_done, t + 1)
                for k in range(4):
                    mm = pe.matmul(misc_ps[:, EXPERTS * k:EXPERTS * (k + 1)], x2T[:, r, P * k:P * (k + 1)], wr[:],
                                   start=True, stop=True)
                mm.then_inc(logit_mm, 1)

            def turn_weights(t):
                wait_apart(pe, pool_setup, 5, (weight_done, t + 1))
                for k in range(4):
                    mm = pe.transpose(misc_ps[0:2 * EXPERTS, P * k:P * (k + 1)], weight2[:, k, :], eye[:])
                mm.then_inc(weight_turned, 1)

            def up_gate(t, g, p, q, r):
                if p == 0:
                    pe.wait_ge(x2_split, t + 1)
                    pe.wait_ge(weight_split, t + 1)
                pe.wait_ge(silu_done, g - 1) if p >= 2 or not is_first(t) else None
                right = [x2T_hl[:, a, q, :] for a in (HI, LO)]
                split3(pe, gate_ps[r][:], hl(w3_hl, 0, p), right).then_inc(gate_mm, 1)
                if p >= 2 or not is_first(t):
                    pe.wait_ge(hidden, g - 1)
                if p < PAIRS:
                    pe.matmul(weight_ps[r], pick[:, p, :], weightT[:, q, :], start=True, stop=True)
                split3(pe, up_ps[r], hl(w3_hl, 1, p), right).then_inc(up_mm, 1)

            def down(t, g, p, q, r):
                if p == 0:
                    pe.wait_ge(y2_done, t + 1)
                    pe.matmul(acc_ps[:], bd_h[:], weightT[:, q, :], start=True, stop=False)
                    pe.matmul(acc_ps[:], bd_l[:], weightT[:, q, :], start=False, stop=False)
                pe.wait_ge(act_split, CREDIT + g + 1)
                mm = split3(pe, acc_ps[:], hl(w3_hl, 2, p), [act_hl[:, a, r, :] for a in (HI, LO)],
                            first=False, last=(p == PAIRS)).then_inc(down_mm, 1)
                return mm

            def turn_out(t):
                pe.wait_ge(y2_done, t + 2)
                for k in range(4):
                    mm = pe.transpose(misc_ps[:, P * k:P * (k + 1)], yT[:, 1, P * k:P * (k + 1)], eye[:])
                mm.then_inc(y2_turned, 1)

            def tile_body(b, u, more):
                t = b * TILES + u
                q, q1 = u % 2, (u + 1) % 2
                for p in range(LAG + 1, UNITS):
                    up_gate(t, t * UNITS + p, p, q, (u + p) % 2)
                    down(t, t * UNITS + p - LAG, p - LAG, q, (u + p) % 2)
                    if more:
                        if p == 6:
                            turn_x2(t + 1)
                        if p == 8:
                            logits(t + 1, q1)
                        if p == 12:
                            turn_weights(t + 1)
                for p in range(LAG):
                    if more:
                        up_gate(t + 1, (t + 1) * UNITS + p, p, q1, (q1 + p) % 2)
                    down(t, t * UNITS + UNITS - LAG + p, UNITS - LAG + p, q, (u + UNITS - LAG + p) % 2)
                if more:
                    up_gate(t + 1, (t + 1) * UNITS + LAG, LAG, q1, (q1 + LAG) % 2)
                turn_out(t)
                if more:
                    down(t + 1, (t + 1) * UNITS, 0, q1, q1)

            turn_x2(0)
            logits(0, 0)
            turn_weights(0)
            pe.wait_ge(pick_done, 2)
            pe.wait_ge(bd_split, 1)
            pe.wait_ge(w_split, 3)
            up_gate(0, 0, 0, 0, 0)
            pe.wait_ge(w_split, 6)
            up_gate(0, 1, 1, 0, 1)
            up_gate(0, 2, 2, 0, 0)
            down(0, 0, 0, 0, 0)
            pe.wait_ge(w_split, 3 * len(CHUNKS))
            with pe.Fori(0, BATCH - 1) as b:
                tile_body(b, 0, True)
                tile_body(b, 1, True)
            tile_body(BATCH - 1, 0, True)
            tile_body(BATCH - 1, 1, False)


_INS = ['L0_attn_x', 'L0_attn_Wq', 'L0_attn_bq', 'L0_attn_Wkv', 'L0_attn_bkv', 'L0_attn_Wo', 'L0_ffn_Wr',
        'L0_ffn_br', 'L0_ffn_Wg_s', 'L0_ffn_bg_s', 'L0_ffn_Wu_s', 'L0_ffn_bu_s', 'L0_ffn_Wd_s', 'L0_ffn_bd_s',
        'L0_ffn_Wg', 'L0_ffn_bg', 'L0_ffn_Wu', 'L0_ffn_bu', 'L0_ffn_Wd', 'L0_ffn_bd', 'L0_c', 'L0_wmod']
_OUTS = [((BATCH, TOKENS, P), 'float32')]


def constants():
    eye = np.eye(P, dtype=np.float32)
    pos = np.arange(TOKENS, dtype=np.float32)[:, None]
    inv_freq = np.exp(np.float32(-math.log(10000.0)) * np.arange(0, P, 2, dtype=np.float32) / np.float32(P))
    angle = (pos * inv_freq[None, :].astype(np.float32)).astype(np.float32)
    pe = np.zeros((TOKENS, P), np.float32)
    pe[:, 0::2] = np.sin(angle)
    pe[:, 1::2] = np.cos(angle)
    mask = np.where(np.tril(np.ones((P, P), bool)), 0.0, MASKED).astype(np.float32)
    pick = np.zeros((2 * EXPERTS, PAIRS, P), np.float32)
    for e in range(EXPERTS):
        for half in range(2):
            pick[half * EXPERTS + e, e // 2, (e % 2) * INNER:(e % 2 + 1) * INNER] = 1.0
    return {"eye": eye, "pe": np.ascontiguousarray(pe.T), "mask": mask, "pick": pick}


def laid_out(name, a):
    if name == "L0_c":
        return a.T
    if name in ("L0_attn_bq", "L0_attn_bkv"):
        return a.reshape(-1, P).T
    if name in ("L0_ffn_bg_s", "L0_ffn_bu_s", "L0_ffn_bd_s"):
        return a.reshape(-1, 1)
    if name in ("L0_ffn_bg", "L0_ffn_bu"):
        return a.reshape(PAIRS, P).T
    if name in ("L0_ffn_Wg", "L0_ffn_Wu"):
        return a.reshape(PAIRS, 2, P, INNER).transpose(2, 0, 1, 3).reshape(P, PAIRS, P)
    if name == "L0_ffn_Wd":
        return a.reshape(PAIRS, P, P).transpose(1, 0, 2)
    return a


def kernel(**inputs):
    import numpy as _np
    import concourse.bacc as _bacc
    from concourse import mybir as _mybir
    from concourse.bass_utils import run_bass_kernel_spmd as _run

    nc = _bacc.Bacc("TRN2", target_bir_lowering=False, num_devices=1)
    arrays, args = {}, []
    for name, a in [(name, laid_out(name, _np.asarray(inputs[name]))) for name in _INS] + list(constants().items()):
        a = _np.ascontiguousarray(a)
        arrays[f"in_{name}_dram"] = a
        args.append(nc.dram_tensor(f"in_{name}_dram", a.shape, _mybir.dt.from_np(a.dtype), kind="ExternalInput").ap())
    for i, (shape, dtype) in enumerate(_OUTS):
        dt = _mybir.dt.from_np(_np.dtype(dtype))
        args.append(nc.dram_tensor(f"out_{i}_dram", shape, dt, kind="ExternalOutput").ap())
    bass_adaln_attention_moe(nc, *args)
    r = _run(nc, [arrays], core_ids=[0])
    got = tuple(r.results[0][f"out_{i}_dram"] for i in range(len(_OUTS)))
    return got[0]
```

```python
import math
from contextlib import ExitStack

import numpy as np

import concourse.bass as bass
from concourse import mybir

F32 = mybir.dt.float32
F32R = mybir.dt.float32r
BF16 = mybir.dt.bfloat16
ALU = mybir.AluOpType
ACT = mybir.ActivationFunctionType
AX_X = mybir.AxisListType.X

P = 128
BATCH, TOKENS = 4, 1024
BLOCKS = TOKENS // P
HEADS = 8
HALF = 512
TILES = TOKENS // HALF
EXPERTS, INNER, TOP = 32, 64, 8
PAIRS = EXPERTS // 2
UNITS = PAIRS + 1
LN_EPS = 1e-5
MASKED = -1e30
SCALE = 1.0 / math.sqrt(P)
HI, LO = 0, 1

SHIFT_A, SCALE_A, GATE_A, SHIFT_F, SCALE_F, GATE_F = range(6)

PASSES = ((HI, HI), (LO, HI), (HI, LO))

ORDER = [3, 2, 1, 0, 7, 6, 5, 4]
PLACE = [ORDER.index(i) for i in range(BLOCKS)]
STEPS = [(0, j) for j in range(4)] + [(1, j) for j in range(8)]
NSTEP = len(STEPS)
PROB_AT = [P * i * (i + 1) // 2 for i in range(BLOCKS + 1)]

PE_A = [("project", 0), ("apply_prev", 10), ("apply_prev", 11), ("score", 7), ("turn", 0), ("score", 6), ("turn", 1),
        ("apply", 0), ("score", 5), ("turn", 2), ("apply", 1), ("score", 4), ("turn", 3), ("apply", 2)]
PE_B = [("score", 3), ("apply", 3), ("score", 2), ("turn", 4), ("turn", 5), ("project", 1), ("score", 1), ("turn", 6),
        ("apply", 4), ("score", 0), ("turn", 7), ("apply", 5), ("turn", 8), ("apply", 6), ("turn", 9),
        ("apply", 7), ("turn", 10), ("apply", 8), ("turn", 11), ("apply", 9)]
DVE_A = [("query", 0), ("out_prev", 1), ("max", 7), ("low", 0), ("max", 6), ("low", 1), ("inverse", 7), ("max", 5),
         ("inverse", 6), ("low", 2), ("max", 4), ("inverse", 5), ("low", 3), ("inverse", 4)]
DVE_B = [("max", 3), ("out", 0), ("max", 2), ("inverse", 3), ("low", 4), ("inverse", 2), ("max", 1),
         ("low", 5), ("query", 1), ("inverse", 1), ("max", 0), ("low", 6), ("inverse", 0)] + [
    ("low", s) for s in range(7, NSTEP)]
ACT_A = [("out_prev", 1), ("high", 0), ("exp", 7), ("high", 1), ("exp", 6), ("high", 2), ("exp", 5), ("high", 3),
         ("exp", 4)]
ACT_B = [("out", 0), ("exp", 3), ("high", 4), ("exp", 2), ("high", 5), ("exp", 1), ("high", 6), ("exp", 0)] + [
    ("high", s) for s in range(7, NSTEP)]
POOL_A = [("weights", 0), ("query", 0), ("norm", 7), ("norm", 6), ("norm", 5), ("norm", 4)]
POOL_B = [("norm", 3), ("norm", 2), ("query", 1), ("norm", 1), ("norm", 0)]
NEXT_HEAD = {("project", 0), ("project", 1), ("query", 0), ("query", 1), ("weights", 0)} | {
    (w, i) for w in ("score", "max", "exp", "inverse", "norm") for i in range(4)}
PE_TAIL = [("apply", 3), ("turn", 4), ("turn", 5), ("turn", 6), ("apply", 4), ("turn", 7), ("apply", 5),
           ("turn", 8), ("apply", 6), ("turn", 9), ("apply", 7), ("x", 0), ("turn", 10), ("apply", 8), ("x", 1),
           ("turn", 11), ("apply", 9), ("apply", 10), ("apply", 11), ("wo", 0), ("keys", 0), ("keys", 1),
           ("project", 0), ("values", 0), ("values", 1), ("project", 1), ("wo", 1), ("y", 0), ("score", 3),
           ("score", 2), ("wo", 2), ("score", 1), ("score", 0), ("y", 1)]
DVE_TAIL = [("stats", 0), ("out", 0), ("low", 4), ("low", 5), ("low", 6), ("x", 0), ("low", 7), ("low", 8), ("x", 1),
            ("low", 9), ("low", 10), ("low", 11), ("out", 1), ("k_sum", 0), ("k_sum", 1), ("query", 0),
            ("k_low", 0), ("k_low", 1), ("query", 1), ("v_low", 0), ("v_low", 1), ("y", 0), ("max", 3), ("max", 2),
            ("inverse", 3), ("inverse", 2), ("max", 1), ("max", 0), ("inverse", 1), ("inverse", 0), ("y", 1)]
ACT_TAIL = [("out", 0), ("high", 4), ("high", 5), ("high", 6), ("high", 7), ("high", 8), ("x", 0), ("high", 9),
            ("x", 1), ("high", 10), ("high", 11), ("out", 1), ("y", 0), ("k_high", 0), ("k_high", 1),
            ("v_high", 0), ("v_high", 1), ("exp", 3), ("exp", 2), ("y", 1), ("exp", 1), ("exp", 0)]
POOL_TAIL = [("rstd", 0), ("weights", 0), ("x", 0), ("x", 1), ("query", 0), ("query", 1), ("norm", 3), ("norm", 2),
             ("norm", 1), ("norm", 0)]
OLD_ROW = {"turn", "apply", "wo", "low", "high", "out"}
RING = 3

CHUNKS = [(0, 1), (1, 3), (3, 9), (9, UNITS)]
LAG = 2


def bass_adaln_attention_moe(nc, x_in, Wq, bq, Wkv, bkv, Wo, Wr, br, Wg_s, bg_s, Wu_s, bu_s, Wd_s, bd_s,
                             Wg, bg, Wu, bu, Wd, bd, c_in, wmod_in, eye_in, pe_in, mask_in, pick_in, out):
    with ExitStack() as ctx:
        def sb(name, shape, dt=F32):
            return ctx.enter_context(nc.sbuf_tensor(name, shape, dt))

        def psum(name, shape):
            return ctx.enter_context(nc.psum_tensor(name, shape, F32))

        def sem(name):
            return ctx.enter_context(nc.semaphore(name))

        x = sb("x", [P, BATCH * BLOCKS, P])
        eye = sb("eye", [P, P])
        eye_b = sb("eye_b", [P, P], BF16)
        mask = sb("mask", [P, P])
        mask_b = sb("mask_b", [P, P], BF16)
        mod = sb("mod", [P, BATCH, 6])
        cur = sb("cur", [P, 6])
        wq = sb("wq", [P, HEADS, P])
        wq_hl = sb("wq_hl", [P, 2, P], F32R)
        wkv = sb("wkv", [P, 2 * P])
        wkv_hl = sb("wkv_hl", [P, 2, 2 * P], F32R)
        wo_hl = sb("wo_hl", [P, 2, HEADS, P], F32R)
        bqT = sb("bqT", [P, HEADS])
        bkvT = sb("bkvT", [P, 2])
        peT = sb("peT", [P, TOKENS])
        stats = sb("stats", [P, BLOCKS, 6])
        mv = sb("mv", [P, BLOCKS, 2])
        var_eps = sb("var_eps", [P, BLOCKS])
        rstd = sb("rstd", [P, BLOCKS])
        minus_half = sb("minus_half", [P, BLOCKS])
        hT = sb("hT", [P, TOKENS])
        hT_hl = sb("hT_hl", [P, 2, TOKENS], F32R)
        kT_hl = sb("kT_hl", [P, 2, TOKENS], F32R)
        v_hl = sb("v_hl", [P, 2, TOKENS], F32R)
        qT = sb("qT", [P, TOKENS])
        qT_hl = sb("qT_hl", [P, 2, TOKENS], F32R)
        nmax = sb("nmax", [P, BLOCKS])
        total = sb("total", [P, BLOCKS])
        rtotal = sb("rtotal", [P, BLOCKS])
        probs = sb("probs", [P, PROB_AT[BLOCKS]])
        pT_hl = sb("pT_hl", [P, 2, RING, HALF], F32R)
        yT = sb("yT", [P, 2, HALF])
        arena = sb("arena", [P, 2 * HEADS * TOKENS], F32R)
        w3 = sb("w3", [P, 3, UNITS, P])
        b2 = sb("b2", [P, 2, UNITS])
        wr = sb("wr", [P, EXPERTS])
        br_rows = sb("br_rows", [P, EXPERTS])
        bd2 = sb("bd2", [2 * EXPERTS, P])
        bd_h = sb("bd_h", [2 * EXPERTS, P], F32R)
        bd_l = sb("bd_l", [2 * EXPERTS, P], F32R)
        bds = sb("bds", [P, 1])
        gate_bds = sb("gate_bds", [P, 1])
        cT = sb("cT", [P, 4, BATCH])
        c_inv = sb("c_inv", [P, BATCH])
        sign = sb("sign", [P, 2, BATCH])
        floor = sb("floor", [P, 2, BATCH])
        lg = sb("lg", [P, 4, EXPERTS])
        aff = sb("aff", [P, 4, EXPERTS])
        top = sb("top", [P, 4, TOP])
        rest = sb("rest", [P, 4, EXPERTS])
        chosen = sb("chosen", [P, 4, EXPERTS])
        top_sum = sb("top_sum", [P, 4])
        top_eps = sb("top_eps", [P, 4])
        top_inv = sb("top_inv", [P, 4])
        weight2 = sb("weight2", [P, 4, 2 * EXPERTS])
        ln_mod = sb("ln_mod", [P, 2])
        oT_hl = arena[:, :].rearrange("p (a h t) -> p a h t", a=2, h=HEADS)
        w3_hl = arena[:, 0:6 * UNITS * P].rearrange("p (a m u n) -> p a m u n", a=2, m=3, u=UNITS)
        xn = yT[:, :, :].rearrange("p u (k e) -> p (u k) e", e=P)
        wo = qT[:, :].rearrange("p (h e) -> p h e", h=HEADS)
        kT = hT
        wmod = probs[:, 0:6 * P]
        gs = probs[:, 0:2 * HALF].rearrange("p (r t) -> p r t", r=2)
        prod = probs[:, 2 * HALF:4 * HALF].rearrange("p (r t) -> p r t", r=2)
        hf = probs[:, 4 * HALF:6 * HALF].rearrange("p (r t) -> p r t", r=2)
        act_hl = kT_hl[:, :, :].rearrange("p a (r t) -> p a r t", r=2)
        x2T = hT[:, :].rearrange("p (r t) -> p r t", r=2)
        x2T_hl = hT_hl[:, :, :].rearrange("p a (r t) -> p a r t", r=2)
        weightT = v_hl[0:2 * EXPERTS, 0, :].rearrange("p (r t) -> p r t", r=2)
        pick_raw = [wq[0:2 * EXPERTS, :, :], wo[0:2 * EXPERTS, :, :]]
        pick = qT_hl[0:2 * EXPERTS, :, :].rearrange("p a (u n) -> p (a u) n", n=P)

        turned = [psum("turned0", [P, HALF]), psum("turned1", [P, HALF])]
        mixed = psum("mixed", [P, HALF])
        project = psum("project", [P, HALF])
        scores = [psum("scores0", [P, 2 * HALF]), psum("scores1", [P, 2 * HALF])]
        y_ps = [mixed[:], scores[0][:, HALF:]]
        gate_ps = turned
        acc_ps = mixed
        misc_ps = project
        up_ps = [scores[0][:, 0:HALF], scores[0][:, HALF:]]
        weight_ps = [scores[1][:, 0:HALF], scores[1][:, HALF:]]

        mod_in = sem("mod_in")
        attn_in = sem("attn_in")
        x_first = sem("x_first")
        x_rest = sem("x_rest")
        ffn_in = sem("ffn_in")
        pick_loaded = sem("pick_loaded")
        stored = sem("stored")
        padded = sem("padded")
        c_exp = sem("c_exp")
        dve_setup = sem("dve_setup")
        mod_mm = sem("mod_mm")
        pool_setup = sem("pool_setup")
        ln_step = sem("ln_step")
        rstd_done = sem("rstd_done")
        xn_done = sem("xn_done")
        x_turned = sem("x_turned")
        hT_done = sem("hT_done")
        hT_high = sem("hT_high")
        hT_split = sem("hT_split")
        k_mm = sem("k_mm")
        k_sum = sem("k_sum")
        k_high = sem("k_high")
        k_split = sem("k_split")
        v_mm = sem("v_mm")
        v_high = sem("v_high")
        v_split = sem("v_split")
        wq_high = sem("wq_high")
        wq_split = sem("wq_split")
        q_mm = sem("q_mm")
        q_sum = sem("q_sum")
        q_high = sem("q_high")
        q_split = sem("q_split")
        score_mm = sem("score_mm")
        max_done = sem("max_done")
        exp_done = sem("exp_done")
        inverted = sem("inverted")
        normed = sem("normed")
        p_turned = sem("p_turned")
        p_high = sem("p_high")
        p_split = sem("p_split")
        applied = sem("applied")
        o_high = sem("o_high")
        o_split = sem("o_split")
        y_mm = sem("y_mm")
        y_done = sem("y_done")
        y_turned = sem("y_turned")
        x1_done = sem("x1_done")
        w_high = sem("w_high")
        w_split = sem("w_split")
        bd_high = sem("bd_high")
        bd_split = sem("bd_split")
        pick_done = sem("pick_done")
        ln2_step = sem("ln2_step")
        rstd2_done = sem("rstd2_done")
        xn2_done = sem("xn2_done")
        x2_turned = sem("x2_turned")
        x2_done = sem("x2_done")
        x2_high = sem("x2_high")
        x2_split = sem("x2_split")
        logit_mm = sem("logit_mm")
        logit_done = sem("logit_done")
        aff_done = sem("aff_done")
        route_step = sem("route_step")
        weight_done = sem("weight_done")
        weight_turned = sem("weight_turned")
        weight_high = sem("weight_high")
        weight_split = sem("weight_split")
        gate_mm = sem("gate_mm")
        up_mm = sem("up_mm")
        silu_done = sem("silu_done")
        prod_done = sem("prod_done")
        hidden = sem("hidden")
        act_high = sem("act_high")
        act_split = sem("act_split")
        down_mm = sem("down_mm")
        gate_cur = sem("gate_cur")
        y2_done = sem("y2_done")
        y2_turned = sem("y2_turned")
        out_done = sem("out_done")

        CREDIT = 2


        def f32(ap):
            return ap.bitcast(F32)

        def row(b):
            return bass.ds(b, 1)

        def wait_apart(engine, loaded, count, *waits):
            known = [(signal, value if isinstance(value, int) else engine.to_reg(value)) for signal, value in waits]
            engine.wait_ge(loaded, count)
            for signal, value in known:
                engine.wait_ge(signal, value)

        def split3(pe, to, left, right, first=True, last=True):
            for n, (a, c) in enumerate(PASSES):
                mm = pe.matmul(to, left[a], right[c], start=first and n == 0, stop=last and n == 2)
            return mm

        def hl(ap, *at):
            return [ap[(slice(None), part) + at] for part in (HI, LO)]

        def is_first(t):
            return isinstance(t, int) and t == 0

        block = ctx.enter_context(nc.Block())

        @block.sync
        def _(sp):
            sp.dma_start(cT[:, 0, :], c_in).then_inc(mod_in, 16)
            sp.dma_start(wmod, wmod_in).then_inc(mod_in, 16)
            xd = x_in.rearrange("b (n p) e -> b p n e", p=P)
            sp.dma_start(x[:, 0:BLOCKS, :], xd[0]).then_inc(x_first, 16)
            sp.dma_start(eye[:], eye_in).then_inc(attn_in, 16)
            sp.dma_start(wkv[:], Wkv).then_inc(attn_in, 16)
            sp.dma_start(wq[:], Wq.rearrange("e (h d) -> e h d", h=HEADS)).then_inc(attn_in, 16)
            sp.dma_start(peT[:], pe_in).then_inc(attn_in, 16)
            sp.dma_start(mask[:], mask_in).then_inc(attn_in, 16)
            sp.dma_start(bqT[:], bq).then_inc(attn_in, 16)
            sp.dma_start(bkvT[:], bkv).then_inc(attn_in, 16)
            sp.dma_start(wo[:], Wo.rearrange("(h d) e -> d h e", h=HEADS)).then_inc(attn_in, 16)
            for b in range(1, BATCH):
                sp.dma_start(x[:, b * BLOCKS:(b + 1) * BLOCKS, :], xd[b]).then_inc(x_rest, 16)
            sp.wait_ge(padded, 1)
            for m, (many, one) in enumerate(((Wg, Wg_s), (Wu, Wu_s))):
                sp.dma_start(w3[:, m, 0:PAIRS, :], many).then_inc(ffn_in, 16)
                sp.dma_start(w3[:, m, PAIRS, 0:INNER], one).then_inc(ffn_in, 16)
            sp.dma_start(w3[:, 2, 0:PAIRS, :], Wd).then_inc(ffn_in, 16)
            sp.dma_start(w3[0:INNER, 2, PAIRS, :], Wd_s).then_inc(ffn_in, 16)
            for m, (many, one) in enumerate(((bg, bg_s), (bu, bu_s))):
                sp.dma_start(b2[:, m, 0:PAIRS], many).then_inc(ffn_in, 16)
                sp.dma_start(b2[0:INNER, m, PAIRS:UNITS], one).then_inc(ffn_in, 16)
            sp.dma_start(bds[:], bd_s).then_inc(ffn_in, 16)
            sp.dma_start(wr[:], Wr).then_inc(ffn_in, 16)
            sp.dma_start(br_rows[:], br.rearrange("(a e) -> a e", a=1).broadcast_to([P, EXPERTS])).then_inc(ffn_in, 16)
            sp.dma_start(bd2[0:EXPERTS, :], bd).then_inc(ffn_in, 16)
            sp.dma_start(bd2[EXPERTS:, :], bd).then_inc(ffn_in, 16)
            sp.wait_ge(y_mm, 2 * BATCH)
            sp.wait_ge(wq_split, BATCH * HEADS)
            for k in range(2):
                sp.dma_start(pick_raw[k], pick_in[:, k * HEADS:(k + 1) * HEADS, :]).then_inc(pick_loaded, 16)
            od = out.rearrange("b (n p) e -> p (b n) e", p=P)
            with sp.Fori(0, BATCH * TILES) as t:
                sp.wait_ge(out_done, t + 1)
                sp.dma_start(od[:, bass.ds(t * 4, 4), :], x[:, bass.ds(t * 4, 4), :]).then_inc(stored, 16)
            sp.wait_ge(stored, 16 * BATCH * TILES)

        ATTN_IN = 16 * 8
        FFN_IN = 16 * 15

        @block.gpsimd
        def _(pool):
            pool.memset(minus_half[:], -0.5).then_inc(pool_setup, 1)
            pool.sem_inc(q_split, CREDIT)
            pool.sem_inc(act_split, CREDIT)
            pool.wait_ge(attn_in, ATTN_IN)
            pool.tensor_scalar(wkv_hl[:, HI, :], wkv[:], 1.0, 1.0, ALU.mult, ALU.mult).then_inc(pool_setup, 1)
            pool.wait_ge(pool_setup, 2)
            pool.tensor_tensor(wkv_hl[:, LO, :], wkv[:], f32(wkv_hl[:, HI, :]), ALU.subtract).then_inc(pool_setup, 1)
            pool.tensor_scalar(eye_b[:], eye[:], 1.0, 1.0, ALU.mult, ALU.mult)
            pool.tensor_scalar(mask_b[:], mask[:], 1.0, 1.0, ALU.mult, ALU.mult)
            pool.tensor_scalar(wo_hl[:, HI, :, :], wo[:], 1.0, 1.0, ALU.mult, ALU.mult).then_inc(pool_setup, 1)
            pool.wait_ge(pool_setup, 4)
            pool.tensor_tensor(wo_hl[:, LO, :, :], wo[:], f32(wo_hl[:, HI, :, :]), ALU.subtract).then_inc(pool_setup, 1)

            def weights(n, h):
                pool.tensor_copy(wq_hl[:, HI, :], wq[:, row(h), :].rearrange("p a d -> p (a d)")).then_inc(wq_high, 1)
                wait_apart(pool, attn_in, ATTN_IN, (wq_high, n + 1))
                pool.tensor_tensor(wq_hl[:, LO, :], wq[:, row(h), :].rearrange("p a d -> p (a d)"),
                                   f32(wq_hl[:, HI, :]), ALU.subtract).then_inc(wq_split, 1)

            def query(n, u):
                at = slice(u * HALF, (u + 1) * HALF)
                wait_apart(pool, attn_in, ATTN_IN, (q_sum, CREDIT + 2 * n + u + 1))
                pool.tensor_scalar(qT_hl[:, HI, at], qT[:, at], 1.0, 1.0, ALU.mult, ALU.mult).then_inc(q_high, 1)
                pool.wait_ge(q_high, 2 * n + u + 1)
                pool.tensor_tensor(qT_hl[:, LO, at], qT[:, at], f32(qT_hl[:, HI, at]), ALU.subtract).then_inc(q_split, 1)

            def norm(n, i):
                wait_apart(pool, attn_in, ATTN_IN, (inverted, BLOCKS * n + PLACE[i] + 1))
                at = slice(PROB_AT[i], PROB_AT[i + 1])
                pool.tensor_scalar(probs[:, at], probs[:, at], rtotal[:, i:i + 1], 1.0, ALU.mult, ALU.mult)\
                    .then_inc(normed, 1)

            def segment(todo, n, h, more):
                for what, i in todo:
                    if (what, i) in NEXT_HEAD:
                        if more:
                            {"weights": lambda n, i: weights(n, h + 1), "norm": norm, "query": query}[what](n + 1, i)
                    else:
                        norm(n, i)

            def rstd_of(b):
                wait_apart(pool, attn_in, ATTN_IN, (ln_step, b * 3 + 3))
                pool.tensor_tensor(rstd[:], var_eps[:], minus_half[:], ALU.pow).then_inc(rstd_done, 1)

            def split_x(b, u):
                at = slice(u * HALF, (u + 1) * HALF)
                wait_apart(pool, attn_in, ATTN_IN, (hT_done, b * 2 + u + 1))
                pool.tensor_scalar(hT_hl[:, HI, at], hT[:, at], 1.0, 1.0, ALU.mult, ALU.mult).then_inc(hT_high, 1)
                pool.wait_ge(hT_high, b * 2 + u + 1)
                pool.tensor_tensor(hT_hl[:, LO, at], hT[:, at], f32(hT_hl[:, HI, at]), ALU.subtract)\
                    .then_inc(hT_split, 1)

            def prepare(b):
                for what, i in POOL_TAIL:
                    if what == "rstd":
                        rstd_of(b)
                    elif what == "x":
                        split_x(b, i)
                    elif what == "weights":
                        weights(b * HEADS, 0)
                    else:
                        {"norm": norm, "query": query}[what](b * HEADS, i)

            def heads(b):
                first = b * HEADS
                segment(POOL_A, first, 0, True)
                with pool.Fori(0, HEADS - 2) as h:
                    segment(POOL_B, first + h, h, True)
                    segment(POOL_A, first + (h + 1), h + 1, True)
                segment(POOL_B, first + (HEADS - 2), HEADS - 2, True)
                segment(POOL_A, first + (HEADS - 1), HEADS - 1, False)

            prepare(0)
            with pool.Fori(0, BATCH - 1) as b:
                heads(b)
                prepare(b + 1)
            heads(BATCH - 1)

            pool.wait_ge(ffn_in, FFN_IN)
            pool.wait_ge(pick_loaded, 32)
            for k in range(2):
                pool.tensor_scalar(pick[:, k * HEADS:(k + 1) * HEADS, :], pick_raw[k], 1.0, 1.0, ALU.mult, ALU.mult).then_inc(pick_done, 1)

            def rstd2(t):
                wait_apart(pool, ffn_in, FFN_IN, (ln2_step, t * 3 + 3))
                pool.tensor_tensor(rstd[:, 0:4], var_eps[:, 0:4], minus_half[:, 0:4], ALU.pow).then_inc(rstd2_done, 1)

            def split_x2(t, r):
                wait_apart(pool, ffn_in, FFN_IN, (x2_done, t + 1))
                pool.tensor_scalar(x2T_hl[:, HI, r, :], x2T[:, r, :], 1.0, 1.0, ALU.mult, ALU.mult).then_inc(x2_high, 1)
                pool.wait_ge(x2_high, t + 1)
                pool.tensor_tensor(x2T_hl[:, LO, r, :], x2T[:, r, :], f32(x2T_hl[:, HI, r, :]), ALU.subtract)\
                    .then_inc(x2_split, 1)

            def split_hidden(g, r):
                wait_apart(pool, ffn_in, FFN_IN, (down_mm, CREDIT + g - 1), (hidden, g + 1))
                pool.tensor_scalar(act_hl[:, HI, r, :], hf[:, r, :], 1.0, 1.0, ALU.mult, ALU.mult).then_inc(act_high, 1)
                pool.wait_ge(act_high, g + 1)
                pool.tensor_tensor(act_hl[:, LO, r, :], hf[:, r, :], f32(act_hl[:, HI, r, :]), ALU.subtract)\
                    .then_inc(act_split, 1)

            def tile_body(b, u, more):
                t = b * TILES + u
                for p in range(UNITS):
                    split_hidden(t * UNITS + p, (u + p) % 2)
                    if more and p == 4:
                        rstd2(t + 1)
                    if more and p == 7:
                        split_x2(t + 1, (u + 1) % 2)

            rstd2(0)
            split_x2(0, 0)
            with pool.Fori(0, BATCH - 1) as b:
                tile_body(b, 0, True)
                tile_body(b, 1, True)
            tile_body(BATCH - 1, 0, True)
            tile_body(BATCH - 1, 1, False)

        @block.vector
        def _(dve):
            dve.sem_inc(q_sum, CREDIT)
            dve.sem_inc(p_split, CREDIT)
            dve.sem_inc(o_split, CREDIT)
            dve.sem_inc(x1_done, CREDIT)
            dve.memset(w3[:, 0:2, PAIRS, INNER:], 0.0)
            dve.memset(w3[INNER:, 2, PAIRS, :], 0.0)
            dve.memset(b2[INNER:, :, PAIRS:UNITS], 0.0).then_inc(padded, 1)
            dve.wait_ge(c_exp, 1)
            dve.tensor_scalar(cT[:, 2, :], cT[:, 1, :], 1.0, None, ALU.add).then_inc(dve_setup, 1)
            dve.wait_ge(dve_setup, 1)
            dve.reciprocal(c_inv[:], cT[:, 2, :]).then_inc(dve_setup, 1)
            dve.wait_ge(dve_setup, 2)
            dve.tensor_tensor(cT[:, 3, :], cT[:, 0, :], c_inv[:], ALU.mult).then_inc(dve_setup, 1)
            dve.wait_ge(mod_mm, 1)
            dve.tensor_copy(mod[:].rearrange("p b j -> p j b"),
                            project[:, 0:6 * BATCH].rearrange("p (j b) -> p j b", j=6)).then_inc(dve_setup, 1)
            dve.wait_ge(dve_setup, 4)
            gates = list(enumerate((GATE_A, GATE_F)))
            for k, j in gates:
                last = dve.tensor_scalar(sign[:, k, :], mod[:, :, j], 0.0, 2.0, ALU.is_ge, ALU.mult)
            last.then_inc(dve_setup, 1)
            dve.wait_ge(dve_setup, 5)
            for k, j in gates:
                last = dve.scalar_tensor_tensor(floor[:, k, :], sign[:, k, :], -1.0, mod[:, :, j], ALU.add, ALU.mult)
            last.then_inc(dve_setup, 1)
            dve.wait_ge(dve_setup, 6)
            dve.tensor_scalar(floor[:], floor[:], 0.25, None, ALU.max).then_inc(dve_setup, 1)
            dve.wait_ge(dve_setup, 7)
            for k, j in gates:
                dve.scalar_tensor_tensor(mod[:, :, j], sign[:, k, :], -1.0, floor[:, k, :], ALU.add, ALU.mult)
            for j in (SCALE_A, SCALE_F):
                last = dve.tensor_scalar(mod[:, :, j], mod[:, :, j], 1.0, None, ALU.add)
            last.then_inc(dve_setup, 1)
            dve.wait_ge(dve_setup, 8)

            def query(n, u):
                at = slice(u * HALF, (u + 1) * HALF)
                dve.wait_ge(q_split, CREDIT + 2 * n + u - 1)
                dve.wait_ge(q_mm, 2 * n + u + 1)
                return at

            def query_of(n, h, u):
                at = query(n, u)
                dve.scalar_tensor_tensor(qT[:, at], project[:], bqT[:, row(h)], peT[:, at], ALU.add, ALU.add)\
                    .then_inc(q_sum, 1)

            def maximum(n, i):
                k = PLACE[i]
                dve.wait_ge(score_mm, BLOCKS * n + k + 1)
                dve.tensor_reduce(nmax[:, i:i + 1], scores[k % 2][:, 0:P * (i + 1)], AX_X, ALU.max, negate=True)\
                    .then_inc(max_done, 1)

            def inverse(n, i):
                dve.wait_ge(exp_done, BLOCKS * n + PLACE[i] + 1)
                dve.reciprocal(rtotal[:, i:i + 1], total[:, i:i + 1]).then_inc(inverted, 1)

            def low(n, s):
                u, j = STEPS[s]
                at = slice(P * max(j - 4 * u, 0), HALF)
                dve.wait_ge(p_high, NSTEP * n + s + 1)
                dve.tensor_tensor(pT_hl[:, LO, s % RING, at], turned[s % 2][:, at], f32(pT_hl[:, HI, s % RING, at]),
                                  ALU.subtract).then_inc(p_split, 1)

            def out_low(n, h, u):
                at = slice(u * HALF, (u + 1) * HALF)
                dve.wait_ge(o_high, 2 * n + u + 1)
                dve.scalar_tensor_tensor(oT_hl[:, LO, row(h), at].rearrange("p a t -> p (a t)"), mixed[:], bkvT[:, 1:2],
                                         f32(oT_hl[:, HI, row(h), at].rearrange("p a t -> p (a t)")),
                                         ALU.add, ALU.subtract).then_inc(o_split, 1)

            def segment(todo, n, h, more, prev):
                for what, i in todo:
                    m, k = (n + 1, h + 1) if (what, i) in NEXT_HEAD else (n, h)
                    if (what, i) in NEXT_HEAD and not more:
                        continue
                    if what == "max":
                        maximum(m, i)
                    elif what == "inverse":
                        inverse(m, i)
                    elif what == "query":
                        query_of(m, k, i)
                    elif what == "low":
                        low(m, i)
                    elif what == "out":
                        out_low(n, h, i)
                    elif prev:
                        out_low(n - 1, h - 1, i)

            def statistics(b):
                dve.tensor_copy(ln_mod[:], mod[:, row(b), SHIFT_A:SCALE_A + 1].rearrange("p a j -> p (a j)"))
                for k in range(BLOCKS):
                    last = dve.bn_stats(stats[:, k, :], x[:, row(b * BLOCKS + k), :].rearrange("p a e -> p (a e)"))
                last.then_inc(ln_step, 1)
                wait_apart(dve, x_first, 16, (ln_step, b * 3 + 1))
                for k in range(BLOCKS):
                    last = dve.bn_aggr(mv[:, k, :], stats[:, k, :])
                last.then_inc(ln_step, 1)
                dve.wait_ge(ln_step, b * 3 + 2)
                dve.tensor_scalar(var_eps[:], mv[:, :, 1], LN_EPS, None, ALU.add).then_inc(ln_step, 1)

            def normalise(b, u):
                if u == 0:
                    dve.wait_ge(rstd_done, b + 1)
                for k in range(4 * u, 4 * u + 4):
                    last = dve.tensor_scalar(xn[:, k, :], x[:, row(b * BLOCKS + k), :].rearrange("p a e -> p (a e)"),
                                             mv[:, k, 0:1], rstd[:, k:k + 1], ALU.subtract, ALU.mult)
                last.then_inc(xn_done, 1)

            def key_sum(b, u):
                at = slice(u * HALF, (u + 1) * HALF)
                dve.wait_ge(k_mm, b * 2 + u + 1)
                dve.scalar_tensor_tensor(kT[:, at], scores[0][:, at], bkvT[:, 0:1], peT[:, at], ALU.add, ALU.add)\
                    .then_inc(k_sum, 1)

            def key_low(b, u):
                at = slice(u * HALF, (u + 1) * HALF)
                dve.wait_ge(k_high, b * 2 + u + 1)
                dve.scalar_tensor_tensor(kT_hl[:, LO, at], kT[:, at], SCALE, f32(kT_hl[:, HI, at]),
                                         ALU.mult, ALU.subtract).then_inc(k_split, 1)

            def value_low(b, u):
                at = slice(u * HALF, (u + 1) * HALF)
                dve.wait_ge(v_high, b * 2 + u + 1)
                dve.tensor_tensor(v_hl[:, LO, at], turned[u][:], f32(v_hl[:, HI, at]), ALU.subtract)\
                    .then_inc(v_split, 1)

            def add_attention(b, u):
                dve.wait_ge(y_turned, b * 2 + u + 1)
                rows = x[:, bass.ds(b * BLOCKS + 4 * u, 4), :]
                dve.tensor_tensor(rows, y_ps[u].rearrange("p (k e) -> p k e", k=4), rows, ALU.add)\
                    .then_inc(x1_done, 1)

            def turn_row(b, old, new):
                n = (b + 1) * HEADS - 1
                if old:
                    dve.tensor_copy(cur[:, GATE_A:GATE_A + 1], mod[:, row(b), GATE_A:GATE_A + 1].rearrange("p a j -> p (a j)"))
                for what, i in DVE_TAIL:
                    if not (old if what in OLD_ROW or what == "y" else new):
                        continue
                    if what == "stats":
                        statistics(b + 1)
                    elif what == "query":
                        query_of(n + 1, 0, i)
                    elif what == "out":
                        out_low(n, HEADS - 1, i)
                    elif what in ("max", "inverse"):
                        {"max": maximum, "inverse": inverse}[what](n + 1, i)
                    elif what == "low":
                        low(n, i)
                    elif what == "y":
                        add_attention(b, i)
                    else:
                        {"x": normalise, "k_sum": key_sum, "k_low": key_low, "v_low": value_low}[what](b + 1, i)

            def heads(b):
                first = b * HEADS
                segment(DVE_A, first, 0, True, False)
                with dve.Fori(0, HEADS - 2) as h:
                    segment(DVE_B, first + h, h, True, True)
                    segment(DVE_A, first + (h + 1), h + 1, True, True)
                segment(DVE_B, first + (HEADS - 2), HEADS - 2, True, True)
                segment(DVE_A, first + (HEADS - 1), HEADS - 1, False, True)

            dve.wait_ge(x_first, 16)
            turn_row(-1, False, True)
            dve.wait_ge(x_rest, 16 * (BATCH - 1))
            with dve.Fori(0, BATCH - 1) as b:
                heads(b)
                turn_row(b, True, True)
            heads(BATCH - 1)
            turn_row(BATCH - 1, True, False)

            def stats2(t, b):
                dve.wait_ge(x1_done, CREDIT + 2 * BATCH)
                dve.tensor_copy(ln_mod[:], mod[:, row(b), SHIFT_F:SCALE_F + 1].rearrange("p a j -> p (a j)"))
                for k in range(4):
                    last = dve.bn_stats(stats[:, k, :], x[:, row(t * 4 + k), :].rearrange("p a e -> p (a e)"))
                last.then_inc(ln2_step, 1)
                wait_apart(dve, ffn_in, FFN_IN, (ln2_step, t * 3 + 1))
                for k in range(4):
                    last = dve.bn_aggr(mv[:, k, :], stats[:, k, :])
                last.then_inc(ln2_step, 1)
                dve.wait_ge(ln2_step, t * 3 + 2)
                dve.tensor_scalar(var_eps[:, 0:4], mv[:, 0:4, 1], LN_EPS, None, ALU.add).then_inc(ln2_step, 1)

            def normalise2(t):
                dve.wait_ge(rstd2_done, t + 1)
                for k in range(4):
                    last = dve.tensor_scalar(xn[:, k, :], x[:, row(t * 4 + k), :].rearrange("p a e -> p (a e)"),
                                             mv[:, k, 0:1], rstd[:, k:k + 1], ALU.subtract, ALU.mult)
                last.then_inc(xn2_done, 1)

            def add_br(t):
                dve.wait_ge(logit_mm, t + 1)
                for k in range(4):
                    last = dve.tensor_tensor(lg[:, k, :], misc_ps[:, k * EXPERTS:(k + 1) * EXPERTS], br_rows[:], ALU.add)
                last.then_inc(logit_done, 1)

            def route(t):
                wait_apart(dve, ffn_in, FFN_IN, (aff_done, t + 1))
                for k in range(4):
                    last = dve.max(top[:, k, :], aff[:, k, :])
                last.then_inc(route_step, 1)
                wait_apart(dve, ffn_in, FFN_IN, (route_step, t * 4 + 1))
                for k in range(4):
                    dve.match_replace(rest[:, k, :], top[:, k, :], aff[:, k, :], 0.0)
                dve.tensor_reduce(top_sum[:], top[:], AX_X, ALU.add).then_inc(route_step, 1)
                dve.wait_ge(route_step, t * 4 + 2)
                dve.tensor_tensor(chosen[:], aff[:], rest[:], ALU.subtract)
                dve.tensor_scalar(top_eps[:], top_sum[:], 1e-9, None, ALU.add).then_inc(route_step, 1)
                dve.wait_ge(route_step, t * 4 + 3)
                dve.reciprocal(top_inv[:], top_eps[:]).then_inc(route_step, 1)
                dve.wait_ge(route_step, t * 4 + 4)
                for k in range(4):
                    for c in range(2):
                        last = dve.tensor_scalar(weight2[:, k, c * EXPERTS:(c + 1) * EXPERTS], chosen[:, k, :],
                                                 top_inv[:, k:k + 1], None, ALU.mult)
                last.then_inc(weight_done, 1)

            def split_weight(t, r):
                dve.wait_ge(weight_turned, t + 1)
                dve.tensor_copy(weightT[:, r, :], misc_ps[0:2 * EXPERTS, :]).then_inc(weight_high, 1)
                dve.wait_ge(weight_high, t + 1)
                dve.tensor_tensor(weightT[EXPERTS:, r, :], misc_ps[EXPERTS:2 * EXPERTS, :],
                                  f32(weightT[EXPERTS:, r, :]), ALU.subtract).then_inc(weight_split, 1)

            def hidden_of(t, p, r):
                g = t * UNITS + p
                dve.wait_ge(silu_done, g + 1)
                dve.wait_ge(up_mm, g + 1)
                if p == PAIRS:
                    dve.wait_ge(act_split, CREDIT + g - 1)
                    dve.scalar_tensor_tensor(hf[:, r, :], up_ps[r], b2[:, 1, p:p + 1], gs[:, r, :], ALU.add, ALU.mult)\
                        .then_inc(hidden, 1)
                    return
                dve.scalar_tensor_tensor(prod[:, r, :], up_ps[r], b2[:, 1, p:p + 1], gs[:, r, :], ALU.add, ALU.mult)\
                    .then_inc(prod_done, 1)
                dve.wait_ge(act_split, CREDIT + g - 1)
                dve.wait_ge(prod_done, t * PAIRS + p + 1)
                dve.tensor_tensor(hf[:, r, :], prod[:, r, :], weight_ps[r], ALU.mult).then_inc(hidden, 1)

            def gate_of(b):
                dve.wait_ge(y2_done, b * TILES + 1)
                dve.tensor_copy(cur[:, GATE_F:], mod[:, row(b), GATE_F:].rearrange("p a j -> p (a j)"))
                dve.tensor_tensor(gate_bds[:], mod[:, row(b), GATE_F:].rearrange("p a j -> p (a j)"), bds[:], ALU.mult)\
                    .then_inc(gate_cur, 1)

            def add_out(t):
                dve.wait_ge(y2_turned, t + 1)
                rows = x[:, bass.ds(t * 4, 4), :]
                dve.tensor_tensor(rows, misc_ps[:].rearrange("p (k e) -> p k e", k=4), rows, ALU.add)\
                    .then_inc(out_done, 1)

            def tile_body(b, u, more):
                t = b * TILES + u
                r1 = (u + 1) % 2
                for p in range(LAG + 1, UNITS):
                    hidden_of(t, p, (u + p) % 2)
                    if p == 3 and u == 0:
                        gate_of(b)
                    if more:
                        if p == 3:
                            stats2(t + 1, b + u)
                        if p == 5:
                            normalise2(t + 1)
                        if p == 9:
                            add_br(t + 1)
                        if p == 11:
                            route(t + 1)
                        if p == 13:
                            split_weight(t + 1, r1)
                if more:
                    for p in range(LAG + 1):
                        hidden_of(t + 1, p, (r1 + p) % 2)
                add_out(t)

            dve.wait_ge(ffn_in, FFN_IN)
            dve.memset(f32(bd_l[:]), 0.0)
            dve.tensor_copy(bd_h[:], bd2[:]).then_inc(bd_high, 1)
            dve.wait_ge(bd_high, 1)
            dve.tensor_tensor(bd_l[0:EXPERTS, :], bd2[0:EXPERTS, :], f32(bd_h[0:EXPERTS, :]), ALU.subtract)\
                .then_inc(bd_split, 1)
            stats2(0, 0)
            normalise2(0)
            n = 0
            for a, c in CHUNKS:
                for m in range(3):
                    n += 1
                    dve.wait_ge(w_high, n)
                    dve.tensor_tensor(w3_hl[:, LO, m, a:c, :], w3[:, m, a:c, :], f32(w3_hl[:, HI, m, a:c, :]),
                                      ALU.subtract).then_inc(w_split, 1)
                if a == 0:
                    add_br(0)
                    route(0)
                    split_weight(0, 0)
            for p in range(LAG + 1):
                hidden_of(0, p, p % 2)
            with dve.Fori(0, BATCH - 1) as b:
                tile_body(b, 0, True)
                tile_body(b, 1, True)
            tile_body(BATCH - 1, 0, True)
            tile_body(BATCH - 1, 1, False)

        @block.scalar
        def _(act):
            act.sem_inc(y2_done, 1)
            act.wait_ge(mod_in, 32)
            act.activation(cT[:, 1, :], cT[:, 0, :], ACT.Exp, scale=-1.0).then_inc(c_exp, 1)

            def exponent(n, i):
                k = PLACE[i]
                act.wait_ge(max_done, BLOCKS * n + k + 1)
                act.activation(probs[:, PROB_AT[i]:PROB_AT[i + 1]], scores[k % 2][:, 0:P * (i + 1)], ACT.Exp,
                               bias=nmax[:, i:i + 1], accum_out=total[:, i:i + 1]).then_inc(exp_done, 1)

            def high(n, s):
                u, j = STEPS[s]
                at = slice(P * max(j - 4 * u, 0), HALF)
                act.wait_ge(applied, NSTEP * n + s + 1)
                act.wait_ge(p_turned, NSTEP * n + s + 1)
                act.activation(pT_hl[:, HI, s % RING, at], turned[s % 2][:, at], ACT.Copy).then_inc(p_high, 1)

            def out_high(n, h, u):
                at = slice(u * HALF, (u + 1) * HALF)
                wait_apart(act, attn_in, ATTN_IN, (applied, RING + NSTEP * n + (4, 12)[u]))
                act.activation(oT_hl[:, HI, row(h), at].rearrange("p a t -> p (a t)"), mixed[:], ACT.Identity,
                               bias=bkvT[:, 1:2]).then_inc(o_high, 1)

            def segment(todo, n, h, more, prev):
                for what, i in todo:
                    if what == "exp":
                        if (what, i) not in NEXT_HEAD:
                            exponent(n, i)
                        elif more:
                            exponent(n + 1, i)
                    elif what == "high":
                        high(n, i)
                    elif what == "out":
                        out_high(n, h, i)
                    elif prev:
                        out_high(n - 1, h - 1, i)

            def modulate(b, u):
                at = slice(u * HALF, (u + 1) * HALF)
                act.wait_ge(x_turned, b * 2 + u + 1)
                act.activation(hT[:, at], scores[0][:, at], ACT.Identity, bias=ln_mod[:, 0:1],
                               scale=ln_mod[:, 1:2]).then_inc(hT_done, 1)

            def key_high(b, u):
                at = slice(u * HALF, (u + 1) * HALF)
                act.wait_ge(k_sum, b * 2 + u + 1)
                act.activation(kT_hl[:, HI, at], kT[:, at], ACT.Copy, scale=SCALE).then_inc(k_high, 1)

            def value_high(b, u):
                at = slice(u * HALF, (u + 1) * HALF)
                act.wait_ge(v_mm, b * 2 + u + 1)
                act.activation(v_hl[:, HI, at], turned[u][:], ACT.Copy).then_inc(v_high, 1)

            def gated(b, u):
                act.wait_ge(y_mm, b * 2 + u + 1)
                act.activation(yT[:, u, :], scores[1][:, u * HALF:(u + 1) * HALF], ACT.Identity,
                               scale=cur[:, GATE_A:GATE_A + 1]).then_inc(y_done, 1)

            def turn_row(b, old, new):
                n = (b + 1) * HEADS - 1
                for what, i in ACT_TAIL:
                    if not (old if what in OLD_ROW or what == "y" else new):
                        continue
                    if what == "exp":
                        exponent(n + 1, i)
                    elif what == "out":
                        out_high(n, HEADS - 1, i)
                    elif what == "high":
                        high(n, i)
                    elif what == "y":
                        gated(b, i)
                    else:
                        {"x": modulate, "k_high": key_high, "v_high": value_high}[what](b + 1, i)

            def heads(b):
                first = b * HEADS
                segment(ACT_A, first, 0, True, False)
                with act.Fori(0, HEADS - 2) as h:
                    segment(ACT_B, first + h, h, True, True)
                    segment(ACT_A, first + (h + 1), h + 1, True, True)
                segment(ACT_B, first + (HEADS - 2), HEADS - 2, True, True)
                segment(ACT_A, first + (HEADS - 1), HEADS - 1, False, True)

            turn_row(-1, False, True)
            with act.Fori(0, BATCH - 1) as b:
                heads(b)
                turn_row(b, True, True)
            heads(BATCH - 1)
            turn_row(BATCH - 1, True, False)

            act.wait_ge(ffn_in, FFN_IN)
            act.wait_ge(y_mm, 2 * BATCH)

            def modulate2(t, r):
                act.wait_ge(x2_turned, t + 1)
                act.activation(x2T[:, r, :], misc_ps[:], ACT.Identity, bias=ln_mod[:, 0:1], scale=ln_mod[:, 1:2])\
                    .then_inc(x2_done, 1)

            def affinity(t):
                act.wait_ge(logit_done, t + 1)
                act.activation(aff[:], lg[:], ACT.Sigmoid).then_inc(aff_done, 1)

            def silu(t, p, r):
                g = t * UNITS + p
                if p >= 2 or not is_first(t):
                    act.wait_ge(hidden, g - 1)
                act.wait_ge(gate_mm, g + 1)
                act.activation(gs[:, r, :], gate_ps[r][:], ACT.Silu, bias=b2[:, 0, p:p + 1]).then_inc(silu_done, 1)

            def gated_out(t, b):
                act.wait_ge(gate_cur, b + 1)
                act.wait_ge(down_mm, CREDIT + (t + 1) * UNITS)
                act.activation(yT[:, 1, :], acc_ps[:], ACT.Identity, bias=gate_bds[:], scale=cur[:, GATE_F:])\
                    .then_inc(y2_done, 1)

            def tile_body(b, u, more):
                t = b * TILES + u
                r1 = (u + 1) % 2
                for p in range(LAG + 1, UNITS):
                    silu(t, p, (u + p) % 2)
                    if more and p == 6:
                        modulate2(t + 1, r1)
                    if more and p == 10:
                        affinity(t + 1)
                if more:
                    for p in range(2):
                        silu(t + 1, p, (r1 + p) % 2)
                gated_out(t, b)
                if more:
                    silu(t + 1, 2, r1)

            modulate2(0, 0)
            for a, c in CHUNKS:
                for m in range(3):
                    act.activation(w3_hl[:, HI, m, a:c, :], w3[:, m, a:c, :], ACT.Copy).then_inc(w_high, 1)
                if a == 0:
                    affinity(0)
            for p in range(LAG + 1):
                silu(0, p, p % 2)
            with act.Fori(0, BATCH - 1) as b:
                tile_body(b, 0, True)
                tile_body(b, 1, True)
            tile_body(BATCH - 1, 0, True)
            tile_body(BATCH - 1, 1, False)

        @block.tensor
        def _(pe):
            pe.sem_inc(applied, RING)
            pe.sem_inc(down_mm, CREDIT)
            pe.wait_ge(mod_in, 32)
            pe.wait_ge(dve_setup, 3)
            for j in range(6):
                mm = pe.matmul(project[:, j * BATCH:(j + 1) * BATCH], wmod[:, j * P:(j + 1) * P], cT[:, 3, :],
                               start=True, stop=True)
            mm.then_inc(mod_mm, 1)
            pe.wait_ge(attn_in, ATTN_IN)
            pe.wait_ge(pool_setup, 5)

            def project_q(n, u):
                at = slice(u * HALF, (u + 1) * HALF)
                pe.wait_ge(wq_split, n + 1)
                pe.wait_ge(q_sum, CREDIT + 2 * n + u)
                split3(pe, project[:], hl(wq_hl), hl(hT_hl, at)).then_inc(q_mm, 1)

            def score(n, i, wait=True):
                k, u = PLACE[i], i // 4
                pe.wait_ge(q_split, CREDIT + 2 * n + u + 1)
                if wait:
                    pe.wait_ge(exp_done, BLOCKS * n + k - 1)
                width = P * (i + 1)
                diagonal = slice(P * i, width)
                for c in range(0, width, HALF):
                    at = slice(c, min(c + HALF, width))
                    q, kk = hl(qT_hl, slice(P * i, P * (i + 1))), hl(kT_hl, at)
                    pe.matmul(scores[k % 2][:, at], q[HI], kk[HI], start=True, stop=False)
                    if at.stop == width:
                        pe.matmul(scores[k % 2][:, diagonal], eye_b[:], mask_b[:], start=False, stop=False)
                    pe.matmul(scores[k % 2][:, at], q[HI], kk[LO], start=False, stop=False)
                    mm = pe.matmul(scores[k % 2][:, at], q[LO], kk[HI], start=False, stop=True)
                mm.then_inc(score_mm, 1)

            def turn(n, s):
                u, j = STEPS[s]
                pe.wait_ge(normed, BLOCKS * n + 4 * (u + 1))
                pe.wait_ge(p_split, CREDIT + NSTEP * n + s - 1)
                for i in range(max(j, 4 * u), 4 * (u + 1)):
                    mm = pe.transpose(turned[s % 2][:, P * (i - 4 * u):P * (i - 4 * u + 1)],
                                      probs[:, PROB_AT[i] + P * j:PROB_AT[i] + P * (j + 1)], eye[:])
                mm.then_inc(p_turned, 1)

            def apply(n, s):
                u, j = STEPS[s]
                at = slice(P * max(j - 4 * u, 0), HALF)
                pe.wait_ge(p_split, CREDIT + NSTEP * n + s + 1)
                if j == 0:
                    pe.wait_ge(o_split, CREDIT + 2 * n + u)
                values = hl(v_hl, slice(P * j, P * (j + 1)))
                split3(pe, mixed[:, at], values, [pT_hl[:, a, s % RING, at] for a in (HI, LO)],
                       first=(j == 0), last=(j == 4 * u + 3)).then_inc(applied, 1)

            def segment(todo, n, more, prev):
                for what, i in todo:
                    if what == "apply_prev":
                        if prev:
                            apply(n - 1, i)
                        continue
                    m = n + 1 if (what, i) in NEXT_HEAD else n
                    if (what, i) in NEXT_HEAD and not more:
                        continue
                    {"score": score, "turn": turn, "apply": apply, "project": project_q}[what](m, i)

            def turn_x(b, u):
                pe.wait_ge(xn_done, b * 2 + u + 1)
                for k in range(4 * u, 4 * u + 4):
                    mm = pe.transpose(scores[0][:, P * k:P * (k + 1)], xn[:, k, :], eye[:])
                mm.then_inc(x_turned, 1)

            def keys(b, u):
                at = slice(u * HALF, (u + 1) * HALF)
                pe.wait_ge(hT_split, b * 2 + u + 1)
                split3(pe, scores[0][:, at], hl(wkv_hl, slice(0, P)), hl(hT_hl, at)).then_inc(k_mm, 1)

            def values(b, u):
                for k in range(4 * u, 4 * u + 4):
                    mm = split3(pe, turned[u][:, P * (k - 4 * u):P * (k - 4 * u + 1)],
                                hl(hT_hl, slice(P * k, P * (k + 1))), hl(wkv_hl, slice(P, 2 * P)))
                mm.then_inc(v_mm, 1)

            def project_out(b, part):
                u = min(part, 1)
                if part < 2:
                    pe.wait_ge(o_split, CREDIT + b * 2 * HEADS + 2 * HEADS - 1 + u)
                at = slice(u * HALF, (u + 1) * HALF)
                for h in (range(HEADS), range(HEADS // 2), range(HEADS // 2, HEADS))[part]:
                    mm = split3(pe, scores[1][:, at], hl(wo_hl, h), hl(oT_hl, h, at),
                                first=(h == 0), last=(h == HEADS - 1))
                if part != 1:
                    mm.then_inc(y_mm, 1)

            def turn_y(b, u):
                pe.wait_ge(y_done, b * 2 + u + 1)
                for k in range(4):
                    mm = pe.transpose(y_ps[u][:, P * k:P * (k + 1)], yT[:, u, P * k:P * (k + 1)], eye[:])
                mm.then_inc(y_turned, 1)

            def turn_row(b, old, new):
                n = (b + 1) * HEADS - 1
                for what, i in PE_TAIL:
                    if not (old if what in OLD_ROW or what == "y" else new):
                        continue
                    if what in ("turn", "apply"):
                        {"turn": turn, "apply": apply}[what](n, i)
                    elif what in ("wo", "y"):
                        {"wo": project_out, "y": turn_y}[what](b, i)
                    elif what == "project":
                        project_q(n + 1, i)
                    elif what == "score":
                        if i == 3:
                            pe.wait_ge(k_split, b * 2 + 4)
                        if i == 2 and old:
                            pe.wait_ge(y_done, b * 2 + 1)
                        score(n + 1, i, wait=PLACE[i] >= 2)
                    else:
                        {"x": turn_x, "keys": keys, "values": values}[what](b + 1, i)

            def heads(b):
                first = b * HEADS
                pe.wait_ge(x1_done, CREDIT + 2 * b)
                pe.wait_ge(v_split, 2 * b + 2)
                segment(PE_A, first, True, False)
                with pe.Fori(0, HEADS - 2) as h:
                    segment(PE_B, first + h, True, True)
                    segment(PE_A, first + (h + 1), True, True)
                segment(PE_B, first + (HEADS - 2), True, True)
                segment(PE_A, first + (HEADS - 1), False, True)

            turn_row(-1, False, True)
            with pe.Fori(0, BATCH - 1) as b:
                heads(b)
                turn_row(b, True, True)
            heads(BATCH - 1)
            turn_row(BATCH - 1, True, False)

            def turn_x2(t):
                pe.wait_ge(xn2_done, t + 1)
                for k in range(4):
                    mm = pe.transpose(misc_ps[:, P * k:P * (k + 1)], xn[:, k, :], eye[:])
                mm.then_inc(x2_turned, 1)

            def logits(t, r):
                pe.wait_ge(x2_done, t + 1)
                for k in range(4):
                    mm = pe.matmul(misc_ps[:, EXPERTS * k:EXPERTS * (k + 1)], x2T[:, r, P * k:P * (k + 1)], wr[:],
                                   start=True, stop=True)
                mm.then_inc(logit_mm, 1)

            def turn_weights(t):
                wait_apart(pe, pool_setup, 5, (weight_done, t + 1))
                for k in range(4):
                    mm = pe.transpose(misc_ps[0:2 * EXPERTS, P * k:P * (k + 1)], weight2[:, k, :], eye[:])
                mm.then_inc(weight_turned, 1)

            def up_gate(t, g, p, q, r):
                if p == 0:
                    pe.wait_ge(x2_split, t + 1)
                    pe.wait_ge(weight_split, t + 1)
                pe.wait_ge(silu_done, g - 1) if p >= 2 or not is_first(t) else None
                right = [x2T_hl[:, a, q, :] for a in (HI, LO)]
                split3(pe, gate_ps[r][:], hl(w3_hl, 0, p), right).then_inc(gate_mm, 1)
                if p >= 2 or not is_first(t):
                    pe.wait_ge(hidden, g - 1)
                if p < PAIRS:
                    pe.matmul(weight_ps[r], pick[:, p, :], weightT[:, q, :], start=True, stop=True)
                split3(pe, up_ps[r], hl(w3_hl, 1, p), right).then_inc(up_mm, 1)

            def down(t, g, p, q, r):
                if p == 0:
                    pe.wait_ge(y2_done, t + 1)
                    pe.matmul(acc_ps[:], bd_h[:], weightT[:, q, :], start=True, stop=False)
                    pe.matmul(acc_ps[:], bd_l[:], weightT[:, q, :], start=False, stop=False)
                pe.wait_ge(act_split, CREDIT + g + 1)
                mm = split3(pe, acc_ps[:], hl(w3_hl, 2, p), [act_hl[:, a, r, :] for a in (HI, LO)],
                            first=False, last=(p == PAIRS)).then_inc(down_mm, 1)
                return mm

            def turn_out(t):
                pe.wait_ge(y2_done, t + 2)
                for k in range(4):
                    mm = pe.transpose(misc_ps[:, P * k:P * (k + 1)], yT[:, 1, P * k:P * (k + 1)], eye[:])
                mm.then_inc(y2_turned, 1)

            def tile_body(b, u, more):
                t = b * TILES + u
                q, q1 = u % 2, (u + 1) % 2
                for p in range(LAG + 1, UNITS):
                    up_gate(t, t * UNITS + p, p, q, (u + p) % 2)
                    down(t, t * UNITS + p - LAG, p - LAG, q, (u + p) % 2)
                    if more:
                        if p == 6:
                            turn_x2(t + 1)
                        if p == 8:
                            logits(t + 1, q1)
                        if p == 12:
                            turn_weights(t + 1)
                for p in range(LAG):
                    if more:
                        up_gate(t + 1, (t + 1) * UNITS + p, p, q1, (q1 + p) % 2)
                    down(t, t * UNITS + UNITS - LAG + p, UNITS - LAG + p, q, (u + UNITS - LAG + p) % 2)
                if more:
                    up_gate(t + 1, (t + 1) * UNITS + LAG, LAG, q1, (q1 + LAG) % 2)
                turn_out(t)
                if more:
                    down(t + 1, (t + 1) * UNITS, 0, q1, q1)

            turn_x2(0)
            logits(0, 0)
            turn_weights(0)
            pe.wait_ge(pick_done, 2)
            pe.wait_ge(bd_split, 1)
            pe.wait_ge(w_split, 3)
            up_gate(0, 0, 0, 0, 0)
            pe.wait_ge(w_split, 6)
            up_gate(0, 1, 1, 0, 1)
            up_gate(0, 2, 2, 0, 0)
            down(0, 0, 0, 0, 0)
            pe.wait_ge(w_split, 3 * len(CHUNKS))
            with pe.Fori(0, BATCH - 1) as b:
                tile_body(b, 0, True)
                tile_body(b, 1, True)
            tile_body(BATCH - 1, 0, True)
            tile_body(BATCH - 1, 1, False)


_INS = ['L0_attn_x', 'L0_attn_Wq', 'L0_attn_bq', 'L0_attn_Wkv', 'L0_attn_bkv', 'L0_attn_Wo', 'L0_ffn_Wr',
        'L0_ffn_br', 'L0_ffn_Wg_s', 'L0_ffn_bg_s', 'L0_ffn_Wu_s', 'L0_ffn_bu_s', 'L0_ffn_Wd_s', 'L0_ffn_bd_s',
        'L0_ffn_Wg', 'L0_ffn_bg', 'L0_ffn_Wu', 'L0_ffn_bu', 'L0_ffn_Wd', 'L0_ffn_bd', 'L0_c', 'L0_wmod']
_OUTS = [((BATCH, TOKENS, P), 'float32')]


def constants():
    eye = np.eye(P, dtype=np.float32)
    pos = np.arange(TOKENS, dtype=np.float32)[:, None]
    inv_freq = np.exp(np.float32(-math.log(10000.0)) * np.arange(0, P, 2, dtype=np.float32) / np.float32(P))
    angle = (pos * inv_freq[None, :].astype(np.float32)).astype(np.float32)
    pe = np.zeros((TOKENS, P), np.float32)
    pe[:, 0::2] = np.sin(angle)
    pe[:, 1::2] = np.cos(angle)
    mask = np.where(np.tril(np.ones((P, P), bool)), 0.0, MASKED).astype(np.float32)
    pick = np.zeros((2 * EXPERTS, PAIRS, P), np.float32)
    for e in range(EXPERTS):
        for half in range(2):
            pick[half * EXPERTS + e, e // 2, (e % 2) * INNER:(e % 2 + 1) * INNER] = 1.0
    return {"eye": eye, "pe": np.ascontiguousarray(pe.T), "mask": mask, "pick": pick}


def laid_out(name, a):
    if name == "L0_c":
        return a.T
    if name in ("L0_attn_bq", "L0_attn_bkv"):
        return a.reshape(-1, P).T
    if name in ("L0_ffn_bg_s", "L0_ffn_bu_s", "L0_ffn_bd_s"):
        return a.reshape(-1, 1)
    if name in ("L0_ffn_bg", "L0_ffn_bu"):
        return a.reshape(PAIRS, P).T
    if name in ("L0_ffn_Wg", "L0_ffn_Wu"):
        return a.reshape(PAIRS, 2, P, INNER).transpose(2, 0, 1, 3).reshape(P, PAIRS, P)
    if name == "L0_ffn_Wd":
        return a.reshape(PAIRS, P, P).transpose(1, 0, 2)
    return a


def kernel(**inputs):
    import numpy as _np
    import concourse.bacc as _bacc
    from concourse import mybir as _mybir
    from concourse.bass_utils import run_bass_kernel_spmd as _run

    nc = _bacc.Bacc("TRN2", target_bir_lowering=False, num_devices=1)
    arrays, args = {}, []
    for name, a in [(name, laid_out(name, _np.asarray(inputs[name]))) for name in _INS] + list(constants().items()):
        a = _np.ascontiguousarray(a)
        arrays[f"in_{name}_dram"] = a
        args.append(nc.dram_tensor(f"in_{name}_dram", a.shape, _mybir.dt.from_np(a.dtype), kind="ExternalInput").ap())
    for i, (shape, dtype) in enumerate(_OUTS):
        dt = _mybir.dt.from_np(_np.dtype(dtype))
        args.append(nc.dram_tensor(f"out_{i}_dram", shape, dt, kind="ExternalOutput").ap())
    bass_adaln_attention_moe(nc, *args)
    r = _run(nc, [arrays], core_ids=[0])
    got = tuple(r.results[0][f"out_{i}_dram"] for i in range(len(_OUTS)))
    return got[0]
```

```python
import math
from contextlib import ExitStack

import numpy as np

import concourse.bass as bass
from concourse import mybir

F32 = mybir.dt.float32
F32R = mybir.dt.float32r
BF16 = mybir.dt.bfloat16
ALU = mybir.AluOpType
ACT = mybir.ActivationFunctionType
AX_X = mybir.AxisListType.X

P = 128
BATCH, TOKENS = 4, 1024
BLOCKS = TOKENS // P
HEADS = 8
HALF = 512
TILES = TOKENS // HALF
EXPERTS, INNER, TOP = 32, 64, 8
PAIRS = EXPERTS // 2
UNITS = PAIRS + 1
LN_EPS = 1e-5
MASKED = -1e30
SCALE = 1.0 / math.sqrt(P)
HI, LO = 0, 1

SHIFT_A, SCALE_A, GATE_A, SHIFT_F, SCALE_F, GATE_F = range(6)

PASSES = ((HI, HI), (LO, HI), (HI, LO))

ORDER = [3, 2, 1, 0, 7, 6, 5, 4]
PLACE = [ORDER.index(i) for i in range(BLOCKS)]
STEPS = [(0, j) for j in range(4)] + [(1, j) for j in range(8)]
NSTEP = len(STEPS)
PROB_AT = [P * i * (i + 1) // 2 for i in range(BLOCKS + 1)]

PE_A = [("project", 0), ("turn", 0), ("apply_prev", 10), ("apply_prev", 11), ("score", 6), ("turn", 1), ("score", 5),
        ("apply", 0), ("turn", 2), ("apply", 1), ("score", 4), ("turn", 3), ("apply", 2)]
PE_B = [("score", 3), ("apply", 3), ("score", 2), ("turn", 4), ("turn", 5), ("project", 1), ("score", 1), ("turn", 6),
        ("apply", 4), ("score", 0), ("turn", 7), ("apply", 5), ("turn", 8), ("apply", 6), ("turn", 9), ("apply", 7),
        ("score", 7), ("turn", 10), ("apply", 8), ("turn", 11), ("apply", 9)]
DVE_A = [("query", 0), ("inverse", 7), ("low", 0), ("out_prev", 1), ("max", 6), ("low", 1), ("max", 5),
         ("inverse", 6), ("low", 2), ("max", 4), ("low", 3), ("inverse", 5), ("max", 3), ("inverse", 4), ("norm", 4)]
DVE_B = [("out", 0), ("max", 2), ("inverse", 3), ("low", 4), ("inverse", 2), ("max", 1), ("low", 5), ("query", 1),
         ("max", 0), ("inverse", 1), ("low", 6), ("inverse", 0), ("low", 7), ("low", 8), ("low", 9), ("max", 7),
         ("low", 10), ("low", 11)]
ACT_A = [("exp", 7), ("high", 0), ("out_prev", 1), ("high", 1), ("exp", 6), ("high", 2), ("exp", 5), ("high", 3),
         ("exp", 4)]
ACT_B = [("out", 0), ("exp", 3), ("high", 4), ("exp", 2), ("high", 5), ("exp", 1), ("high", 6), ("exp", 0),
         ("high", 7), ("high", 8), ("high", 9), ("high", 10), ("high", 11)]
POOL_A = [("weights", 0), ("query", 0), ("norm", 7), ("norm", 6), ("norm", 5)]
POOL_B = [("norm", 3), ("norm", 2), ("query", 1), ("norm", 1), ("norm", 0)]
NEXT_HEAD = {("score", 7), ("max", 7), ("project", 0), ("project", 1), ("query", 0), ("query", 1), ("weights", 0)} | {
    (w, i) for w in ("score", "max", "exp", "inverse", "norm") for i in range(4)}
PE_TAIL = [("wo", 0), ("apply", 3), ("turn", 4), ("turn", 5), ("wo", 1), ("turn", 6), ("apply", 4), ("turn", 7),
           ("apply", 5), ("turn", 8), ("apply", 6), ("turn", 9), ("apply", 7), ("turn", 10), ("apply", 8), ("x", 0),
           ("ffn", 0), ("turn", 11), ("apply", 9), ("apply", 10), ("x", 1), ("ffn", 1), ("wo", 2), ("apply", 11),
           ("ffn", 2), ("wo", 3), ("ffn", 3), ("keys", 0), ("keys", 1), ("project", 0), ("values", 0), ("project", 1),
           ("values", 1), ("wo", 4), ("wo", 5), ("y", 0), ("score", 3), ("score", 2), ("wo", 6), ("ffn", 4),
           ("wo", 7), ("score", 1), ("score", 0), ("y", 1), ("score", 7)]
DVE_TAIL = [("stats", 0), ("ffn", 0), ("low", 4), ("out", 0), ("low", 5), ("stats", 1), ("low", 6), ("aggregate", 0),
            ("ffn", 1), ("low", 7), ("low", 8), ("x", 0), ("ffn", 2), ("low", 9), ("low", 10), ("x", 1), ("ffn", 3),
            ("low", 11), ("out", 1), ("ffn", 4), ("ffn", 5), ("ffn", 6), ("k_sum", 0), ("k_sum", 1), ("query", 0),
            ("k_low", 0), ("k_low", 1), ("query", 1), ("v_low", 0), ("v_low", 1), ("y", 0), ("ffn", 7), ("max", 3),
            ("max", 2), ("inverse", 3), ("inverse", 2), ("max", 1), ("max", 0), ("inverse", 1), ("inverse", 0),
            ("y", 1), ("max", 7)]
ACT_TAIL = [("out", 0), ("high", 4), ("high", 5), ("high", 6), ("high", 7), ("high", 8), ("high", 9), ("high", 10),
            ("x", 0), ("ffn", 0), ("high", 11), ("x", 1), ("ffn", 1), ("out", 1), ("ffn", 2), ("y", 0), ("ffn", 3),
            ("k_high", 0), ("k_high", 1), ("v_high", 0), ("v_high", 1), ("exp", 3), ("exp", 2), ("y", 1), ("exp", 1),
            ("exp", 0)]
POOL_TAIL = [("rstd", 0), ("weights", 0), ("x", 0), ("x", 1), ("query", 0), ("query", 1), ("weights", 1), ("norm", 3),
             ("norm", 2), ("norm", 1), ("norm", 0)]
OLD_ROW = {"turn", "apply", "wo", "low", "high", "out", "y"}
RING = 3

LAG = 3
AHEAD = 3


def score_at(i):
    width = P * (i + 1)
    return 0 if width <= HALF else HALF - width // 2


def slot(p):
    return p % RING


def split_next(p):
    return range(AHEAD + 1) if p == 0 else range(p + AHEAD, min(p + AHEAD + 1, UNITS))


def bass_adaln_attention_moe(nc, x_in, Wq, bq, Wkv, bkv, Wo, Wr, br, Wg_s, bg_s, Wu_s, bu_s, Wd_s, bd_s,
                             Wg, bg, Wu, bu, Wd, bd, c_in, wmod_in, eye_in, pe_in, mask_in, pick_in, out):
    with ExitStack() as ctx:
        def sb(name, shape, dt=F32):
            return ctx.enter_context(nc.sbuf_tensor(name, shape, dt))

        def psum(name, shape):
            return ctx.enter_context(nc.psum_tensor(name, shape, F32))

        def sem(name):
            return ctx.enter_context(nc.semaphore(name))

        x = sb("x", [P, BATCH * BLOCKS, P])
        eye = sb("eye", [P, P])
        eye_b = sb("eye_b", [P, P], BF16)
        mask = sb("mask", [P, P])
        mask_b = sb("mask_b", [P, P], BF16)
        mod = sb("mod", [P, BATCH, 6])
        cur = sb("cur", [P, 6])
        wq = sb("wq", [P, HEADS, P])
        wq_hl = sb("wq_hl", [P, 2, P], F32R)
        wkv = sb("wkv", [P, 2 * P])
        wkv_hl = sb("wkv_hl", [P, 2, 2 * P], F32R)
        wo_hl = sb("wo_hl", [P, 2, HEADS, P], F32R)
        bqT = sb("bqT", [P, HEADS])
        bkvT = sb("bkvT", [P, 2])
        peT = sb("peT", [P, TOKENS])
        stats = sb("stats", [P, BLOCKS, 6])
        mv = sb("mv", [P, BLOCKS, 2])
        var_eps = sb("var_eps", [P, BLOCKS])
        rstd = sb("rstd", [P, BLOCKS])
        minus_half = sb("minus_half", [P, BLOCKS])
        hT = sb("hT", [P, TOKENS])
        hT_hl = sb("hT_hl", [P, 2, TOKENS], F32R)
        kT_hl = sb("kT_hl", [P, 2, TOKENS], F32R)
        v_hl = sb("v_hl", [P, 2, TOKENS], F32R)
        qT = sb("qT", [P, TOKENS])
        qT_hl = sb("qT_hl", [P, 2, TOKENS], F32R)
        nmax = sb("nmax", [P, BLOCKS])
        total = sb("total", [P, BLOCKS])
        rtotal = sb("rtotal", [P, BLOCKS])
        probs = sb("probs", [P, PROB_AT[BLOCKS]])
        pT_hl = sb("pT_hl", [P, 2, RING, HALF], F32R)
        yT = sb("yT", [P, 2, HALF])
        arena = sb("arena", [P, 2 * HEADS * TOKENS], F32R)
        w3 = sb("w3", [P, 3, UNITS, P])
        b2 = sb("b2", [P, 2, UNITS])
        wr = sb("wr", [P, EXPERTS])
        br_rows = sb("br_rows", [P, EXPERTS])
        bd2 = sb("bd2", [2 * EXPERTS, P])
        bd_h = sb("bd_h", [2 * EXPERTS, P], F32R)
        bd_l = sb("bd_l", [2 * EXPERTS, P], F32R)
        bds = sb("bds", [P, 1])
        gate_bds = sb("gate_bds", [P, 1])
        cT = sb("cT", [P, 4, BATCH])
        c_inv = sb("c_inv", [P, BATCH])
        sign = sb("sign", [P, 2, BATCH])
        floor = sb("floor", [P, 2, BATCH])
        top = sb("top", [P, BLOCKS, TOP])
        top_sum = sb("top_sum", [P, BLOCKS])
        top_eps = sb("top_eps", [P, BLOCKS])
        top_inv = sb("top_inv", [P, BLOCKS])
        weight2 = sb("weight2", [P, BLOCKS, 2 * EXPERTS])
        ln_mod = sb("ln_mod", [P, 2])
        oT_hl = arena[:, :].rearrange("p (a h t) -> p a h t", a=2, h=HEADS)
        w3_hl = arena[:, 0:6 * UNITS * P].rearrange("p (a m u n) -> p a m u n", a=2, m=3, u=UNITS)
        xn = yT[:, :, :].rearrange("p u (k e) -> p (u k) e", e=P)
        wo = qT[:, :].rearrange("p (h e) -> p h e", h=HEADS)
        kT = hT
        wmod = probs[:, 0:6 * P]
        gs = probs[:, 0:2 * HALF].rearrange("p (r t) -> p r t", r=2)
        prod = probs[:, 2 * HALF:4 * HALF].rearrange("p (r t) -> p r t", r=2)
        hf = probs[:, 4 * HALF:6 * HALF].rearrange("p (r t) -> p r t", r=2)
        act_hl = pT_hl
        routing = peT[:, :].rearrange("p (j k e) -> p j k e", j=4, k=BLOCKS)
        lg, aff, rest, chosen = [routing[:, j] for j in range(4)]
        x2T = hT[:, :].rearrange("p (r t) -> p r t", r=2)
        x2T_hl = hT_hl[:, :, :].rearrange("p a (r t) -> p a r t", r=2)
        weightT = v_hl[0:2 * EXPERTS, 0, :].rearrange("p (r t) -> p r t", r=2)
        pick_raw = [wq[0:2 * EXPERTS, :, :], wo[0:2 * EXPERTS, :, :]]
        pick = qT_hl[0:2 * EXPERTS, :, :].rearrange("p a (u n) -> p (a u) n", n=P)

        turned = [psum("turned0", [P, HALF]), psum("turned1", [P, HALF])]
        mixed = psum("mixed", [P, HALF])
        project = psum("project", [P, HALF])
        scores = [psum("scores0", [P, 2 * HALF]), psum("scores1", [P, 2 * HALF])]
        wo_ps = [project[:], scores[1][:, HALF:]]
        y_ps = [mixed[:], turned[1][:]]
        gate_ps = turned
        acc_ps = mixed
        misc_ps = project
        first_ps = [scores[0][:, 0:HALF], scores[0][:, HALF:]]
        up_ps = [scores[0][:, 0:HALF], scores[0][:, HALF:]]
        weight_ps = [scores[1][:, 0:HALF], scores[1][:, HALF:]]

        c_loaded = sem("c_loaded")
        mod_in = sem("mod_in")
        eye_loaded = sem("eye_loaded")
        attn_in = sem("attn_in")
        x_first = sem("x_first")
        x_rest = sem("x_rest")
        ffn_in = sem("ffn_in")
        pick_loaded = sem("pick_loaded")
        stored = sem("stored")
        padded = sem("padded")
        c_exp = sem("c_exp")
        wo_high = sem("wo_high")
        wo_split = sem("wo_split")
        dve_setup = sem("dve_setup")
        mod_mm = sem("mod_mm")
        pool_setup = sem("pool_setup")
        ln_step = sem("ln_step")
        rstd_done = sem("rstd_done")
        xn_done = sem("xn_done")
        x_turned = sem("x_turned")
        hT_done = sem("hT_done")
        hT_high = sem("hT_high")
        hT_split = sem("hT_split")
        k_mm = sem("k_mm")
        k_sum = sem("k_sum")
        k_high = sem("k_high")
        k_split = sem("k_split")
        v_mm = sem("v_mm")
        v_high = sem("v_high")
        v_split = sem("v_split")
        wq_high = sem("wq_high")
        wq_split = sem("wq_split")
        q_mm = sem("q_mm")
        q_sum = sem("q_sum")
        q_high = sem("q_high")
        q_split = sem("q_split")
        score_mm = sem("score_mm")
        max_done = sem("max_done")
        exp_done = sem("exp_done")
        inverted = sem("inverted")
        normed = sem("normed")
        normed_last = sem("normed_last")
        p_turned = sem("p_turned")
        p_high = sem("p_high")
        p_split = sem("p_split")
        applied = sem("applied")
        o_high = sem("o_high")
        o_split = sem("o_split")
        y_mm = sem("y_mm")
        y_done = sem("y_done")
        y_turned = sem("y_turned")
        x1_done = sem("x1_done")
        w_high = sem("w_high")
        w_split = sem("w_split")
        w_split_pool = sem("w_split_pool")
        bd_high = sem("bd_high")
        bd_split = sem("bd_split")
        pick_done = sem("pick_done")
        ln2_step = sem("ln2_step")
        rstd2_done = sem("rstd2_done")
        xn2_done = sem("xn2_done")
        x2_turned = sem("x2_turned")
        x2_done = sem("x2_done")
        x2_high = sem("x2_high")
        x2_split = sem("x2_split")
        logit_mm = sem("logit_mm")
        logit_done = sem("logit_done")
        aff_done = sem("aff_done")
        route_step = sem("route_step")
        weight_done = sem("weight_done")
        weight_turned = sem("weight_turned")
        weight_high = sem("weight_high")
        weight_split = sem("weight_split")
        gate_mm = sem("gate_mm")
        up_mm = sem("up_mm")
        silu_done = sem("silu_done")
        prod_done = sem("prod_done")
        hidden = sem("hidden")
        act_high = sem("act_high")
        act_split = sem("act_split")
        down_mm = sem("down_mm")
        gate_cur = sem("gate_cur")
        y2_done = sem("y2_done")
        y2_turned = sem("y2_turned")
        out_done = sem("out_done")

        CREDIT = 2


        def f32(ap):
            return ap.bitcast(F32)

        def row(b):
            return bass.ds(b, 1)

        def wait_apart(engine, loaded, count, *waits):
            known = [(signal, value if isinstance(value, int) else engine.to_reg(value)) for signal, value in waits]
            engine.wait_ge(loaded, count)
            for signal, value in known:
                engine.wait_ge(signal, value)

        def split3(pe, to, left, right, first=True, last=True):
            for n, (a, c) in enumerate(PASSES):
                mm = pe.matmul(to, left[a], right[c], start=first and n == 0, stop=last and n == 2)
            return mm

        def hl(ap, *at):
            return [ap[(slice(None), part) + at] for part in (HI, LO)]

        def is_first(t):
            return isinstance(t, int) and t == 0

        block = ctx.enter_context(nc.Block())

        @block.sync
        def _(sp):
            sp.dma_start(cT[:, 0, :], c_in).then_inc(c_loaded, 16)
            xd = x_in.rearrange("b (n p) e -> b p n e", p=P)
            sp.dma_start(x[:, 0:BLOCKS, :], xd[0]).then_inc(x_first, 16)
            sp.dma_start(wmod, wmod_in).then_inc(mod_in, 16)
            sp.dma_start(eye[:], eye_in).then_inc(eye_loaded, 16)
            sp.dma_start(wkv[:], Wkv).then_inc(attn_in, 16)
            sp.dma_start(wq[:], Wq.rearrange("e (h d) -> e h d", h=HEADS)).then_inc(attn_in, 16)
            sp.dma_start(peT[:], pe_in).then_inc(attn_in, 16)
            sp.dma_start(mask[:], mask_in).then_inc(attn_in, 16)
            sp.dma_start(bqT[:], bq).then_inc(attn_in, 16)
            sp.dma_start(bkvT[:], bkv).then_inc(attn_in, 16)
            sp.dma_start(wo[:], Wo.rearrange("(h d) e -> d h e", h=HEADS)).then_inc(attn_in, 16)
            for b in range(1, BATCH):
                sp.dma_start(x[:, b * BLOCKS:(b + 1) * BLOCKS, :], xd[b]).then_inc(x_rest, 16)
            sp.wait_ge(padded, 1)
            for m, (many, one) in enumerate(((Wg, Wg_s), (Wu, Wu_s))):
                sp.dma_start(w3[:, m, 0:PAIRS, :], many).then_inc(ffn_in, 16)
                sp.dma_start(w3[:, m, PAIRS, 0:INNER], one).then_inc(ffn_in, 16)
            sp.dma_start(w3[:, 2, 0:PAIRS, :], Wd).then_inc(ffn_in, 16)
            sp.dma_start(w3[0:INNER, 2, PAIRS, :], Wd_s).then_inc(ffn_in, 16)
            for m, (many, one) in enumerate(((bg, bg_s), (bu, bu_s))):
                sp.dma_start(b2[:, m, 0:PAIRS], many).then_inc(ffn_in, 16)
                sp.dma_start(b2[0:INNER, m, PAIRS:UNITS], one).then_inc(ffn_in, 16)
            sp.dma_start(bds[:], bd_s).then_inc(ffn_in, 16)
            sp.dma_start(wr[:], Wr).then_inc(ffn_in, 16)
            sp.dma_start(br_rows[:], br.rearrange("(a e) -> a e", a=1).broadcast_to([P, EXPERTS])).then_inc(ffn_in, 16)
            sp.dma_start(bd2[0:EXPERTS, :], bd).then_inc(ffn_in, 16)
            sp.dma_start(bd2[EXPERTS:, :], bd).then_inc(ffn_in, 16)
            sp.wait_ge(wq_split, BATCH * HEADS)
            sp.wait_ge(q_split, CREDIT + BATCH * HEADS * 2)
            for k in range(2):
                sp.dma_start(pick_raw[k], pick_in[:, k * HEADS:(k + 1) * HEADS, :]).then_inc(pick_loaded, 16)
            od = out.rearrange("b (n p) e -> p (b n) e", p=P)
            with sp.Fori(0, BATCH * TILES) as t:
                sp.wait_ge(out_done, t + 1)
                sp.dma_start(od[:, bass.ds(t * 4, 4), :], x[:, bass.ds(t * 4, 4), :]).then_inc(stored, 16)
            sp.wait_ge(stored, 16 * BATCH * TILES)

        ATTN_IN = 16 * 7
        FFN_IN = 16 * 15

        @block.gpsimd
        def _(pool):
            pool.memset(minus_half[:], -0.5).then_inc(pool_setup, 1)
            pool.sem_inc(q_split, CREDIT)
            pool.sem_inc(act_split, CREDIT)
            pool.wait_ge(pool_setup, 1)
            pool.wait_ge(ln_step, 3)
            pool.tensor_tensor(rstd[:], var_eps[:], minus_half[:], ALU.pow).then_inc(rstd_done, 1)
            pool.wait_ge(attn_in, ATTN_IN)
            pool.wait_ge(eye_loaded, 16)
            pool.tensor_scalar(wkv_hl[:, HI, :], wkv[:], 1.0, 1.0, ALU.mult, ALU.mult).then_inc(pool_setup, 1)
            pool.wait_ge(pool_setup, 2)
            pool.tensor_tensor(wkv_hl[:, LO, :], wkv[:], f32(wkv_hl[:, HI, :]), ALU.subtract).then_inc(pool_setup, 1)
            pool.tensor_scalar(eye_b[:], eye[:], 1.0, 1.0, ALU.mult, ALU.mult)
            pool.tensor_scalar(mask_b[:], mask[:], 1.0, 1.0, ALU.mult, ALU.mult).then_inc(pool_setup, 1)

            def weights(n, h):
                pool.tensor_copy(wq_hl[:, HI, :], wq[:, row(h), :].rearrange("p a d -> p (a d)")).then_inc(wq_high, 1)
                wait_apart(pool, attn_in, ATTN_IN, (wq_high, n + 1))
                pool.tensor_tensor(wq_hl[:, LO, :], wq[:, row(h), :].rearrange("p a d -> p (a d)"),
                                   f32(wq_hl[:, HI, :]), ALU.subtract).then_inc(wq_split, 1)

            def query(n, u):
                at = slice(u * HALF, (u + 1) * HALF)
                wait_apart(pool, attn_in, ATTN_IN, (q_sum, CREDIT + 2 * n + u + 1))
                pool.tensor_scalar(qT_hl[:, HI, at], qT[:, at], 1.0, 1.0, ALU.mult, ALU.mult).then_inc(q_high, 1)
                pool.wait_ge(q_high, 2 * n + u + 1)
                pool.tensor_tensor(qT_hl[:, LO, at], qT[:, at], f32(qT_hl[:, HI, at]), ALU.subtract)\
                    .then_inc(q_split, 1)

            def norm(n, i):
                wait_apart(pool, attn_in, ATTN_IN, (inverted, BLOCKS * n + PLACE[i] + 1))
                at = slice(PROB_AT[i], PROB_AT[i + 1])
                pool.tensor_scalar(probs[:, at], probs[:, at], rtotal[:, i:i + 1], 1.0, ALU.mult, ALU.mult)\
                    .then_inc(normed, 1)

            def segment(todo, n, h, more):
                for what, i in todo:
                    if (what, i) in NEXT_HEAD:
                        if more:
                            {"weights": lambda n, i: weights(n, h + 1), "norm": norm, "query": query}[what](n + 1, i)
                    else:
                        norm(n, i)

            def rstd_of(b):
                wait_apart(pool, attn_in, ATTN_IN, (ln_step, b * 3 + 3))
                pool.tensor_tensor(rstd[:], var_eps[:], minus_half[:], ALU.pow).then_inc(rstd_done, 1)

            def split_x(b, u):
                at = slice(u * HALF, (u + 1) * HALF)
                wait_apart(pool, attn_in, ATTN_IN, (hT_done, b * 2 + u + 1))
                pool.tensor_scalar(hT_hl[:, HI, at], hT[:, at], 1.0, 1.0, ALU.mult, ALU.mult).then_inc(hT_high, 1)
                pool.wait_ge(hT_high, b * 2 + u + 1)
                pool.tensor_tensor(hT_hl[:, LO, at], hT[:, at], f32(hT_hl[:, HI, at]), ALU.subtract)\
                    .then_inc(hT_split, 1)

            def prepare(b):
                for what, i in POOL_TAIL:
                    if what == "rstd":
                        if not is_first(b):
                            rstd_of(b)
                    elif what == "x":
                        split_x(b, i)
                    elif what == "weights":
                        weights(b * HEADS + i, i)
                    else:
                        {"norm": norm, "query": query}[what](b * HEADS, i)

            def heads(b):
                first = b * HEADS
                segment(POOL_A[1:], first, 0, True)
                with pool.Fori(0, HEADS - 2) as h:
                    segment(POOL_B, first + h, h, True)
                    segment(POOL_A, first + (h + 1), h + 1, True)
                segment(POOL_B, first + (HEADS - 2), HEADS - 2, True)
                segment(POOL_A, first + (HEADS - 1), HEADS - 1, False)

            def rstd2(n, many):
                wait_apart(pool, ffn_in, FFN_IN, (ln2_step, n * 3 + 3))
                pool.tensor_tensor(rstd[:, 0:many], var_eps[:, 0:many], minus_half[:, 0:many], ALU.pow)\
                    .then_inc(rstd2_done, 1)

            def split_x2(t, r):
                wait_apart(pool, ffn_in, FFN_IN, (x2_high, t + 1))
                pool.tensor_tensor(x2T_hl[:, LO, r, :], x2T[:, r, :], f32(x2T_hl[:, HI, r, :]), ALU.subtract)\
                    .then_inc(x2_split, 1)

            def low_weights(p):
                for k in split_next(p):
                    if k % 2 == 1:
                        pool.wait_ge(w_high, k + 1)
                        pool.tensor_tensor(w3_hl[:, LO, :, k, :], w3[:, :, k, :], f32(w3_hl[:, HI, :, k, :]),
                                           ALU.subtract).then_inc(w_split_pool, 1)

            def split_hidden(g, r, z):
                wait_apart(pool, ffn_in, FFN_IN, (act_high, g + 1))
                pool.tensor_tensor(act_hl[:, LO, z, :], hf[:, r, :], f32(act_hl[:, HI, z, :]), ALU.subtract)\
                    .then_inc(act_split, 1)

            def tile_body(b, u, ahead, more=True):
                t = b * TILES + u
                for p in range(UNITS):
                    if is_first(t):
                        low_weights(p)
                    split_hidden(t * UNITS + p, (u + p) % 2, slot(p))
                    if ahead and p == 4:
                        rstd2(t + 1, 4)
                    if more and p == 9:
                        split_x2(t + 1, (u + 1) % 2)

            prepare(0)
            with pool.Fori(0, BATCH - 1) as b:
                heads(b)
                prepare(b + 1)
            heads(BATCH - 1)

            pool.wait_ge(ffn_in, FFN_IN)
            rstd2(0, BLOCKS)
            split_x2(0, 0)
            pool.wait_ge(pick_loaded, 32)
            for k in range(2):
                pool.tensor_scalar(pick[:, k * HEADS:(k + 1) * HEADS, :], pick_raw[k], 1.0, 1.0, ALU.mult, ALU.mult)\
                    .then_inc(pick_done, 1)

            tile_body(0, 0, True)
            with pool.Fori(0, BATCH - 2) as b:
                tile_body(b, 1, True)
                tile_body(b + 1, 0, True)
            tile_body(BATCH - 2, 1, True)
            tile_body(BATCH - 1, 0, False)
            tile_body(BATCH - 1, 1, False, False)

        @block.vector
        def _(dve):
            dve.sem_inc(q_sum, CREDIT)
            dve.sem_inc(p_split, CREDIT)
            dve.sem_inc(o_split, CREDIT)
            dve.sem_inc(x1_done, CREDIT)
            dve.memset(w3[:, 0:2, PAIRS, INNER:], 0.0)
            dve.memset(w3[INNER:, 2, PAIRS, :], 0.0)
            dve.memset(b2[INNER:, :, PAIRS:UNITS], 0.0).then_inc(padded, 1)
            dve.wait_ge(c_exp, 1)
            dve.tensor_scalar(cT[:, 2, :], cT[:, 1, :], 1.0, None, ALU.add).then_inc(dve_setup, 1)
            dve.wait_ge(dve_setup, 1)
            dve.reciprocal(c_inv[:], cT[:, 2, :]).then_inc(dve_setup, 1)
            dve.wait_ge(dve_setup, 2)
            dve.tensor_tensor(cT[:, 3, :], cT[:, 0, :], c_inv[:], ALU.mult).then_inc(dve_setup, 1)
            def query(n, u):
                at = slice(u * HALF, (u + 1) * HALF)
                dve.wait_ge(q_split, CREDIT + 2 * n + u - 1)
                dve.wait_ge(q_mm, 2 * n + u + 1)
                return at

            def query_of(n, h, u):
                at = query(n, u)
                dve.scalar_tensor_tensor(qT[:, at], project[:], bqT[:, row(h)], peT[:, at], ALU.add, ALU.add)\
                    .then_inc(q_sum, 1)

            def maximum(n, i):
                k = PLACE[i]
                dve.wait_ge(score_mm, BLOCKS * n + k + 1)
                at = slice(score_at(i), score_at(i) + P * (i + 1))
                dve.tensor_reduce(nmax[:, i:i + 1], scores[k % 2][:, at], AX_X, ALU.max, negate=True)\
                    .then_inc(max_done, 1)

            def inverse(n, i):
                dve.wait_ge(exp_done, BLOCKS * n + PLACE[i] + 1)
                dve.reciprocal(rtotal[:, i:i + 1], total[:, i:i + 1]).then_inc(inverted, 1)

            def norm(n, i):
                dve.wait_ge(inverted, BLOCKS * n + PLACE[i] + 1)
                at = slice(PROB_AT[i], PROB_AT[i + 1])
                dve.tensor_scalar(probs[:, at], probs[:, at], rtotal[:, i:i + 1], None, ALU.mult)\
                    .then_inc(normed_last, 1)

            def low(n, s):
                u, j = STEPS[s]
                at = slice(P * max(j - 4 * u, 0), HALF)
                dve.wait_ge(p_high, NSTEP * n + s + 1)
                dve.tensor_tensor(pT_hl[:, LO, s % RING, at], turned[s % 2][:, at], f32(pT_hl[:, HI, s % RING, at]),
                                  ALU.subtract).then_inc(p_split, 1)

            def out_low(n, h, u):
                at = slice(u * HALF, (u + 1) * HALF)
                dve.wait_ge(o_high, 2 * n + u + 1)
                dve.scalar_tensor_tensor(oT_hl[:, LO, row(h), at].rearrange("p a t -> p (a t)"), mixed[:], bkvT[:, 1:2],
                                         f32(oT_hl[:, HI, row(h), at].rearrange("p a t -> p (a t)")),
                                         ALU.add, ALU.subtract).then_inc(o_split, 1)

            def segment(todo, n, h, more, prev):
                for what, i in todo:
                    m, k = (n + 1, h + 1) if (what, i) in NEXT_HEAD else (n, h)
                    if (what, i) in NEXT_HEAD and not more:
                        continue
                    if what == "max":
                        maximum(m, i)
                    elif what == "norm":
                        norm(m, i)
                    elif what == "inverse":
                        inverse(m, i)
                    elif what == "query":
                        query_of(m, k, i)
                    elif what == "low":
                        low(m, i)
                    elif what == "out":
                        out_low(n, h, i)
                    elif prev:
                        out_low(n - 1, h - 1, i)

            def ln_mod_of(b):
                dve.tensor_copy(ln_mod[:], mod[:, row(b), SHIFT_A:SCALE_A + 1].rearrange("p a j -> p (a j)"))

            def mod_vectors():
                dve.wait_ge(mod_mm, 1)
                dve.tensor_copy(mod[:].rearrange("p b j -> p j b"),
                                project[:, 0:6 * BATCH].rearrange("p (j b) -> p j b", j=6)).then_inc(dve_setup, 1)
                dve.wait_ge(dve_setup, 4)
                gates = list(enumerate((GATE_A, GATE_F)))
                for k, j in gates:
                    last = dve.tensor_scalar(sign[:, k, :], mod[:, :, j], 0.0, 2.0, ALU.is_ge, ALU.mult)
                last.then_inc(dve_setup, 1)
                dve.wait_ge(dve_setup, 5)
                for k, j in gates:
                    last = dve.scalar_tensor_tensor(floor[:, k, :], sign[:, k, :], -1.0, mod[:, :, j],
                                                    ALU.add, ALU.mult)
                last.then_inc(dve_setup, 1)
                dve.wait_ge(dve_setup, 6)
                dve.tensor_scalar(floor[:], floor[:], 0.25, None, ALU.max).then_inc(dve_setup, 1)
                dve.wait_ge(dve_setup, 7)
                for k, j in gates:
                    dve.scalar_tensor_tensor(mod[:, :, j], sign[:, k, :], -1.0, floor[:, k, :], ALU.add, ALU.mult)
                for j in (SCALE_A, SCALE_F):
                    last = dve.tensor_scalar(mod[:, :, j], mod[:, :, j], 1.0, None, ALU.add)
                last.then_inc(dve_setup, 1)
                dve.wait_ge(dve_setup, 8)
                ln_mod_of(0)

            def statistics(b, u):
                for k in range(4 * u, 4 * u + 4):
                    last = dve.bn_stats(stats[:, k, :], x[:, row(b * BLOCKS + k), :].rearrange("p a e -> p (a e)"))
                if u == 1:
                    last.then_inc(ln_step, 1)

            def aggregate(b):
                wait_apart(dve, x_first, 16, (ln_step, b * 3 + 1))
                for k in range(BLOCKS):
                    last = dve.bn_aggr(mv[:, k, :], stats[:, k, :])
                last.then_inc(ln_step, 1)
                dve.wait_ge(ln_step, b * 3 + 2)
                dve.tensor_scalar(var_eps[:], mv[:, :, 1], LN_EPS, None, ALU.add).then_inc(ln_step, 1)

            def normalise(b, u):
                if u == 0:
                    dve.wait_ge(rstd_done, b + 1)
                for k in range(4 * u, 4 * u + 4):
                    last = dve.tensor_scalar(xn[:, k, :], x[:, row(b * BLOCKS + k), :].rearrange("p a e -> p (a e)"),
                                             mv[:, k, 0:1], rstd[:, k:k + 1], ALU.subtract, ALU.mult)
                last.then_inc(xn_done, 1)

            def key_sum(b, u):
                at = slice(u * HALF, (u + 1) * HALF)
                dve.wait_ge(k_mm, b * 2 + u + 1)
                dve.scalar_tensor_tensor(kT[:, at], scores[0][:, at], bkvT[:, 0:1], peT[:, at], ALU.add, ALU.add)\
                    .then_inc(k_sum, 1)

            def key_low(b, u):
                at = slice(u * HALF, (u + 1) * HALF)
                dve.wait_ge(k_high, b * 2 + u + 1)
                dve.scalar_tensor_tensor(kT_hl[:, LO, at], kT[:, at], SCALE, f32(kT_hl[:, HI, at]),
                                         ALU.mult, ALU.subtract).then_inc(k_split, 1)

            def value_low(b, u):
                at = slice(u * HALF, (u + 1) * HALF)
                dve.wait_ge(v_high, b * 2 + u + 1)
                dve.tensor_tensor(v_hl[:, LO, at], turned[u][:], f32(v_hl[:, HI, at]), ALU.subtract)\
                    .then_inc(v_split, 1)

            def add_attention(b, u):
                dve.wait_ge(y_turned, b * 2 + u + 1)
                rows = x[:, bass.ds(b * BLOCKS + 4 * u, 4), :]
                dve.tensor_tensor(rows, y_ps[u].rearrange("p (k e) -> p k e", k=4), rows, ALU.add)\
                    .then_inc(x1_done, 1)

            def turn_row(b, old, new):
                n = (b + 1) * HEADS - 1
                if old:
                    gate = mod[:, row(b), GATE_A:GATE_A + 1]
                    dve.tensor_copy(cur[:, GATE_A:GATE_A + 1], gate.rearrange("p a j -> p (a j)"))
                for what, i in DVE_TAIL:
                    if not (old if what in OLD_ROW else not new if what == "ffn" else new):
                        continue
                    if what == "stats":
                        if old and i == 0:
                            ln_mod_of(b + 1)
                        statistics(b + 1, i)
                    elif what == "aggregate":
                        aggregate(b + 1)
                        if not old:
                            mod_vectors()
                    elif what == "ffn":
                        prepare_tile(i)
                    elif what == "query":
                        query_of(n + 1, 0, i)
                    elif what == "out":
                        out_low(n, HEADS - 1, i)
                    elif what in ("max", "inverse"):
                        {"max": maximum, "inverse": inverse}[what](n + 1, i)
                    elif what == "low":
                        low(n, i)
                    elif what == "y":
                        add_attention(b, i)
                    else:
                        {"x": normalise, "k_sum": key_sum, "k_low": key_low, "v_low": value_low}[what](b + 1, i)
                        if (what, i) == ("x", 1) and not old:
                            dve.wait_ge(wo_high, 1)
                            dve.tensor_tensor(wo_hl[:, LO, :, :], wo[:], f32(wo_hl[:, HI, :, :]), ALU.subtract)\
                                .then_inc(wo_split, 1)
                            dve.wait_ge(wo_split, 1)

            def heads(b):
                first = b * HEADS
                segment(DVE_A, first, 0, True, False)
                with dve.Fori(0, HEADS - 2) as h:
                    segment(DVE_B, first + h, h, True, True)
                    segment(DVE_A, first + (h + 1), h + 1, True, True)
                segment(DVE_B, first + (HEADS - 2), HEADS - 2, True, True)
                segment(DVE_A, first + (HEADS - 1), HEADS - 1, False, True)

            def stats2(t, b, many=4):
                dve.wait_ge(x1_done, CREDIT + 2 if is_first(t) else CREDIT + 2 * BATCH)
                dve.tensor_copy(ln_mod[:], mod[:, row(b), SHIFT_F:SCALE_F + 1].rearrange("p a j -> p (a j)"))
                for k in range(many):
                    last = dve.bn_stats(stats[:, k, :], x[:, row(t * 4 + k), :].rearrange("p a e -> p (a e)"))
                last.then_inc(ln2_step, 1)

            def aggregate2(n, many=4):
                wait_apart(dve, ffn_in, FFN_IN, (ln2_step, n * 3 + 1))
                for k in range(many):
                    last = dve.bn_aggr(mv[:, k, :], stats[:, k, :])
                last.then_inc(ln2_step, 1)
                dve.wait_ge(ln2_step, n * 3 + 2)
                dve.tensor_scalar(var_eps[:, 0:many], mv[:, 0:many, 1], LN_EPS, None, ALU.add).then_inc(ln2_step, 1)

            def normalise2(t, n, ks):
                if 0 in ks:
                    dve.wait_ge(rstd2_done, n + 1)
                for k in ks:
                    last = dve.tensor_scalar(xn[:, k, :], x[:, row(t * 4 + k), :].rearrange("p a e -> p (a e)"),
                                             mv[:, k, 0:1], rstd[:, k:k + 1], ALU.subtract, ALU.mult)
                if ks[-1] % 4 == 3:
                    last.then_inc(xn2_done, 1)

            def add_br(t, u, bank=misc_ps):
                dve.wait_ge(logit_mm, t + 1)
                for k in range(4):
                    last = dve.tensor_tensor(lg[:, 4 * u + k, :], bank[:, k * EXPERTS:(k + 1) * EXPERTS], br_rows[:],
                                             ALU.add)
                last.then_inc(logit_done, 1)

            def top_eight(b):
                wait_apart(dve, ffn_in, FFN_IN, (aff_done, b + 1))
                for k in range(BLOCKS):
                    last = dve.max(top[:, k, :], aff[:, k, :])
                last.then_inc(route_step, 1)

            def choose(b):
                wait_apart(dve, ffn_in, FFN_IN, (route_step, b * 4 + 1))
                for k in range(BLOCKS):
                    dve.match_replace(rest[:, k, :], top[:, k, :], aff[:, k, :], 0.0)
                dve.tensor_reduce(top_sum[:], top[:], AX_X, ALU.add).then_inc(route_step, 1)

            def invert(b):
                dve.wait_ge(route_step, b * 4 + 2)
                dve.tensor_tensor(chosen, aff, rest, ALU.subtract)
                dve.tensor_scalar(top_eps[:], top_sum[:], 1e-9, None, ALU.add).then_inc(route_step, 1)
                dve.wait_ge(route_step, b * 4 + 3)
                dve.reciprocal(top_inv[:], top_eps[:]).then_inc(route_step, 1)

            def weigh(b, u):
                if u == 0:
                    dve.wait_ge(route_step, b * 4 + 4)
                for k in range(4 * u, 4 * u + 4):
                    last = dve.tensor_scalar(weight2[:, k, :].rearrange("p (c e) -> p c e", c=2),
                                             chosen[:, k:k + 1, :].broadcast_to([P, 2, EXPERTS]),
                                             top_inv[:, k:k + 1], None, ALU.mult)
                last.then_inc(weight_done, 1)

            def split_weight(t, r, bank=misc_ps):
                dve.wait_ge(weight_high, t + 1)
                dve.tensor_tensor(weightT[EXPERTS:, r, :], bank[EXPERTS:2 * EXPERTS, :],
                                  f32(weightT[EXPERTS:, r, :]), ALU.subtract).then_inc(weight_split, 1)

            def prepare_tile(step):
                if step == 0:
                    dve.wait_ge(ffn_in, FFN_IN)
                    dve.memset(f32(bd_l[:]), 0.0)
                    dve.tensor_copy(bd_h[:], bd2[:]).then_inc(bd_high, 1)
                    dve.wait_ge(bd_high, 1)
                    dve.tensor_tensor(bd_l[0:EXPERTS, :], bd2[0:EXPERTS, :], f32(bd_h[0:EXPERTS, :]), ALU.subtract)\
                        .then_inc(bd_split, 1)
                    stats2(0, 0, BLOCKS)
                elif step == 1:
                    aggregate2(0, BLOCKS)
                elif step == 2:
                    normalise2(0, 0, range(4))
                elif step == 3:
                    normalise2(0, 0, range(4, BLOCKS))
                elif step in (4, 5):
                    add_br(step - 4, step - 4, first_ps[step - 4])
                elif step == 6:
                    top_eight(0)
                    choose(0)
                    invert(0)
                    weigh(0, 0)
                    weigh(0, 1)
                else:
                    split_weight(0, 0, first_ps[0])

            def low_weights(p):
                for k in split_next(p):
                    if k % 2 == 0:
                        dve.wait_ge(w_high, k + 1)
                        dve.tensor_tensor(w3_hl[:, LO, :, k, :], w3[:, :, k, :], f32(w3_hl[:, HI, :, k, :]),
                                          ALU.subtract).then_inc(w_split, 1)

            def hidden_of(t, p, r):
                g = t * UNITS + p
                dve.wait_ge(silu_done, g + 1)
                dve.wait_ge(up_mm, g + 1)
                if p == PAIRS:
                    dve.wait_ge(act_split, CREDIT + g - 1)
                    dve.scalar_tensor_tensor(hf[:, r, :], up_ps[r], b2[:, 1, p:p + 1], gs[:, r, :], ALU.add, ALU.mult)\
                        .then_inc(hidden, 1)
                    return
                dve.scalar_tensor_tensor(prod[:, r, :], up_ps[r], b2[:, 1, p:p + 1], gs[:, r, :], ALU.add, ALU.mult)\
                    .then_inc(prod_done, 1)
                dve.wait_ge(act_split, CREDIT + g - 1)
                dve.wait_ge(prod_done, t * PAIRS + p + 1)
                dve.tensor_tensor(hf[:, r, :], prod[:, r, :], weight_ps[r], ALU.mult).then_inc(hidden, 1)

            def gate_of(b):
                dve.wait_ge(y2_done, b * TILES + 1)
                dve.tensor_copy(cur[:, GATE_F:], mod[:, row(b), GATE_F:].rearrange("p a j -> p (a j)"))
                dve.tensor_tensor(gate_bds[:], mod[:, row(b), GATE_F:].rearrange("p a j -> p (a j)"), bds[:], ALU.mult)\
                    .then_inc(gate_cur, 1)

            def add_out(t):
                dve.wait_ge(y2_turned, t + 1)
                rows = x[:, bass.ds(t * 4, 4), :]
                dve.tensor_tensor(rows, misc_ps[:].rearrange("p (k e) -> p k e", k=4), rows, ALU.add)\
                    .then_inc(out_done, 1)

            def tile_body(b, u, ahead, more=True):
                t = b * TILES + u
                r1 = (u + 1) % 2
                for p in range(LAG + 1, UNITS):
                    if is_first(t):
                        low_weights(p)
                    hidden_of(t, p, (u + p) % 2)
                    if p == LAG + 1 and u == 0:
                        gate_of(b)
                    if ahead:
                        if p == 4:
                            stats2(t + 2, b + 1)
                            aggregate2(t + 1)
                        if p == 6:
                            normalise2(t + 2, t + 1, (0, 1))
                        if p == 7:
                            normalise2(t + 2, t + 1, (2, 3))
                        if p == 9:
                            add_br(t + 2, u)
                        if u == 1:
                            if p == 10:
                                top_eight(b + 1)
                            if p == 11:
                                choose(b + 1)
                            if p == 12:
                                invert(b + 1)
                            if p == 13:
                                weigh(b + 1, 0)
                            if p == 14:
                                weigh(b + 1, 1)
                    if more and p == 15:
                        split_weight(t + 1, r1)
                if more:
                    for p in range(LAG + 1):
                        hidden_of(t + 1, p, (r1 + p) % 2)
                add_out(t)

            dve.wait_ge(x_first, 16)
            turn_row(-1, False, True)
            dve.wait_ge(x_rest, 16 * (BATCH - 1))
            with dve.Fori(0, BATCH - 1) as b:
                heads(b)
                turn_row(b, True, True)
            heads(BATCH - 1)
            turn_row(BATCH - 1, True, False)

            for p in range(LAG + 1):
                low_weights(p)
                hidden_of(0, p, p % 2)
            tile_body(0, 0, True)
            with dve.Fori(0, BATCH - 2) as b:
                tile_body(b, 1, True)
                tile_body(b + 1, 0, True)
            tile_body(BATCH - 2, 1, True)
            tile_body(BATCH - 1, 0, False)
            tile_body(BATCH - 1, 1, False, False)

        @block.scalar
        def _(act):
            act.sem_inc(y2_done, 1)
            act.wait_ge(c_loaded, 16)
            act.activation(cT[:, 1, :], cT[:, 0, :], ACT.Exp, scale=-1.0).then_inc(c_exp, 1)
            act.wait_ge(attn_in, ATTN_IN)
            act.activation(wo_hl[:, HI, :, :], wo[:], ACT.Copy).then_inc(wo_high, 1)

            def exponent(n, i):
                k = PLACE[i]
                act.wait_ge(max_done, BLOCKS * n + k + 1)
                at = slice(score_at(i), score_at(i) + P * (i + 1))
                act.activation(probs[:, PROB_AT[i]:PROB_AT[i + 1]], scores[k % 2][:, at], ACT.Exp,
                               bias=nmax[:, i:i + 1], accum_out=total[:, i:i + 1]).then_inc(exp_done, 1)

            def high(n, s):
                u, j = STEPS[s]
                at = slice(P * max(j - 4 * u, 0), HALF)
                act.wait_ge(applied, NSTEP * n + s + 1)
                act.wait_ge(p_turned, NSTEP * n + s + 1)
                act.activation(pT_hl[:, HI, s % RING, at], turned[s % 2][:, at], ACT.Copy).then_inc(p_high, 1)

            def out_high(n, h, u):
                at = slice(u * HALF, (u + 1) * HALF)
                wait_apart(act, attn_in, ATTN_IN, (applied, RING + NSTEP * n + (4, 12)[u]))
                act.activation(oT_hl[:, HI, row(h), at].rearrange("p a t -> p (a t)"), mixed[:], ACT.Identity,
                               bias=bkvT[:, 1:2]).then_inc(o_high, 1)

            def segment(todo, n, h, more, prev):
                for what, i in todo:
                    if what == "exp":
                        if (what, i) not in NEXT_HEAD:
                            exponent(n, i)
                        elif more:
                            exponent(n + 1, i)
                    elif what == "high":
                        high(n, i)
                    elif what == "out":
                        out_high(n, h, i)
                    elif prev:
                        out_high(n - 1, h - 1, i)

            def modulate(b, u):
                at = slice(u * HALF, (u + 1) * HALF)
                act.wait_ge(x_turned, b * 2 + u + 1)
                act.activation(hT[:, at], scores[0][:, at], ACT.Identity, bias=ln_mod[:, 0:1],
                               scale=ln_mod[:, 1:2]).then_inc(hT_done, 1)

            def key_high(b, u):
                at = slice(u * HALF, (u + 1) * HALF)
                act.wait_ge(k_sum, b * 2 + u + 1)
                act.activation(kT_hl[:, HI, at], kT[:, at], ACT.Copy, scale=SCALE).then_inc(k_high, 1)

            def value_high(b, u):
                at = slice(u * HALF, (u + 1) * HALF)
                act.wait_ge(v_mm, b * 2 + u + 1)
                act.activation(v_hl[:, HI, at], turned[u][:], ACT.Copy).then_inc(v_high, 1)

            def gated(b, u):
                act.wait_ge(y_mm, b * 2 + u + 1)
                act.activation(yT[:, u, :], wo_ps[u], ACT.Identity,
                               scale=cur[:, GATE_A:GATE_A + 1]).then_inc(y_done, 1)

            def turn_row(b, old, new):
                n = (b + 1) * HEADS - 1
                for what, i in ACT_TAIL:
                    if not (old if what in OLD_ROW else not new if what == "ffn" else new):
                        continue
                    if what == "exp":
                        exponent(n + 1, i)
                    elif what == "out":
                        out_high(n, HEADS - 1, i)
                    elif what == "high":
                        high(n, i)
                    elif what == "y":
                        gated(b, i)
                    elif what == "ffn":
                        prepare_tile(i)
                    else:
                        {"x": modulate, "k_high": key_high, "v_high": value_high}[what](b + 1, i)

            def heads(b):
                first = b * HEADS
                segment(ACT_A, first, 0, True, False)
                with act.Fori(0, HEADS - 2) as h:
                    segment(ACT_B, first + h, h, True, True)
                    segment(ACT_A, first + (h + 1), h + 1, True, True)
                segment(ACT_B, first + (HEADS - 2), HEADS - 2, True, True)
                segment(ACT_A, first + (HEADS - 1), HEADS - 1, False, True)

            def modulate2(t, r, bank=misc_ps):
                act.wait_ge(x2_turned, t + 1)
                act.activation(x2T[:, r, :], bank[:], ACT.Identity, bias=ln_mod[:, 0:1], scale=ln_mod[:, 1:2])\
                    .then_inc(x2_done, 1)

            def high_x2(t, r):
                wait_apart(act, ffn_in, FFN_IN, (x2_done, t + 1))
                act.activation(x2T_hl[:, HI, r, :], x2T[:, r, :], ACT.Copy).then_inc(x2_high, 1)

            def high_weight(t, r, bank=misc_ps):
                act.wait_ge(weight_turned, t + 1)
                act.activation(weightT[:, r, :], bank[0:2 * EXPERTS, :], ACT.Copy).then_inc(weight_high, 1)

            def high_weights(p):
                for k in split_next(p):
                    act.activation(w3_hl[:, HI, :, k, :], w3[:, :, k, :], ACT.Copy).then_inc(w_high, 1)

            def high_hidden(t, p, r):
                g = t * UNITS + p
                wait_apart(act, ffn_in, FFN_IN, (down_mm, CREDIT + g - (1 if p < 2 else 2)), (hidden, g + 1))
                act.activation(act_hl[:, HI, slot(p), :], hf[:, r, :], ACT.Copy).then_inc(act_high, 1)

            def prepare_tile(step):
                if step in (0, 1):
                    modulate2(step, step, first_ps[step])
                elif step == 2:
                    high_x2(0, 0)
                    affinity(0)
                else:
                    high_weight(0, 0, first_ps[0])

            def affinity(b):
                act.wait_ge(logit_done, 2 * b + 2)
                act.activation(aff, lg, ACT.Sigmoid).then_inc(aff_done, 1)

            def silu(t, p, r):
                g = t * UNITS + p
                if p >= 2 or not is_first(t):
                    act.wait_ge(hidden, g - 1)
                act.wait_ge(gate_mm, g + 1)
                act.activation(gs[:, r, :], gate_ps[r][:], ACT.Silu, bias=b2[:, 0, p:p + 1]).then_inc(silu_done, 1)

            def gated_out(t, b):
                act.wait_ge(gate_cur, b + 1)
                act.wait_ge(down_mm, CREDIT + (t + 1) * UNITS)
                act.activation(yT[:, 1, :], acc_ps[:], ACT.Identity, bias=gate_bds[:], scale=cur[:, GATE_F:])\
                    .then_inc(y2_done, 1)

            def tile_body(b, u, ahead, more=True):
                t = b * TILES + u
                r1 = (u + 1) % 2
                for p in range(LAG + 1, UNITS):
                    if is_first(t):
                        high_weights(p)
                    silu(t, p, (u + p) % 2)
                    high_hidden(t, p - 1, (u + p - 1) % 2)
                    if more and p == 7:
                        high_x2(t + 1, r1)
                    if ahead and p == 8:
                        modulate2(t + 2, u)
                    if ahead and u == 1 and p == 10:
                        affinity(b + 1)
                    if more and p == 15:
                        high_weight(t + 1, r1)
                if more:
                    silu(t + 1, 0, r1)
                high_hidden(t, UNITS - 1, (u + UNITS - 1) % 2)
                if more:
                    for p in range(1, LAG):
                        silu(t + 1, p, (r1 + p) % 2)
                        high_hidden(t + 1, p - 1, (r1 + p - 1) % 2)
                gated_out(t, b)
                if more:
                    silu(t + 1, LAG, (r1 + LAG) % 2)
                    high_hidden(t + 1, LAG - 1, (r1 + LAG - 1) % 2)

            turn_row(-1, False, True)
            with act.Fori(0, BATCH - 1) as b:
                heads(b)
                turn_row(b, True, True)
            heads(BATCH - 1)
            turn_row(BATCH - 1, True, False)

            act.wait_ge(ffn_in, FFN_IN)
            act.wait_ge(y_mm, 2 * BATCH)
            for p in range(LAG + 1):
                high_weights(p)
                silu(0, p, p % 2)
                if p > 0:
                    high_hidden(0, p - 1, (p - 1) % 2)
            tile_body(0, 0, True)
            with act.Fori(0, BATCH - 2) as b:
                tile_body(b, 1, True)
                tile_body(b + 1, 0, True)
            tile_body(BATCH - 2, 1, True)
            tile_body(BATCH - 1, 0, False)
            tile_body(BATCH - 1, 1, False, False)

        @block.tensor
        def _(pe):
            pe.sem_inc(applied, RING)
            pe.sem_inc(down_mm, CREDIT)
            pe.wait_ge(mod_in, 16)
            pe.wait_ge(dve_setup, 3)
            for j in range(6):
                mm = pe.matmul(project[:, j * BATCH:(j + 1) * BATCH], wmod[:, j * P:(j + 1) * P], cT[:, 3, :],
                               start=True, stop=True)
            mm.then_inc(mod_mm, 1)
            pe.wait_ge(eye_loaded, 16)

            def project_q(n, u):
                at = slice(u * HALF, (u + 1) * HALF)
                pe.wait_ge(wq_split, n + 1)
                pe.wait_ge(q_sum, CREDIT + 2 * n + u)
                split3(pe, project[:], hl(wq_hl), hl(hT_hl, at)).then_inc(q_mm, 1)

            def score(n, i, wait=True):
                k, u = PLACE[i], i // 4
                pe.wait_ge(q_split, CREDIT + 2 * n + u + 1)
                if wait:
                    pe.wait_ge(exp_done, BLOCKS * n + k - 1)
                start, width = score_at(i), P * (i + 1)
                bank = scores[k % 2]
                for c in ((0, width),) if width <= HALF else ((0, width // 2), (width // 2, width)):
                    q, kk = hl(qT_hl, slice(P * i, P * (i + 1))), hl(kT_hl, slice(*c))
                    to = bank[:, start + c[0]:start + c[1]]
                    pe.matmul(to, q[HI], kk[HI], start=True, stop=False)
                    if c[1] == width:
                        pe.matmul(bank[:, start + width - P:start + width], eye_b[:], mask_b[:], start=False, stop=False)
                    pe.matmul(to, q[HI], kk[LO], start=False, stop=False)
                    mm = pe.matmul(to, q[LO], kk[HI], start=False, stop=True)
                mm.then_inc(score_mm, 1)

            def turn(n, s):
                u, j = STEPS[s]
                pe.wait_ge(normed, (BLOCKS - 1) * n + (4, 7)[u])
                if u == 1:
                    pe.wait_ge(normed_last, n + 1)
                pe.wait_ge(p_split, CREDIT + NSTEP * n + s - 1)
                for i in range(max(j, 4 * u), 4 * (u + 1)):
                    mm = pe.transpose(turned[s % 2][:, P * (i - 4 * u):P * (i - 4 * u + 1)],
                                      probs[:, PROB_AT[i] + P * j:PROB_AT[i] + P * (j + 1)], eye[:])
                mm.then_inc(p_turned, 1)

            def apply(n, s):
                u, j = STEPS[s]
                at = slice(P * max(j - 4 * u, 0), HALF)
                pe.wait_ge(p_split, CREDIT + NSTEP * n + s + 1)
                if j == 0:
                    pe.wait_ge(o_split, CREDIT + 2 * n + u)
                values = hl(v_hl, slice(P * j, P * (j + 1)))
                split3(pe, mixed[:, at], values, [pT_hl[:, a, s % RING, at] for a in (HI, LO)],
                       first=(j == 0), last=(j == 4 * u + 3)).then_inc(applied, 1)

            def segment(todo, n, more, prev):
                for what, i in todo:
                    if what == "apply_prev":
                        if prev:
                            apply(n - 1, i)
                        continue
                    m = n + 1 if (what, i) in NEXT_HEAD else n
                    if (what, i) in NEXT_HEAD and not more:
                        continue
                    {"score": score, "turn": turn, "apply": apply, "project": project_q}[what](m, i)

            def turn_x(b, u):
                pe.wait_ge(xn_done, b * 2 + u + 1)
                for k in range(4 * u, 4 * u + 4):
                    mm = pe.transpose(scores[0][:, P * k:P * (k + 1)], xn[:, k, :], eye[:])
                mm.then_inc(x_turned, 1)

            def keys(b, u):
                at = slice(u * HALF, (u + 1) * HALF)
                pe.wait_ge(hT_split, b * 2 + u + 1)
                split3(pe, scores[0][:, at], hl(wkv_hl, slice(0, P)), hl(hT_hl, at)).then_inc(k_mm, 1)

            def values(b, u):
                for k in range(4 * u, 4 * u + 4):
                    mm = split3(pe, turned[u][:, P * (k - 4 * u):P * (k - 4 * u + 1)],
                                hl(hT_hl, slice(P * k, P * (k + 1))), hl(wkv_hl, slice(P, 2 * P)))
                mm.then_inc(v_mm, 1)

            def project_out(b, part):
                u, h = part // 4, part % 4 * 2
                at = slice(u * HALF, (u + 1) * HALF)
                if part == 0:
                    pe.wait_ge(wo_split, 1)
                    pe.wait_ge(q_sum, CREDIT + b * 2 * HEADS + 2 * HEADS)
                if part == 3:
                    pe.wait_ge(o_split, CREDIT + b * 2 * HEADS + 2 * HEADS - 1)
                if part == 4:
                    pe.wait_ge(o_split, CREDIT + b * 2 * HEADS + 2 * HEADS)
                for k in (h, h + 1):
                    mm = split3(pe, wo_ps[u], hl(wo_hl, k), hl(oT_hl, k, at), first=(k == 0), last=(k == HEADS - 1))
                if h + 2 == HEADS:
                    mm.then_inc(y_mm, 1)

            def turn_y(b, u):
                pe.wait_ge(y_done, b * 2 + u + 1)
                for k in range(4):
                    mm = pe.transpose(y_ps[u][:, P * k:P * (k + 1)], yT[:, u, P * k:P * (k + 1)], eye[:])
                mm.then_inc(y_turned, 1)

            def turn_row(b, old, new):
                n = (b + 1) * HEADS - 1
                for what, i in PE_TAIL:
                    if not (old if what in OLD_ROW else not new if what == "ffn" else new):
                        continue
                    if what in ("turn", "apply"):
                        {"turn": turn, "apply": apply}[what](n, i)
                    elif what == "ffn":
                        if i in (0, 1):
                            turn_x2(i, first_ps[i], 4 * i)
                        elif i in (2, 3):
                            logits(i - 2, i - 2, first_ps[i - 2])
                        else:
                            turn_weights(0, 0, first_ps[0])
                    elif what in ("wo", "y"):
                        if (what, i) == ("y", 1) and new:
                            pe.wait_ge(v_split, b * 2 + 4)
                        {"wo": project_out, "y": turn_y}[what](b, i)
                    elif what == "project":
                        if i == 0 and old:
                            pe.wait_ge(y_done, b * 2 + 1)
                        project_q(n + 1, i)
                    elif what == "score":
                        if i == 3:
                            pe.wait_ge(k_split, b * 2 + 4)
                        score(n + 1, i, wait=PLACE[i] >= 2)
                    else:
                        if (what, i) == ("keys", 0) and not old:
                            pe.wait_ge(attn_in, ATTN_IN)
                            pe.wait_ge(pool_setup, 4)
                        {"x": turn_x, "keys": keys, "values": values}[what](b + 1, i)

            def heads(b):
                first = b * HEADS
                pe.wait_ge(v_split, 2 * b + 2)
                before = PE_A.index(("turn", 0))
                segment(PE_A[:before], first, True, False)
                pe.wait_ge(x1_done, CREDIT + 2 * b)
                segment(PE_A[before:], first, True, False)
                with pe.Fori(0, HEADS - 2) as h:
                    segment(PE_B, first + h, True, True)
                    segment(PE_A, first + (h + 1), True, True)
                segment(PE_B, first + (HEADS - 2), True, True)
                segment(PE_A, first + (HEADS - 1), False, True)

            def turn_x2(t, bank=misc_ps, first_block=0):
                pe.wait_ge(xn2_done, t + 1)
                for k in range(4):
                    mm = pe.transpose(bank[:, P * k:P * (k + 1)], xn[:, first_block + k, :], eye[:])
                mm.then_inc(x2_turned, 1)

            def logits(t, r, bank=misc_ps):
                pe.wait_ge(x2_done, t + 1)
                for k in range(4):
                    mm = pe.matmul(bank[:, EXPERTS * k:EXPERTS * (k + 1)], x2T[:, r, P * k:P * (k + 1)], wr[:],
                                   start=True, stop=True)
                mm.then_inc(logit_mm, 1)

            def turn_weights(b, u, bank=misc_ps):
                wait_apart(pe, pool_setup, 4, (weight_done, 2 * b + 1 + u))
                for k in range(4):
                    mm = pe.transpose(bank[0:2 * EXPERTS, P * k:P * (k + 1)], weight2[:, 4 * u + k, :], eye[:])
                mm.then_inc(weight_turned, 1)

            def up_gate(t, g, p, q, r):
                if p == 0:
                    pe.wait_ge(x2_split, t + 1)
                    pe.wait_ge(weight_split, t + 1)
                if is_first(t):
                    pe.wait_ge((w_split, w_split_pool)[p % 2], p // 2 + 1)
                if p >= 2 or not is_first(t):
                    pe.wait_ge(silu_done, g - 1)
                right = [x2T_hl[:, a, q, :] for a in (HI, LO)]
                split3(pe, gate_ps[r][:], hl(w3_hl, 0, p), right).then_inc(gate_mm, 1)
                if p >= 2 or not is_first(t):
                    pe.wait_ge(hidden, g - 1)
                if p < PAIRS:
                    pe.matmul(weight_ps[r], pick[:, p, :], weightT[:, q, :], start=True, stop=True)
                split3(pe, up_ps[r], hl(w3_hl, 1, p), right).then_inc(up_mm, 1)

            def down(t, g, p, q):
                if p == 0:
                    pe.wait_ge(y2_done, t + 1)
                    pe.matmul(acc_ps[:], bd_h[:], weightT[:, q, :], start=True, stop=False)
                    pe.matmul(acc_ps[:], bd_l[:], weightT[:, q, :], start=False, stop=False)
                pe.wait_ge(act_split, CREDIT + g + 1)
                mm = split3(pe, acc_ps[:], hl(w3_hl, 2, p), [act_hl[:, a, slot(p), :] for a in (HI, LO)],
                            first=False, last=(p == PAIRS)).then_inc(down_mm, 1)
                return mm

            def turn_out(t):
                pe.wait_ge(y2_done, t + 2)
                for k in range(4):
                    mm = pe.transpose(misc_ps[:, P * k:P * (k + 1)], yT[:, 1, P * k:P * (k + 1)], eye[:])
                mm.then_inc(y2_turned, 1)

            def tile_body(b, u, ahead, more=True):
                t = b * TILES + u
                q, q1 = u % 2, (u + 1) % 2
                for p in range(LAG + 1, UNITS):
                    up_gate(t, t * UNITS + p, p, q, (u + p) % 2)
                    down(t, t * UNITS + p - LAG, p - LAG, q)
                    if ahead and p == 8:
                        turn_x2(t + 2)
                    if ahead and p == 9:
                        logits(t + 2, q)
                    if more and p == 14:
                        turn_weights(b + u, q1)
                for p in range(LAG):
                    if more:
                        up_gate(t + 1, (t + 1) * UNITS + p, p, q1, (q1 + p) % 2)
                    down(t, t * UNITS + UNITS - LAG + p, UNITS - LAG + p, q)
                if more:
                    up_gate(t + 1, (t + 1) * UNITS + LAG, LAG, q1, (q1 + LAG) % 2)
                turn_out(t)
                if more:
                    down(t + 1, (t + 1) * UNITS, 0, q1)

            turn_row(-1, False, True)
            with pe.Fori(0, BATCH - 1) as b:
                heads(b)
                turn_row(b, True, True)
            heads(BATCH - 1)
            turn_row(BATCH - 1, True, False)

            pe.wait_ge(pick_done, 2)
            pe.wait_ge(bd_split, 1)
            pe.wait_ge(x1_done, CREDIT + 2 * BATCH)
            for p in range(LAG + 1):
                up_gate(0, p, p, 0, p % 2)
            down(0, 0, 0, 0)
            tile_body(0, 0, True)
            with pe.Fori(0, BATCH - 2) as b:
                tile_body(b, 1, True)
                tile_body(b + 1, 0, True)
            tile_body(BATCH - 2, 1, True)
            tile_body(BATCH - 1, 0, False)
            tile_body(BATCH - 1, 1, False, False)


_INS = ['L0_attn_x', 'L0_attn_Wq', 'L0_attn_bq', 'L0_attn_Wkv', 'L0_attn_bkv', 'L0_attn_Wo', 'L0_ffn_Wr',
        'L0_ffn_br', 'L0_ffn_Wg_s', 'L0_ffn_bg_s', 'L0_ffn_Wu_s', 'L0_ffn_bu_s', 'L0_ffn_Wd_s', 'L0_ffn_bd_s',
        'L0_ffn_Wg', 'L0_ffn_bg', 'L0_ffn_Wu', 'L0_ffn_bu', 'L0_ffn_Wd', 'L0_ffn_bd', 'L0_c', 'L0_wmod']
_OUTS = [((BATCH, TOKENS, P), 'float32')]


def constants():
    eye = np.eye(P, dtype=np.float32)
    pos = np.arange(TOKENS, dtype=np.float32)[:, None]
    inv_freq = np.exp(np.float32(-math.log(10000.0)) * np.arange(0, P, 2, dtype=np.float32) / np.float32(P))
    angle = (pos * inv_freq[None, :].astype(np.float32)).astype(np.float32)
    pe = np.zeros((TOKENS, P), np.float32)
    pe[:, 0::2] = np.sin(angle)
    pe[:, 1::2] = np.cos(angle)
    mask = np.where(np.tril(np.ones((P, P), bool)), 0.0, MASKED).astype(np.float32)
    pick = np.zeros((2 * EXPERTS, PAIRS, P), np.float32)
    for e in range(EXPERTS):
        for half in range(2):
            pick[half * EXPERTS + e, e // 2, (e % 2) * INNER:(e % 2 + 1) * INNER] = 1.0
    return {"eye": eye, "pe": np.ascontiguousarray(pe.T), "mask": mask, "pick": pick}


def laid_out(name, a):
    if name == "L0_c":
        return a.T
    if name in ("L0_attn_bq", "L0_attn_bkv"):
        return a.reshape(-1, P).T
    if name in ("L0_ffn_bg_s", "L0_ffn_bu_s", "L0_ffn_bd_s"):
        return a.reshape(-1, 1)
    if name in ("L0_ffn_bg", "L0_ffn_bu"):
        return a.reshape(PAIRS, P).T
    if name in ("L0_ffn_Wg", "L0_ffn_Wu"):
        return a.reshape(PAIRS, 2, P, INNER).transpose(2, 0, 1, 3).reshape(P, PAIRS, P)
    if name == "L0_ffn_Wd":
        return a.reshape(PAIRS, P, P).transpose(1, 0, 2)
    return a


def kernel(**inputs):
    import numpy as _np
    import concourse.bacc as _bacc
    from concourse import mybir as _mybir
    from concourse.bass_utils import run_bass_kernel_spmd as _run

    nc = _bacc.Bacc("TRN2", target_bir_lowering=False, num_devices=1)
    arrays, args = {}, []
    for name, a in [(name, laid_out(name, _np.asarray(inputs[name]))) for name in _INS] + list(constants().items()):
        a = _np.ascontiguousarray(a)
        arrays[f"in_{name}_dram"] = a
        args.append(nc.dram_tensor(f"in_{name}_dram", a.shape, _mybir.dt.from_np(a.dtype), kind="ExternalInput").ap())
    for i, (shape, dtype) in enumerate(_OUTS):
        dt = _mybir.dt.from_np(_np.dtype(dtype))
        args.append(nc.dram_tensor(f"out_{i}_dram", shape, dt, kind="ExternalOutput").ap())
    bass_adaln_attention_moe(nc, *args)
    r = _run(nc, [arrays], core_ids=[0])
    got = tuple(r.results[0][f"out_{i}_dram"] for i in range(len(_OUTS)))
    return got[0]
```
